# Optimizing a Trainium2 kernel written in Bass

```python
import numpy as np
import jax
import jax.numpy as jnp

def _softmax(x, axis=-1):
    return jax.nn.softmax(x, axis=axis)

def _gelu(x):
    return jax.nn.gelu(x, approximate=True)

def _silu(x):
    return jax.nn.silu(x)

def _sigmoid(x):
    return jax.nn.sigmoid(x)

def _layernorm(x, axis=-1, eps=1e-05):
    m = jnp.mean(x, axis=axis, keepdims=True)
    v = jnp.var(x, axis=axis, keepdims=True)
    return (x - m) / jnp.sqrt(v + eps)

def _scatter_add(tgt, idx, src, axis=0):
    return tgt.at[idx].add(src)

def _segment_sum(src, seg, n):
    return jax.ops.segment_sum(src, seg, n)
kernel_name = 'mk_decoder_postln_d1_seqx_r4_3c2bed'

def setup_inputs(seed: int=0):
    np.random.seed(seed)
    _w = jnp.asarray

    def _rec_inputs():
        import jax
        import jax.numpy as jnp
        _rk = jax.random.key(seed)
        x = -0.0002928 + 1 * jax.random.normal(jax.random.fold_in(_rk, 1), (1, 2048, 256), jnp.float32)
        _lenS = 2048 - jax.random.randint(jax.random.fold_in(_rk, 7), (1,), 0, max(1, 2048 // 4) + 1, jnp.int32)
        _lenS2 = 1601 - jax.random.randint(jax.random.fold_in(_rk, 8), (1,), 0, max(1, 1601 // 4) + 1, jnp.int32)
        _ctx_1024P = jax.random.normal(jax.random.fold_in(_rk, 11), (1, 16, 256), jnp.float32)
        _ctx_1024c = jax.random.dirichlet(jax.random.fold_in(_rk, 511), 0.3 * jnp.ones((16,), jnp.float32), (1, 1601))
        _ctx_1024t = jnp.einsum('bsk,bkd->bsd', _ctx_1024c, _ctx_1024P)
        _ctx_1024t = _ctx_1024t * jax.lax.rsqrt(jnp.mean(jnp.square(_ctx_1024t)) + 1e-12) * 0.953939
        ctx_1024 = -1.39393e-06 + 0.999914 * (_ctx_1024t + 0.3 * jax.random.normal(jax.random.fold_in(_rk, 611), (1, 1601, 256), jnp.float32))
        return (x, ctx_1024)
    x, ctx_1024 = _rec_inputs()

    def _L0_attn_setup():
        import jax, jax.numpy as jnp
        import numpy as np
        B_SZ, SEQ, D_IN = (8, 1024, 256)
        STATE, HEADS = (256, 16)
        HEAD_DIM = STATE // HEADS
        LN_EPS = 1e-05
        key = jax.random.key(seed)
        ks = jax.random.split(key, 10)
        inp = {'x': jax.random.normal(ks[0], (B_SZ, SEQ, D_IN), dtype=jnp.float32), 'W_in': jax.random.normal(ks[1], (STATE, D_IN), dtype=jnp.float32) * (1.0 / np.sqrt(D_IN)), 'b_in': jnp.zeros((STATE,), dtype=jnp.float32), 'log_A': jax.random.normal(ks[2], (HEADS, HEAD_DIM), dtype=jnp.float32) * 0.1 + 0.1, 'B_p': jax.random.normal(ks[3], (HEADS, HEAD_DIM), dtype=jnp.float32) * 0.1 + 0.1, 'C_p': jax.random.normal(ks[4], (HEADS, HEAD_DIM), dtype=jnp.float32) * 0.1 + 0.1, 'W_out': jax.random.normal(ks[5], (STATE, STATE), dtype=jnp.float32) * (1.0 / np.sqrt(STATE)), 'b_out': jnp.zeros((STATE,), dtype=jnp.float32), 'gamma': jnp.ones((STATE,), dtype=jnp.float32), 'beta': jnp.zeros((STATE,), dtype=jnp.float32)}
        return inp
    _L0_attn_all = _L0_attn_setup()
    _L0_attn_in = {k: v for k, v in _L0_attn_all.items() if k in ('W_in', 'b_in', 'log_A', 'B_p', 'C_p', 'W_out', 'b_out', 'gamma', 'beta')}
    del _L0_attn_all

    def _L0_xattn_setup():
        import jax, jax.numpy as jnp
        import numpy as np
        HEADS = 8
        DIM_HEAD = 64
        DIM = 256
        CTX_DIM = 256
        HIDDEN = HEADS * DIM_HEAD
        key = jax.random.key(seed)
        ks = jax.random.split(key, 7)
        b, n, m = (2, 512, 512)
        x = jax.random.normal(ks[0], (b, n, DIM), dtype=jnp.float32)
        context = jax.random.normal(ks[1], (b, m, CTX_DIM), dtype=jnp.float32)
        Wq = jax.random.normal(ks[2], (DIM, HIDDEN), dtype=jnp.float32) * (1.0 / np.sqrt(DIM))
        Wk = jax.random.normal(ks[3], (CTX_DIM, HIDDEN), dtype=jnp.float32) * (1.0 / np.sqrt(CTX_DIM))
        Wv = jax.random.normal(ks[4], (CTX_DIM, HIDDEN), dtype=jnp.float32) * (1.0 / np.sqrt(CTX_DIM))
        Wo = jax.random.normal(ks[5], (HIDDEN, DIM), dtype=jnp.float32) * (1.0 / np.sqrt(HIDDEN))
        bo = jax.random.normal(ks[6], (DIM,), dtype=jnp.float32) * 0.01
        return {'x': x, 'context': context, 'Wq': Wq, 'Wk': Wk, 'Wv': Wv, 'Wo': Wo, 'bo': bo}
    _L0_xattn_all = _L0_xattn_setup()
    _L0_xattn_in = {k: v for k, v in _L0_xattn_all.items() if k in ('Wq', 'Wk', 'Wv', 'Wo', 'bo')}
    del _L0_xattn_all

    def _L0_ffn_setup():
        import jax, jax.numpy as jnp
        import numpy as np
        B, S, H = (2, 512, 256)
        N, F, SF, K = (16, 256, 1024, 1)
        key = jax.random.key(seed)
        ks = jax.random.split(key, 7)
        std = 0.02
        return {'hidden_states': jax.random.normal(ks[0], (B, S, H), dtype=jnp.float32), 'router_w': jax.random.normal(ks[1], (N, H), dtype=jnp.float32) * std, 'gate_up_proj': jax.random.normal(ks[2], (N, H, 2 * F), dtype=jnp.float32) * std, 'down_proj': jax.random.normal(ks[3], (N, F, H), dtype=jnp.float32) * std, 'shared_gate_w': jax.random.normal(ks[4], (SF, H), dtype=jnp.float32) * std, 'shared_up_w': jax.random.normal(ks[5], (SF, H), dtype=jnp.float32) * std, 'shared_down_w': jax.random.normal(ks[6], (H, SF), dtype=jnp.float32) * std}
    _L0_ffn_all = _L0_ffn_setup()
    _L0_ffn_in = {k: v for k, v in _L0_ffn_all.items() if k in ('router_w', 'gate_up_proj', 'down_proj', 'shared_gate_w', 'shared_up_w', 'shared_down_w')}
    del _L0_ffn_all
    return {'x': x, 'ctx_1024': ctx_1024, 'L0_attn_W_in': _L0_attn_in['W_in'], 'L0_attn_b_in': _L0_attn_in['b_in'], 'L0_attn_log_A': _L0_attn_in['log_A'], 'L0_attn_B_p': _L0_attn_in['B_p'], 'L0_attn_C_p': _L0_attn_in['C_p'], 'L0_attn_W_out': _L0_attn_in['W_out'], 'L0_attn_b_out': _L0_attn_in['b_out'], 'L0_attn_gamma': _L0_attn_in['gamma'], 'L0_attn_beta': _L0_attn_in['beta'], 'L0_xattn_Wq': _L0_xattn_in['Wq'], 'L0_xattn_Wk': _L0_xattn_in['Wk'], 'L0_xattn_Wv': _L0_xattn_in['Wv'], 'L0_xattn_Wo': _L0_xattn_in['Wo'], 'L0_xattn_bo': _L0_xattn_in['bo'], 'L0_ffn_router_w': _L0_ffn_in['router_w'], 'L0_ffn_gate_up_proj': _L0_ffn_in['gate_up_proj'], 'L0_ffn_down_proj': _L0_ffn_in['down_proj'], 'L0_ffn_shared_gate_w': _L0_ffn_in['shared_gate_w'], 'L0_ffn_shared_up_w': _L0_ffn_in['shared_up_w'], 'L0_ffn_shared_down_w': _L0_ffn_in['shared_down_w']}

def reference(x, ctx_1024, L0_attn_W_in, L0_attn_b_in, L0_attn_log_A, L0_attn_B_p, L0_attn_C_p, L0_attn_W_out, L0_attn_b_out, L0_attn_gamma, L0_attn_beta, L0_xattn_Wq, L0_xattn_Wk, L0_xattn_Wv, L0_xattn_Wo, L0_xattn_bo, L0_ffn_router_w, L0_ffn_gate_up_proj, L0_ffn_down_proj, L0_ffn_shared_gate_w, L0_ffn_shared_up_w, L0_ffn_shared_down_w):
    import jax
    import jax.numpy as jnp

    def _L0_attn_ref(x, W_in, b_in, log_A, B_p, C_p, W_out, b_out, gamma, beta):
        import jax, jax.numpy as jnp
        import numpy as np
        B_SZ, SEQ, D_IN = (8, 1024, 256)
        STATE, HEADS = (256, 16)
        HEAD_DIM = STATE // HEADS
        LN_EPS = 1e-05
        Bsz, S, _ = x.shape
        H, Dh = log_A.shape
        h = jnp.einsum('bsd,ed->bse', x, W_in) + b_in
        h = h.reshape(Bsz, S, H, Dh)
        decay = jnp.exp(-jax.nn.softplus(log_A))

        def step(s, xt):
            s = s * decay + B_p * xt
            return (s, C_p * s)
        s0 = jnp.zeros((Bsz, H, Dh), dtype=h.dtype)
        _, ys = jax.lax.scan(step, s0, jnp.swapaxes(h, 0, 1))
        y = jnp.swapaxes(ys, 0, 1).reshape(Bsz, S, H * Dh)
        out = jnp.einsum('bse,fe->bsf', y, W_out) + b_out
        mu = out.mean(-1, keepdims=True)
        var = out.var(-1, keepdims=True)
        return (out - mu) * jax.lax.rsqrt(var + LN_EPS) * gamma + beta

    def _L0_xattn_ref(x, context, Wq, Wk, Wv, Wo, bo):
        import jax, jax.numpy as jnp
        import numpy as np
        HEADS = 8
        DIM_HEAD = 64
        DIM = 256
        CTX_DIM = 256
        HIDDEN = HEADS * DIM_HEAD
        b, n, _ = x.shape
        m = context.shape[1]
        scale = DIM_HEAD ** (-0.5)
        q = (x @ Wq).reshape(b, n, HEADS, DIM_HEAD).transpose(0, 2, 1, 3)
        k = (context @ Wk).reshape(b, m, HEADS, DIM_HEAD).transpose(0, 2, 1, 3)
        v = (context @ Wv).reshape(b, m, HEADS, DIM_HEAD).transpose(0, 2, 1, 3)
        scores = jnp.einsum('bhnd,bhmd->bhnm', q, k) * scale
        attn = jax.nn.softmax(scores, axis=-1)
        out = jnp.einsum('bhnm,bhmd->bhnd', attn, v)
        out = out.transpose(0, 2, 1, 3).reshape(b, n, HIDDEN)
        return out @ Wo + bo

    def _L0_ffn_ref(hidden_states, router_w, gate_up_proj, down_proj, shared_gate_w, shared_up_w, shared_down_w):
        import jax, jax.numpy as jnp
        import numpy as np
        B, S, H = (2, 512, 256)
        N, F, SF, K = (16, 256, 1024, 1)
        b, s, h = hidden_states.shape
        hidden = hidden_states.reshape(-1, h)
        t = hidden.shape[0]
        logits = hidden @ router_w.T
        top_vals, top_idx = jax.lax.top_k(logits, K)
        scores = jnp.full_like(logits, -jnp.inf)
        scores = scores.at[jnp.arange(t)[:, None], top_idx].set(top_vals)
        scores = jax.nn.sigmoid(scores.astype(jnp.float32)).astype(hidden.dtype)
        routed_in = hidden[None, :, :] * scores.T[:, :, None]
        gate_up = jnp.einsum('nth,nhf->ntf', routed_in, gate_up_proj)
        gate, up = jnp.split(gate_up, 2, axis=-1)
        routed_out = jnp.einsum('ntf,nfh->nth', up * jax.nn.silu(gate), down_proj)
        expert_sum = routed_out.sum(axis=0)
        shared = jax.nn.silu(hidden @ shared_gate_w.T) * (hidden @ shared_up_w.T) @ shared_down_w.T
        return (shared + expert_sum).reshape(b, s, h)
    x = _layernorm(x + _L0_attn_ref(x, L0_attn_W_in, L0_attn_b_in, L0_attn_log_A, L0_attn_B_p, L0_attn_C_p, L0_attn_W_out, L0_attn_b_out, L0_attn_gamma, L0_attn_beta), axis=-1)
    x = _layernorm(x + _L0_xattn_ref(x, ctx_1024, L0_xattn_Wq, L0_xattn_Wk, L0_xattn_Wv, L0_xattn_Wo, L0_xattn_bo), axis=-1)
    x = _layernorm(x + _L0_ffn_ref(x, L0_ffn_router_w, L0_ffn_gate_up_proj, L0_ffn_down_proj, L0_ffn_shared_gate_w, L0_ffn_shared_up_w, L0_ffn_shared_down_w), axis=-1)
    return x

_drawn_inputs = setup_inputs


def setup_inputs(seed=0):
    import zlib

    import numpy as np

    out = dict(_drawn_inputs(seed))
    spreads = {'L0_attn_b_in': (0.0, 0.372),
     'L0_attn_b_out': (0.0, 0.1),
     'L0_attn_gamma': (1.0, 0.2),
     'L0_attn_beta': (0.0, 0.1)}
    factors = {'L0_attn_log_A': 8.0,
     'L0_xattn_bo': 6.315,
     'L0_ffn_router_w': 8.0,
     'L0_ffn_gate_up_proj': 8.0,
     'L0_ffn_down_proj': 8.0,
     'L0_ffn_shared_gate_w': 8.0,
     'L0_ffn_shared_up_w': 8.0,
     'L0_ffn_shared_down_w': 8.0}
    for name, (base, spread) in spreads.items():
        noise = np.random.default_rng([zlib.crc32(name.encode()), seed]).standard_normal(out[name].shape)
        drawn = base * np.exp(spread * noise) if base else spread * noise
        out[name] = jnp.asarray(drawn.astype(out[name].dtype))
    for name, factor in factors.items():
        out[name] = (out[name] * factor).astype(out[name].dtype)
    return out
```

```python
from contextlib import ExitStack

import concourse.bass as bass
from concourse import mybir

F32 = mybir.dt.float32
F32R = mybir.dt.float32r
I32 = mybir.dt.int32
ALU = mybir.AluOpType
ACT = mybir.ActivationFunctionType
AX = mybir.AxisListType

P = 128
S, D = 2048, 256
TILES = S // P
DK = D // P
KEYS = 1601
KEYS_PAD = 1602
KT = (KEYS + P - 1) // P
LAST = KEYS - (KT - 1) * P
HEADS, DH = 8, 64
HID = HEADS * DH
PAIRS = HEADS // 2
QC = 512
CHUNKS = S // QC
QT = QC // P
EPS = 1e-5
KC = [(0, 402), (402, 400), (802, 400), (1202, 400)]


def before_attention(nc, io, mem):
    K1, K2, V, ident = mem["K1"], mem["K2"], mem["V"], mem["ident"]
    with ExitStack() as ctx:
        def sb(name, shape, dt=F32):
            return ctx.enter_context(nc.sbuf_tensor(name, shape, dt))

        def sem(name):
            return ctx.enter_context(nc.semaphore(name))

        xT = sb("xT", [P, DK, S])
        z = xT[:, :, :].rearrange("p k (a n) -> p (k a) n", n=D)
        state = sb("state", [P, DK, S])
        xring = sb("xring", [P, 2, 4, D])
        w_in = sb("w_in", [P, DK, D])
        w_out = sb("w_out", [P, DK, D])
        ctxT = sb("ctxT", [P, DK, KEYS_PAD])
        wk = sb("wk", [P, DK, HID])
        wv = sb("wv", [P, DK, HID])
        cols = sb("cols", [P, 4, DK])
        rows = sb("rows", [P, 4, D])
        decay = sb("decay", [P, 3, DK])
        bB = sb("bB", [P, DK])
        stats = sb("stats", [P, 4, 2, 6])
        mv = sb("mv", [P, 2, TILES, 2])
        ve = sb("ve", [P, 2, TILES])
        rstd = sb("rstd", [P, 2, TILES])
        mhalf = sb("mhalf", [P, 4])
        x1Tb = sb("x1Tb", [P, 2, DK, P])
        banks = [ctx.enter_context(nc.psum_tensor(f"bank_a{i}", [P, 512], F32)) for i in range(8)]

        d_x = [sem(f"d_xT{c}") for c in range(4)]
        d_small, d_ctx, d_wk, d_wv = sem("d_small"), sem("d_ctx"), sem("d_wk"), sem("d_wv")
        d_xring = [sem(f"d_xring{i}") for i in range(2)]
        d_dup = sem("d_dup")
        d_x1 = sem("d_x1")
        d_x1T = [sem(f"d_x1T{i}") for i in range(2)]
        prep = sem("prep")
        a_exp = sem("a_exp")
        p_in, a_u, v_scan = sem("p_in"), sem("a_u"), sem("v_scan")
        p_out, v_z = sem("p_out"), sem("v_z")
        v_link = sem("v_link")
        v_mv1, v_mv2 = sem("v_mv1"), sem("v_mv2")
        g_const, g_link, g_xb, g_rstd1, g_rstd2 = sem("g_const"), sem("g_link"), sem("g_xb"), sem("g_rstd1"), sem("g_rstd2")
        v_b, v_x1 = sem("v_b"), sem("v_x1")
        p_k, a_khi, v_klo = sem("p_k"), sem("a_khi"), sem("v_klo")
        p_v, a_v = sem("p_v"), sem("a_v")
        p_t, a_t = sem("p_t"), sem("a_t")
        g_x1b = sem("g_x1b")

        G = TILES // 4
        kunits = [(p, j) for p in range(PAIRS) for j in range(len(KC))]
        kv = []
        for n in range(16):
            kv.append(("k", n))
            if n < KT:
                kv.append(("v", n))

        def order(key, val, tr, out=None):
            n = 0
            for t in range(TILES):
                if out:
                    out(t)
                for kind, u in kv[n:n + 2]:
                    (key if kind == "k" else val)(u)
                n += 2
                if tr and t == TILES - 2:
                    for q in range(4):
                        tr(q)
            if tr:
                for q in range(4, TILES):
                    tr(q)

        block = ctx.enter_context(nc.Block())

        @block.sync
        def _(sp):
            sp.dma_start(w_in[:], io["w_inT"].rearrange("(k p) n -> p k n", p=P)).then_inc(d_small, 16)
            sp.dma_start(cols[:], io["cols"]).then_inc(d_small, 16)
            for c in range(4):
                sp.dma_start(xT[:, :, c * 512:(c + 1) * 512],
                             io["xT"].rearrange("(k p) n -> p k n", p=P)[:, :, c * 512:(c + 1) * 512]).then_inc(d_x[c], 16)
            sp.dma_start(w_out[:], io["w_outT"].rearrange("(k p) n -> p k n", p=P)).then_inc(d_small, 16)
            sp.dma_start(wk[:], io["wk"].rearrange("(k p) n -> p k n", p=P)).then_inc(d_wk, 16)
            sp.dma_start(ctxT[:], io["ctxT"].rearrange("(k p) n -> p k n", p=P)).then_inc(d_ctx, 16)
            sp.dma_start(wv[:], io["wv"].rearrange("(k p) n -> p k n", p=P)).then_inc(d_wv, 16)
            for i, n in enumerate(("b_out", "gamma", "beta", "bo")):
                sp.dma_start(rows[:, i, :], io[n].partition_broadcast(P)).then_inc(d_small, 16)
            sp.dma_start(ident[:], io["ident"]).then_inc(d_small, 16)
            for g in range(G):
                if g >= 2:
                    sp.wait_ge(v_b, 4 * (g - 1))
                sp.dma_start(xring[:, g % 2], io["x"].rearrange("(t p) n -> p t n", p=P)[:, 4 * g:4 * g + 4, :]
                             ).then_inc(d_xring[g % 2], 16)
            for h in range(HEADS):
                sp.wait_ge(a_khi, 2 * len(KC) * (h // 2 + 1))
                sp.dma_start(K1[DH:P, h, :].bitcast(F32), K1[0:DH, h, :].bitcast(F32)).then_inc(d_dup, 16)
            for g in range(G):
                sp.wait_ge(g_x1b, g + 1)
                sp.dma_start(io["x1b"].rearrange("(t p) n -> p t n", p=P)[:, 4 * g:4 * g + 4, :],
                             z[:, 4 * g:4 * g + 4, :]).then_inc(d_x1, 16)
            sp.wait_ge(d_x1, 16 * G)
            sp.wait_ge(d_dup, 16 * HEADS)

        @block.gpsimd
        def _(pool):
            pool.memset(mhalf[:], -0.5).then_inc(g_const, 1)
            pool.wait_ge(g_const, 1)
            pool.memset(K2[DH:DH + 1, :, :].bitcast(F32), 1.0).then_inc(g_const, 1)
            pool.wait_ge(g_const, 2)
            pool.wait_ge(d_small, 16 * 8)
            links = [0]

            def link(ins):
                links[0] += 1
                ins.then_inc(g_link, 1)
                pool.wait_ge(g_link, links[0])

            def xb(g):
                pool.wait_ge(d_xring[g % 2], 16 * (g // 2 + 1))
                for t in range(4):
                    ins = pool.tensor_tensor(xring[:, g % 2, t], xring[:, g % 2, t], rows[:, 2, :], ALU.add)
                    ins.then_inc(g_xb, 1)

            def inverse(n, g, ready, done):
                pool.wait_ge(ready, 4 * (g + 1))
                link(pool.tensor_scalar(ve[:, n, 4 * g:4 * g + 4], mv[:, n, 4 * g:4 * g + 4, 1], EPS, None, ALU.add))
                pool.tensor_tensor(rstd[:, n, 4 * g:4 * g + 4], ve[:, n, 4 * g:4 * g + 4], mhalf[:], ALU.pow
                                   ).then_inc(done, 1)

            def x1b(g):
                pool.wait_ge(p_t, 4 * (g + 1))
                pool.wait_ge(v_x1, 4 * (g + 1))
                for t in range(4 * g, 4 * g + 4):
                    ins = pool.tensor_tensor(z[:, t, :], z[:, t, :], rows[:, 3, :], ALU.add)
                ins.then_inc(g_x1b, 1)

            xb(0)
            xb(1)
            for g in range(G + 2):
                if g < G:
                    inverse(0, g, v_mv1, g_rstd1)
                if 1 <= g <= G:
                    inverse(1, g - 1, v_mv2, g_rstd2)
                if g + 2 < G:
                    xb(g + 2)
                if g >= 2:
                    x1b(g - 2)

        @block.scalar
        def _(act):
            act.wait_ge(d_small, 16 * 8)
            act.activation(decay[:, 0], cols[:, 1], ACT.Exp).then_inc(a_exp, 1)
            act.wait_ge(prep, 3)
            for n in range(8):
                c, e = n // 2, n % 2
                act.wait_ge(p_in, n + 1)
                act.activation(state[:, e, c * 512:(c + 1) * 512], banks[n % 2][:], ACT.Identity,
                               bias=bB[:, e:e + 1], scale=cols[:, 2, e:e + 1]).then_inc(a_u, 1)

            def key_high(n):
                p, j = kunits[n]
                k0, kn = KC[j]
                act.wait_ge(p_k, n + 1)
                for h in range(2):
                    act.activation(K1[0:DH, 2 * p + h, k0:k0 + kn], banks[4 + n % 2][DH * h:DH * h + DH, 0:kn],
                                   ACT.Copy).then_inc(a_khi, 1)

            def value(n):
                rows_n = P if n < KT - 1 else LAST
                act.wait_ge(p_v, n + 1)
                act.activation(V[0:rows_n, n, :], banks[6 + n % 2][0:rows_n, :], ACT.Copy).then_inc(a_v, 1)

            def transposed(t):
                act.wait_ge(p_t, t + 1)
                if t >= 2:
                    act.wait_ge(d_x1T[t % 2], 16 * (t // 2))
                act.activation(x1Tb[:, t % 2], banks[t % 2][:, 0:D].rearrange("p (k n) -> p k n", k=DK),
                               ACT.Copy).then_inc(a_t, 1)
                act.wait_ge(a_t, t + 1)
                act.dma_start(io["x1T"].rearrange("(k p) n -> p k n", p=P)[:, :, t * P:(t + 1) * P],
                              x1Tb[:, t % 2]).then_inc(d_x1T[t % 2], 16)

            order(key_high, value, transposed)
            act.wait_ge(d_x1T[0], 16 * TILES // 2)
            act.wait_ge(d_x1T[1], 16 * TILES // 2)

        @block.vector
        def _(dve):
            links = [0]

            def link(ins):
                links[0] += 1
                ins.then_inc(v_link, 1)
                dve.wait_ge(v_link, links[0])

            dve.wait_ge(d_small, 16 * 8)
            dve.wait_ge(a_exp, 1)
            dve.tensor_tensor(bB[:], cols[:, 0], cols[:, 2], ALU.mult).then_inc(prep, 1)
            dve.tensor_scalar(decay[:, 1], decay[:, 0], 1.0, None, ALU.add).then_inc(prep, 1)
            dve.wait_ge(prep, 2)
            dve.reciprocal(decay[:, 2], decay[:, 1]).then_inc(prep, 1)
            for k in range(DK):
                dve.tensor_scalar(w_out[:, k], w_out[:, k], cols[:, 3, k:k + 1], None, ALU.mult).then_inc(prep, 1)
            dve.wait_ge(prep, 3)
            for n in range(8):
                c, e = n // 2, n % 2
                dve.wait_ge(a_u, n + 1)
                if c:
                    dve.wait_ge(v_scan, n - 1)
                u = state[:, e, c * 512:(c + 1) * 512]
                dve.tensor_tensor_scan(u, decay[:, 2, e:e + 1].to_broadcast([P, 512]), u,
                                       state[:, e, c * 512 - 1:c * 512] if c else 0.0,
                                       ALU.mult, ALU.add).then_inc(v_scan, 1)

            def key_low(n):
                p, j = kunits[n]
                k0, kn = KC[j]
                dve.wait_ge(a_khi, 2 * (n + 1))
                for h in range(2):
                    dve.tensor_tensor(K2[0:DH, 2 * p + h, k0:k0 + kn], banks[4 + n % 2][DH * h:DH * h + DH, 0:kn],
                                      K1[0:DH, 2 * p + h, k0:k0 + kn].bitcast(F32), ALU.subtract).then_inc(v_klo, 1)

            def norm_a(t):
                dve.wait_ge(p_out, t + 1)
                dve.tensor_tensor(z[:, t], banks[2 + t % 2][:, 0:D], rows[:, 0, :], ALU.add).then_inc(v_z, 1)
                dve.wait_ge(v_z, t + 1)
                link(dve.bn_stats(stats[:, t % 4, 0, :], z[:, t]))
                dve.bn_aggr(mv[:, 0, t], stats[:, t % 4, 0, :]).then_inc(v_mv1, 1)

            def norm_b(t):
                if t % 4 == 0:
                    dve.wait_ge(g_rstd1, t // 4 + 1)
                dve.wait_ge(g_xb, t + 1)
                link(dve.scalar_tensor_tensor(z[:, t], z[:, t], mv[:, 0, t, 0:1], rows[:, 1, :], ALU.subtract, ALU.mult))
                dve.scalar_tensor_tensor(z[:, t], z[:, t], rstd[:, 0, t:t + 1], xring[:, (t // 4) % 2, t % 4],
                                         ALU.mult, ALU.add).then_inc(v_b, 1)
                dve.wait_ge(v_b, t + 1)
                link(dve.bn_stats(stats[:, t % 4, 1, :], z[:, t]))
                dve.bn_aggr(mv[:, 1, t], stats[:, t % 4, 1, :]).then_inc(v_mv2, 1)

            def norm_c(t):
                if t % 4 == 0:
                    dve.wait_ge(g_rstd2, t // 4 + 1)
                dve.tensor_scalar(z[:, t], z[:, t], mv[:, 1, t, 0:1], rstd[:, 1, t:t + 1],
                                  ALU.subtract, ALU.mult).then_inc(v_x1, 1)

            def token_tile(t):
                norm_a(t)
                if t >= 5:
                    norm_b(t - 5)
                if t >= 10:
                    norm_c(t - 10)

            order(key_low, lambda n: None, None, token_tile)
            for t in range(TILES, TILES + 10):
                if t - 5 < TILES:
                    norm_b(t - 5)
                if t - 10 < TILES:
                    norm_c(t - 10)

        @block.tensor
        def _(pe):
            for n in range(8):
                c, e = n // 2, n % 2
                if n == 0:
                    pe.wait_ge(d_small, 16 * 8)
                pe.wait_ge(d_x[c], 16)
                if n >= 2:
                    pe.wait_ge(a_u, n - 1)
                for k in range(DK):
                    mm = pe.matmul(banks[n % 2][:], w_in[:, k, e * P:(e + 1) * P], xT[:, k, c * 512:(c + 1) * 512],
                                   start=(k == 0), stop=(k == DK - 1))
                mm.then_inc(p_in, 1)
            pe.wait_ge(d_wk, 16)
            pe.wait_ge(d_wv, 16)
            pe.wait_ge(d_ctx, 16)
            pe.wait_ge(prep, 5)
            pe.wait_ge(a_u, 8)

            def out_proj(t):
                pe.wait_ge(v_scan, 2 * (t // 4 + 1))
                if t >= 2:
                    pe.wait_ge(v_z, t - 1)
                for k in range(DK):
                    mm = pe.matmul(banks[2 + t % 2][:, 0:D], state[:, k, t * P:(t + 1) * P], w_out[:, k, :],
                                   start=(k == 0), stop=(k == DK - 1))
                mm.then_inc(p_out, 1)

            def key(n):
                p, j = kunits[n]
                k0, kn = KC[j]
                if n >= 2:
                    pe.wait_ge(v_klo, 2 * (n - 1))
                for k in range(DK):
                    mm = pe.matmul(banks[4 + n % 2][:, 0:kn], wk[:, k, p * P:(p + 1) * P], ctxT[:, k, k0:k0 + kn],
                                   start=(k == 0), stop=(k == DK - 1))
                mm.then_inc(p_k, 1)

            def val(n):
                rows_n = P if n < KT - 1 else LAST
                if n >= 2:
                    pe.wait_ge(a_v, n - 1)
                for k in range(DK):
                    mm = pe.matmul(banks[6 + n % 2][0:rows_n, :], ctxT[:, k, n * P:n * P + rows_n], wv[:, k, :],
                                   start=(k == 0), stop=(k == DK - 1))
                mm.then_inc(p_v, 1)

            def transpose(t):
                pe.wait_ge(v_x1, t + 1)
                if t >= 2:
                    pe.wait_ge(a_t, t - 1)
                for k in range(DK):
                    mm = pe.transpose(banks[t % 2][:, k * P:(k + 1) * P], z[:, t, k * P:(k + 1) * P], ident[:])
                mm.then_inc(p_t, 1)

            order(key, val, transpose, out_proj)


STEP_MX = 1 + 2 * QT * len(KC)
CHUNK_MX = PAIRS * STEP_MX + 2
G_ADDS = KT - 2
SEED = 1
RING = 4


def attention(nc, io, mem):
    K1, K2, V, ident = mem["K1"], mem["K2"], mem["V"], mem["ident"]
    with ExitStack() as ctx:
        def sb(name, shape, dt=F32):
            return ctx.enter_context(nc.sbuf_tensor(name, shape, dt))

        def sem(name):
            return ctx.enter_context(nc.semaphore(name))

        wq = sb("wq", [P, DK, HID])
        wo = sb("wo", [P, PAIRS, D])
        x1T = sb("x1T", [P, DK, QC])
        x1 = sb("x1", [P, QT, D])
        Q1 = sb("Q1", [P, 2, 2, QC], F32R)
        Q2 = sb("Q2", [P, 2, 2, QC], F32R)
        probs = sb("probs", [P, RING, 2 * QC])
        accD = sb("accD", [P, 2 * QC])
        accG = sb("accG", [P, 2 * QC])
        ones = sb("ones", [P, DH])
        o_raw = sb("o_raw", [P, QC])
        rsum = sb("rsum", [P, QC])
        oT = sb("oT", [P, PAIRS, QC])
        mxp = sb("mxp", [P, 2, 2 * QT, len(KC)])
        nm = sb("nm", [P, 2, 2 * QT])
        mrow = sb("mrow", [2 * QT, 2, P], F32R)
        st6 = sb("st6", [P, QT, 6])
        mv3 = sb("mv3", [P, QT, 2])
        ve3 = sb("ve3", [P, QT])
        rstd3 = sb("rstd3", [P, QT])
        eps3 = sb("eps3", [P, QT])
        mhalf3 = sb("mhalf3", [P, QT])
        st = [ctx.enter_context(nc.psum_tensor(f"st{i}", [P, 2 * QC], F32)) for i in range(2)]
        av = ctx.enter_context(nc.psum_tensor("av", [P, QC], F32))
        misc = ctx.enter_context(nc.psum_tensor("misc", [P, QC], F32))
        mx = [ctx.enter_context(nc.psum_tensor(f"mx{i}", [P, QC], F32)) for i in range(2)]

        d_w, d_x1Tc, d_x1c, d_x2 = sem("d_w"), sem("d_x1Tc"), sem("d_x1c"), sem("d_x2")
        d_q2 = [sem(f"d_q2_{i}") for i in range(2)]
        d_m = [sem(f"d_m_{i}") for i in range(2)]
        p_q, a_hi, v_lo = sem("p_q"), sem("a_hi"), sem("v_lo")
        p_mx, v_mx, v_nm, p_mT, v_mT = sem("p_mx"), sem("v_mx"), sem("v_nm"), sem("p_mT"), sem("v_mT")
        p_qk = sem("p_qk")
        a_probs = sem("a_probs")
        p_pv = sem("p_pv")
        v_add, g_add = sem("v_add"), sem("g_add")
        a_av, p_sum, v_misc, v_o = sem("a_av"), sem("p_sum"), sem("v_misc"), sem("v_o")
        p_wo, v_r, v_mv3, g_rs3, v_x2 = sem("p_wo"), sem("v_r"), sem("v_mv3"), sem("g_rs3"), sem("v_x2")
        v_stats = sem("v_stats")
        s_free = sem("s_free")
        v_link3, g_link3, g_ones = sem("v_link3"), sem("g_link3"), sem("g_ones")

        def rows_of(t):
            return P if t < KT - 1 else LAST

        def mx_use(c, p, j):
            return c * CHUNK_MX + STEP_MX * (p + 1) + j

        def out_use(c, last):
            return c * CHUNK_MX + STEP_MX * (PAIRS if last else PAIRS + 1)

        def max_use(c, p):
            return c * 2 * PAIRS + max(2 * p - 1, 0)

        def sum_use(c, p):
            return c * 2 * PAIRS + min(2 * p + 2, 2 * PAIRS - 1)

        def parity(p):
            return (p + 1) % 2

        block = ctx.enter_context(nc.Block())

        @block.sync
        def _(sp):
            sp.dma_start(wq[:], io["wq"].rearrange("(k p) n -> p k n", p=P)).then_inc(d_w, 16)
            sp.dma_start(x1T[:], io["x1T"].rearrange("(k p) n -> p k n", p=P)[:, :, 0:QC]).then_inc(d_x1Tc, 16)
            sp.dma_start(wo[:], io["wo"].rearrange("(k p) n -> p k n", p=P)).then_inc(d_w, 16)
            sp.dma_start(x1[:], io["x1b"].rearrange("(t p) n -> p t n", p=P)[:, 0:QT, :]).then_inc(d_x1c, 16)

            def queries(F, par, n):
                sp.wait_ge(a_hi, (F + 1) * 2)
                sp.sem_inc(s_free, 1)
                if n:
                    sp.wait_ge(p_qk, SEED + (F - 1) * KT)
                sp.sem_inc(s_free, 1)
                sp.dma_start(Q2[0:DH, par].bitcast(F32), Q1[0:DH, par].bitcast(F32)).then_inc(d_q2[par], 16)

            def maxima(F, par):
                sp.wait_ge(v_mT, F + 1)
                sp.sem_inc(s_free, 1)
                for h in range(2):
                    sp.dma_start(Q2[DH:DH + 1, par, h, :].bitcast(F32), mrow[QT * h:QT * h + QT, par, :].bitcast(F32)
                                 ).then_inc(d_m[par], 16)

            def chunk(c, last):
                for p in range(PAIRS):
                    F = c * PAIRS + (p + 1)
                    maxima(c * PAIRS + p, p % 2)
                    if not (last and p == PAIRS - 1):
                        queries(F, parity(p), True)
                    if p == PAIRS - 2 and not last:
                        sp.wait_ge(p_q, (c + 1) * PAIRS)
                        sp.sem_inc(s_free, 1)
                        sp.sem_inc(s_free, 1)
                        sp.dma_start(x1T[:], io["x1T"].rearrange("(k p) n -> p k n", p=P)[:, :, bass.ds((c + 1) * QC, QC)]
                                     ).then_inc(d_x1Tc, 16)
                sp.wait_ge(v_x2, (c + 1) * QT)
                sp.sem_inc(s_free, 1)
                sp.dma_start(io["x2"].rearrange("(t p) n -> p t n", p=P)[:, bass.ds(c * QT, QT), :], x1[:]).then_inc(d_x2, 16)
                sp.sem_inc(s_free, 1)
                sp.wait_ge(d_x2, (c + 1) * 16)
                sp.sem_inc(s_free, 1)
                if not last:
                    sp.sem_inc(s_free, 1)
                    sp.dma_start(x1[:], io["x1b"].rearrange("(t p) n -> p t n", p=P)[:, bass.ds((c + 1) * QT, QT), :]
                                 ).then_inc(d_x1c, 16)

            queries(0, 0, False)
            with sp.Fori(0, CHUNKS - 1) as c:
                chunk(c, False)
            chunk(CHUNKS - 1, True)

        @block.gpsimd
        def _(pool):
            pool.sem_inc(g_add, G_ADDS)
            pool.memset(ones[:], 1.0).then_inc(g_ones, 1)
            pool.wait_ge(g_ones, 1)
            pool.memset(mhalf3[:], -0.5).then_inc(g_ones, 1)
            pool.wait_ge(g_ones, 2)
            pool.memset(eps3[:], EPS).then_inc(g_ones, 1)
            pool.wait_ge(g_ones, 3)

            def chunk(c):
                for p in range(PAIRS):
                    for n, t in enumerate(range(2, KT)):
                        r = rows_of(t)
                        pool.wait_ge(a_probs, (c * PAIRS + p) * KT + (2 + t + 1))
                        if n == 0:
                            pool.wait_ge(p_sum, SEED + c * PAIRS + p)
                            pool.wait_ge(v_add, c * PAIRS + (p + 1))
                            so_far = accD
                        else:
                            so_far = accG
                            pool.wait_ge(g_add, (c * PAIRS + p) * G_ADDS + (G_ADDS + n))
                        pool.tensor_tensor(accG[0:r], so_far[0:r], probs[0:r, (p * KT + t) % RING], ALU.add).then_inc(g_add, 1)
                pool.wait_ge(g_add, (c * PAIRS + PAIRS) * G_ADDS + G_ADDS)
                pool.wait_ge(v_mv3, (c + 1) * QT)
                pool.tensor_tensor(ve3[:], mv3[:, :, 1], eps3[:], ALU.add).then_inc(g_link3, 1)
                pool.wait_ge(g_link3, c + 1)
                pool.tensor_tensor(rstd3[:], ve3[:], mhalf3[:], ALU.pow).then_inc(g_rs3, 1)
                pool.wait_ge(g_rs3, c + 1)

            with pool.Fori(0, CHUNKS) as c:
                chunk(c)

        @block.scalar
        def _(act):
            act.sem_inc(a_probs, 2)
            act.sem_inc(a_av, SEED)

            def q_high(F, par, h, n):
                act.wait_ge(p_q, F + 1)
                if n and h == 0:
                    act.wait_ge(p_qk, SEED + (F - 1) * KT)
                act.activation(Q1[0:DH, par, h], mx[par][DH * h:DH * h + DH, :], ACT.Copy).then_inc(a_hi, 1)

            def exp(c, p, t):
                g = p * KT + t
                s, r = g % RING, rows_of(t)
                act.wait_ge(p_qk, SEED + c * PAIRS * KT + (g + 1))
                act.wait_ge(p_pv, c * PAIRS * KT + (g + 1))
                old = (t - RING) % KT
                if old < 2:
                    act.wait_ge(v_add, c * PAIRS + (p + 1))
                else:
                    since = p + (1 if t >= RING else 0)
                    act.wait_ge(g_add, c * PAIRS * G_ADDS + (since * G_ADDS + (old - 1)))
                act.activation(probs[0:r, s], st[g % 2][0:r, :], ACT.Exp, scale=DH ** -0.5).then_inc(a_probs, 1)

            def copy_av(c, p):
                act.wait_ge(p_pv, (c * PAIRS + (p + 1)) * KT + RING)
                act.wait_ge(v_o, SEED + c * PAIRS + p)
                act.activation(o_raw[:], av[:], ACT.Copy).then_inc(a_av, 1)

            def chunk(c, last):
                for p in range(PAIRS):
                    ahead = not (last and p == PAIRS - 1)
                    F = c * PAIRS + (p + 1)
                    if ahead:
                        q_high(F, parity(p), 0, True)
                        q_high(F, parity(p), 1, True)
                    if p > 0:
                        copy_av(c, p - 1)
                    for t in range(KT):
                        exp(c, p, t)
                copy_av(c, PAIRS - 1)

            for h in range(2):
                q_high(0, 0, h, False)
            with act.Fori(0, CHUNKS - 1) as c:
                chunk(c, False)
            chunk(CHUNKS - 1, True)

        @block.vector
        def _(dve):
            def q_low(F, par):
                for h in range(2):
                    dve.wait_ge(a_hi, F * 2 + (h + 1))
                    ins = dve.tensor_tensor(Q1[DH:P, par, h], mx[par][DH * h:DH * h + DH, :],
                                            Q1[0:DH, par, h].bitcast(F32), ALU.subtract).then_inc(v_lo, 1)
                dve.wait_ge(v_lo, F * 2 + 2)
                dve.sem_inc(v_mx, 1)

            def piece_maxima(F, use, par):
                for u in range(2 * QT):
                    for j, (k0, kn) in enumerate(KC):
                        n = len(KC) * u + j + 1
                        dve.wait_ge(p_mx, F * (STEP_MX - 1) + n)
                        dve.tensor_reduce(mxp[:, par, u, j:j + 1], mx[(par + n) % 2][:, 0:kn], AX.X, ALU.max
                                          ).then_inc(v_mx, 1)
                dve.wait_ge(v_mx, use + STEP_MX)
                dve.tensor_reduce(nm[:, par], mxp[:, par], AX.X, ALU.max, negate=True).then_inc(v_nm, 1)

            def max_row(F, par):
                dve.wait_ge(p_mT, F + 1)
                dve.tensor_copy(mrow[:, par], misc[0:2 * QT, 0:P]).then_inc(v_mT, 1)
                dve.wait_ge(v_mT, F + 1)
                dve.sem_inc(v_misc, 1)

            def divide(c, p):
                S0 = c * PAIRS + p
                dve.wait_ge(p_sum, SEED + S0 + 1)
                dve.wait_ge(v_o, SEED + S0)
                dve.reciprocal(rsum[:], misc[:]).then_inc(v_misc, 1)
                dve.wait_ge(v_misc, SEED + sum_use(c, p) + 1)
                dve.wait_ge(a_av, SEED + S0 + 1)
                if p == 0:
                    dve.wait_ge(p_wo, SEED + c * QT)
                dve.tensor_tensor(oT[:, p], o_raw[:], rsum[:], ALU.mult).then_inc(v_o, 1)

            def chunk(c, last):
                for p in range(PAIRS):
                    ahead = not (last and p == PAIRS - 1)
                    F = c * PAIRS + (p + 1)
                    max_row(c * PAIRS + p, p % 2)
                    if ahead:
                        q_low(F, parity(p))
                    dve.wait_ge(a_probs, (c * PAIRS + p) * KT + 4)
                    dve.wait_ge(g_add, (c * PAIRS + p) * G_ADDS + 1)
                    dve.tensor_tensor(accD[:], probs[:, (p * KT) % RING], probs[:, (p * KT + 1) % RING], ALU.add
                                      ).then_inc(v_add, 1)
                    if p > 0:
                        divide(c, p - 1)
                    if ahead:
                        piece_maxima(F, mx_use(c, p, 0), parity(p))
                divide(c, PAIRS - 1)
                for i in range(QT):
                    if i % 2 == 0:
                        dve.wait_ge(p_wo, SEED + c * QT + (i + 2))
                    if i == 0:
                        dve.wait_ge(d_x1c, (c + 1) * 16)
                    bank = mx[(out_use(0, last) + i // 2) % 2]
                    dve.tensor_tensor(x1[:, i], bank[:, (i % 2) * D:(i % 2 + 1) * D], x1[:, i], ALU.add).then_inc(v_r, 1)
                    dve.wait_ge(v_r, c * QT + (i + 1))
                    if i % 2:
                        dve.sem_inc(v_mx, 1)
                    dve.bn_stats(st6[:, i], x1[:, i]).then_inc(v_link3, 1)
                    dve.wait_ge(v_link3, c * QT + (i + 1))
                    dve.sem_inc(v_stats, 1)
                    dve.bn_aggr(mv3[:, i], st6[:, i]).then_inc(v_mv3, 1)
                dve.wait_ge(g_rs3, c + 1)
                for i in range(QT):
                    dve.tensor_scalar(x1[:, i], x1[:, i], mv3[:, i, 0:1], rstd3[:, i:i + 1], ALU.subtract, ALU.mult
                                      ).then_inc(v_x2, 1)

            dve.sem_inc(v_o, SEED)
            dve.sem_inc(v_misc, SEED)
            q_low(0, 0)
            piece_maxima(0, 0, 0)
            with dve.Fori(0, CHUNKS - 1) as c:
                chunk(c, False)
            chunk(CHUNKS - 1, True)

        @block.tensor
        def _(pe):
            pe.sem_inc(p_pv, RING)
            for begun in (p_qk, p_sum, p_wo):
                pe.sem_inc(begun, SEED)

            def q_proj(pair, par):
                for k in range(DK):
                    mm = pe.matmul(mx[par][:], wq[:, k, pair * P:(pair + 1) * P], x1T[:, k, :],
                                   start=(k == 0), stop=(k == DK - 1))
                mm.then_inc(p_q, 1)

            def max_scores(F, pair, par, use, n):
                u, j = (n - 1) // len(KC), (n - 1) % len(KC)
                h, i = u // QT, u % QT
                k0, kn = KC[j]
                if n == 1:
                    pe.wait_ge(v_lo, F * 2 + 2)
                if use is not None:
                    pe.wait_ge(v_mx, use + (n - 1))
                elif n >= 2:
                    pe.wait_ge(v_mx, n - 1)
                pe.matmul(mx[(par + n) % 2][:, 0:kn], Q1[:, par, h, i * P:(i + 1) * P], K1[:, 2 * pair + h, k0:k0 + kn],
                          start=True, stop=True).then_inc(p_mx, 1)

            def max_transpose(c, p):
                pe.wait_ge(v_nm, c * PAIRS + (p + 1))
                pe.wait_ge(v_misc, SEED + max_use(c, p))
                pe.transpose(misc[0:2 * QT, 0:P], nm[:, p % 2], ident[:]).then_inc(p_mT, 1)

            def scores_1(c, p, t):
                g, r = p * KT + t, rows_of(t)
                pe.wait_ge(a_probs, c * PAIRS * KT + (g + 1))
                for h in range(2):
                    pe.matmul(st[g % 2][0:r, h * QC:(h + 1) * QC], K1[:, 2 * p + h, t * P:t * P + r], Q1[:, p % 2, h],
                              start=True, stop=False)

            def scores_2(c, p, t):
                g, r = p * KT + t, rows_of(t)
                par = p % 2
                if t == 0:
                    pe.wait_ge(d_q2[par], (c * 2 + (p // 2 + 1)) * 16)
                    pe.wait_ge(d_m[par], (c * 2 + (p // 2 + 1)) * 32)
                for h in range(2):
                    mm = pe.matmul(st[g % 2][0:r, h * QC:(h + 1) * QC], K2[0:DH + 1, 2 * p + h, t * P:t * P + r],
                                   Q2[0:DH + 1, par, h], start=False, stop=True)
                mm.then_inc(p_qk, 1)

            def values(c, p, t):
                g, r = p * KT + t, rows_of(t)
                pe.wait_ge(a_probs, c * PAIRS * KT + (g + 3))
                if t == 0:
                    pe.wait_ge(a_av, SEED + c * PAIRS + p)
                for h in range(2):
                    mm = pe.matmul(av[h * DH:(h + 1) * DH, :], V[0:r, t, (2 * p + h) * DH:(2 * p + h + 1) * DH],
                                   probs[0:r, g % RING, h * QC:(h + 1) * QC], start=(t == 0), stop=(t == KT - 1))
                mm.then_inc(p_pv, 1)

            def sums(c, p):
                S0 = c * PAIRS + p
                pe.wait_ge(g_add, (S0 + 2) * G_ADDS)
                pe.wait_ge(v_misc, SEED + sum_use(c, p))
                for h in range(2):
                    mm = pe.matmul(misc[h * DH:(h + 1) * DH, :], ones[:], accG[:, h * QC:(h + 1) * QC], start=True, stop=True)
                mm.then_inc(p_sum, 1)

            def output(c, last):
                for end in (False, True):
                    pe.wait_ge(v_o, SEED + c * PAIRS + (PAIRS if end else PAIRS - 1))
                    for i in range(QT):
                        use = out_use(c, last) + i // 2
                        bank = mx[(out_use(0, last) + i // 2) % 2]
                        if not end and i % 2 == 0:
                            pe.wait_ge(v_mx, use - 1)
                        for p in ((PAIRS - 1,) if end else range(PAIRS - 1)):
                            mm = pe.matmul(bank[:, (i % 2) * D:(i % 2 + 1) * D], oT[:, p, i * P:(i + 1) * P], wo[:, p, :],
                                           start=(p == 0 and i % 2 == 0), stop=end, skip_group_check=True)
                        if end:
                            mm.then_inc(p_wo, 1)

            def chunk(c, last):
                for p in range(PAIRS):
                    ahead = not (last and p == PAIRS - 1)
                    F, pair, par = c * PAIRS + (p + 1), (p + 1) % PAIRS, parity(p)
                    use = mx_use(c, p, 0)
                    done = [0]

                    def next_piece():
                        done[0] += 1
                        if ahead and done[0] < STEP_MX:
                            max_scores(F, pair, par, use, done[0])

                    scores_1(c, p, 0)
                    scores_1(c, p, 1)
                    max_transpose(c, p)
                    if ahead:
                        pe.wait_ge(v_mx, use - 1)
                        if pair == 0:
                            pe.wait_ge(d_x1Tc, (c + 2) * 16)
                        q_proj(pair, par)
                    if p > 0:
                        values(c, p - 1, KT - 1)
                    scores_2(c, p, 0)
                    scores_2(c, p, 1)
                    if p > 0:
                        sums(c, p - 1)
                    values(c, p, 0)
                    for t in range(2, KT):
                        scores_1(c, p, t)
                        next_piece()
                        scores_2(c, p, t)
                        next_piece()
                        values(c, p, t - 1)
                        next_piece()
                values(c, PAIRS - 1, KT - 1)
                sums(c, PAIRS - 1)
                output(c, last)

            pe.wait_ge(d_w, 32)
            pe.wait_ge(d_x1Tc, 16)
            pe.wait_ge(g_ones, 1)
            q_proj(0, 0)
            for n in range(1, STEP_MX):
                max_scores(0, 0, 0, None, n)
            with pe.Fori(0, CHUNKS - 1) as c:
                chunk(c, False)
            chunk(CHUNKS - 1, True)


EXPERTS, FE = 16, 256
SF = 1024
FK = SF // P
ETILES = TILES + EXPERTS - 1
GRID_REV, GRID_THR, GRID_J = 0, EXPERTS, EXPERTS + TILES


def route_and_share(nc, io, mem):
    base, pos, te, ident = mem["base"], mem["pos"], mem["te"], mem["ident2"]
    with ExitStack() as ctx:
        def sb(name, shape, dt=F32):
            return ctx.enter_context(nc.sbuf_tensor(name, shape, dt))

        def sem(name):
            return ctx.enter_context(nc.semaphore(name))

        x2 = sb("x2", [P, TILES, D])
        x2s = sb("x2s", [P, TILES, D])
        x2T = sb("x2T", [P, DK, S])
        wr = sb("wr", [P, DK, EXPERTS])
        wg = sb("wg", [P, DK, SF])
        wu = sb("wu", [P, DK, SF])
        wd = sb("wd", [P, FK, D])
        upper = sb("upper", [P, P])
        allone = sb("allone", [P, P])
        grid = sb("grid", [P, EXPERTS + TILES + 2 * TILES])
        zero = sb("zero", [P, 4, D])
        silu = sb("silu", [P, 2, 512])
        hT = sb("hT", [P, FK, 512])
        lg = sb("lg", [P, TILES, EXPERTS])
        top = sb("top", [P, TILES])
        esc = sb("esc", [P, 3, TILES])
        work = sb("work", [P, 2, TILES, EXPERTS])
        oneh = sb("oneh", [P, TILES, EXPERTS])
        rev = sb("rev", [P, TILES])
        carry = sb("carry", [P, TILES + 1, EXPERTS])
        nt = sb("nt", [P, EXPERTS])
        incl = sb("incl", [P, EXPERTS])
        off = sb("off", [P, 2, EXPERTS])
        posf = sb("posf", [P, TILES])
        cmpj = sb("cmpj", [P, 2 * TILES, EXPERTS])
        tef = sb("tef", [P, 2, 2 * TILES])
        onesr = sb("onesr", [P, EXPERTS])
        bt = [ctx.enter_context(nc.psum_tensor(f"bt{i}", [P, 512], F32)) for i in range(2)]
        bg = [ctx.enter_context(nc.psum_tensor(f"bg{i}", [P, 512], F32)) for i in range(2)]
        bu = [ctx.enter_context(nc.psum_tensor(f"bu{i}", [P, 512], F32)) for i in range(2)]
        br = ctx.enter_context(nc.psum_tensor("br", [P, 512], F32))
        bp = ctx.enter_context(nc.psum_tensor("bp", [P, 512], F32))

        d_x2i, d_r, d_wg, d_wu, d_wd, d_zero, d_scatter = (sem("d_x2i"), sem("d_r"), sem("d_wg"), sem("d_wu"),
                                                           sem("d_wd"), sem("d_zero"), sem("d_scatter"))
        g_zero = sem("g_zero")
        p_tr, a_tr, p_lg = sem("p_tr"), sem("a_tr"), sem("p_lg")
        v_route = sem("v_route")
        a_sc, v_oh, p_px, v_pos, v_score, g_x2s = (sem("a_sc"), sem("v_oh"), sem("p_px"), sem("v_pos"),
                                                   sem("v_score"), sem("g_x2s"))
        p_gu, a_silu, v_h, p_dn, v_base = sem("p_gu"), sem("a_silu"), sem("v_h"), sem("p_dn"), sem("v_base")

        block = ctx.enter_context(nc.Block())

        @block.sync
        def _(sp):
            sp.dma_start(ident[:], io["ident"]).then_inc(d_r, 16)
            sp.dma_start(x2[:], io["x2"].rearrange("(t p) n -> p t n", p=P)).then_inc(d_x2i, 16)
            sp.dma_start(wr[:], io["routerT"].rearrange("(k p) n -> p k n", p=P)).then_inc(d_r, 16)
            sp.dma_start(grid[:], io["grid"]).then_inc(d_r, 16)
            sp.dma_start(upper[:], io["upper"]).then_inc(d_r, 16)
            sp.dma_start(wg[:], io["s_gateT"].rearrange("(k p) n -> p k n", p=P)).then_inc(d_wg, 16)
            sp.dma_start(wu[:], io["s_upT"].rearrange("(k p) n -> p k n", p=P)).then_inc(d_wu, 16)
            sp.dma_start(wd[:], io["s_downT"].rearrange("(k p) n -> p k n", p=P)).then_inc(d_wd, 16)
            sp.wait_ge(g_zero, 1)
            for t in range(0, 2 * TILES, 4):
                sp.dma_start(io["sorted_x"].rearrange("(t p) n -> p t n", p=P)[:, t:t + 4, :], zero[:]).then_inc(d_zero, 16)
            sp.wait_ge(d_zero, 16 * 2 * TILES // 4)
            sp.wait_ge(d_scatter, 16 * TILES)

        @block.gpsimd
        def _(pool):
            pool.memset(zero[:], 0.0).then_inc(g_zero, 1)
            pool.wait_ge(g_zero, 1)
            pool.memset(allone[:], 1.0).then_inc(g_zero, 1)
            pool.wait_ge(g_zero, 2)
            pool.memset(onesr[:], 1.0).then_inc(g_zero, 1)
            pool.wait_ge(g_zero, 3)
            pool.memset(carry[:, 0, :], 0.0).then_inc(g_zero, 1)
            pool.wait_ge(g_zero, 4)
            pool.wait_ge(v_score, 2)
            for t in range(TILES):
                pool.tensor_scalar(x2s[:, t], x2[:, t], esc[:, 2, t:t + 1], 0.0, ALU.mult, ALU.add).then_inc(g_x2s, 1)
            pool.wait_ge(v_pos, 1)
            pool.wait_ge(d_zero, 16 * 2 * TILES // 4)
            for t in range(TILES):
                pool.wait_ge(g_x2s, t + 1)
                pool.indirect_dma_start(io["sorted_x"][:, :], bass.IndirectOffsetOnAxis(pos[:, t:t + 1], 0),
                                        x2s[:, t, :], None).then_inc(d_scatter, 16)

        @block.scalar
        def _(act):
            for t in range(TILES):
                act.wait_ge(p_tr, t + 1)
                act.activation(x2T[:, :, t * P:(t + 1) * P], bt[t % 2][:, 0:D].rearrange("p (k n) -> p k n", k=DK),
                               ACT.Copy).then_inc(a_tr, 1)
            act.wait_ge(v_route, 2)
            act.activation(esc[:, 0], top[:], ACT.Exp, scale=-1.0).then_inc(a_sc, 1)

            def gates(c):
                for f in range(FK):
                    act.wait_ge(p_gu, c * FK + (f + 1))
                    if f > 1 or not isinstance(c, int):
                        act.wait_ge(v_h, c * FK + max(f - 1, 0))
                    act.activation(silu[:, f % 2], bg[f % 2][:], ACT.Silu).then_inc(a_silu, 1)

            gates(0)
            with act.Fori(1, CHUNKS) as c:
                gates(c)

        @block.vector
        def _(dve):
            n_route = [0]

            def step(ins):
                n_route[0] += 1
                ins.then_inc(v_route, 1)
                dve.wait_ge(v_route, n_route[0])

            def by_tile(ap):
                return ap.unsqueeze(2).to_broadcast([P, TILES, EXPERTS])

            def by_expert(ap, n=TILES):
                return ap.unsqueeze(1).to_broadcast([P, n, EXPERTS])

            def choose():
                dve.wait_ge(p_lg, 1)
                dve.wait_ge(d_r, 64)
                step(dve.tensor_copy(lg[:], br[:, 0:TILES * EXPERTS].rearrange("p (t n) -> p t n", n=EXPERTS)))
                step(dve.tensor_reduce(top[:], lg[:], AX.X, ALU.max))
                step(dve.tensor_tensor(work[:, 0], lg[:], by_tile(top[:]), ALU.is_equal))
                step(dve.tensor_tensor(work[:, 1], work[:, 0], by_expert(grid[:, GRID_REV:GRID_REV + EXPERTS]), ALU.mult))
                step(dve.tensor_reduce(rev[:], work[:, 1], AX.X, ALU.max))
                dve.tensor_tensor(oneh[:], by_expert(grid[:, GRID_REV:GRID_REV + EXPERTS]), by_tile(rev[:]), ALU.is_equal
                                  ).then_inc(v_oh, 1)
                dve.wait_ge(a_sc, 1)
                dve.tensor_scalar(esc[:, 1], esc[:, 0], 1.0, None, ALU.add).then_inc(v_score, 1)
                dve.wait_ge(v_score, 1)
                dve.reciprocal(esc[:, 2], esc[:, 1]).then_inc(v_score, 1)

            def count():
                dve.wait_ge(p_px, 1)
                dve.wait_ge(g_zero, 4)
                for t in range(TILES):
                    step(dve.tensor_tensor(carry[:, t + 1], bp[:, 256 + t * EXPERTS:256 + (t + 1) * EXPERTS], carry[:, t],
                                           ALU.add))

            def place():
                counts = carry[:, TILES, :].unsqueeze(2).to_broadcast([P, EXPERTS, TILES])
                thresholds = grid[:, GRID_THR:GRID_THR + TILES].unsqueeze(1).to_broadcast([P, EXPERTS, TILES])
                step(dve.tensor_tensor(work[:, 0], counts, thresholds, ALU.is_gt))
                step(dve.tensor_reduce(nt[:], work[:, 0], AX.X, ALU.add))
                step(dve.tensor_tensor_scan(incl[:], onesr[:], nt[:], 0.0, ALU.mult, ALU.add))
                step(dve.tensor_tensor(off[:, 0], incl[:], nt[:], ALU.subtract))
                step(dve.tensor_scalar(off[:, 1], off[:, 0], float(P), None, ALU.mult))
                step(dve.tensor_tensor(work[:, 0], bp[:, 0:256].rearrange("p (t n) -> p t n", n=EXPERTS),
                                       carry[:, 0:TILES, :], ALU.add))
                step(dve.tensor_tensor(work[:, 1], work[:, 0], by_expert(off[:, 1]), ALU.add))
                step(dve.tensor_tensor(work[:, 0], work[:, 1], oneh[:], ALU.mult))
                step(dve.tensor_reduce(posf[:], work[:, 0], AX.X, ALU.add))
                dve.tensor_copy(pos[:], posf[:]).then_inc(v_pos, 1)

            def experts():
                tiles = grid[:, GRID_J:GRID_J + 2 * TILES].unsqueeze(2).to_broadcast([P, 2 * TILES, EXPERTS])
                step(dve.tensor_tensor(cmpj[:], by_expert(incl[:], 2 * TILES), tiles, ALU.is_le))
                step(dve.tensor_reduce(tef[:, 0], cmpj[:], AX.X, ALU.add))
                step(dve.tensor_scalar(tef[:, 1], tef[:, 0], float(EXPERTS - 1), None, ALU.min))
                step(dve.tensor_copy(te[:], tef[:, 1]))

            def hidden(c, f):
                dve.wait_ge(a_silu, c * FK + (f + 1))
                dve.tensor_tensor(hT[:, f], silu[:, f % 2], bu[f % 2][:], ALU.mult).then_inc(v_h, 1)

            def residual(c):
                for i in range(QT):
                    dve.wait_ge(p_dn, c * QT + (i + 1))
                    t = c * QT + i
                    b = base[:, t] if isinstance(t, int) else base[:, bass.ds(t, 1), :].squeeze(1)
                    xx = x2[:, t] if isinstance(t, int) else x2[:, bass.ds(t, 1), :].squeeze(1)
                    dve.tensor_tensor(b, bt[i % 2][:, 0:D], xx, ALU.add).then_inc(v_base, 1)

            hidden_steps = {0: choose, 2: count, 4: place, 6: experts}
            for f in range(FK):
                if f in hidden_steps:
                    hidden_steps[f]()
                hidden(0, f)
            residual(0)
            with dve.Fori(1, CHUNKS) as c:
                for f in range(FK):
                    hidden(c, f)
                residual(c)

        @block.tensor
        def _(pe):
            pe.wait_ge(d_r, 64)
            pe.wait_ge(d_x2i, 16)

            def logits(t):
                pe.wait_ge(a_tr, t + 1)
                for k in range(DK):
                    mm = pe.matmul(br[:, t * EXPERTS:(t + 1) * EXPERTS], x2T[:, k, t * P:(t + 1) * P], wr[:, k, :],
                                   start=(k == 0), stop=(k == DK - 1))
                if t == TILES - 1:
                    mm.then_inc(p_lg, 1)

            for t in range(TILES):
                if t >= 2:
                    pe.wait_ge(a_tr, t - 1)
                for k in range(DK):
                    mm = pe.transpose(bt[t % 2][:, k * P:(k + 1) * P], x2[:, t, k * P:(k + 1) * P], ident[:])
                mm.then_inc(p_tr, 1)
                if t >= 2:
                    logits(t - 2)
            logits(TILES - 2)
            logits(TILES - 1)

            def gate_up(c, f):
                cols = slice(c * 512, (c + 1) * 512) if isinstance(c, int) else bass.ds(c * 512, 512)
                if f >= 2 or not isinstance(c, int):
                    pe.wait_ge(v_h, c * FK + max(f - 1, 0))
                for w, bank in ((wg, bg), (wu, bu)):
                    for k in range(DK):
                        mm = pe.matmul(bank[f % 2][:], w[:, k, f * P:(f + 1) * P], x2T[:, k, cols],
                                       start=(k == 0), stop=(k == DK - 1))
                mm.then_inc(p_gu, 1)

            def down(c):
                pe.wait_ge(v_h, (c + 1) * FK)
                for i in range(QT):
                    if i >= 2 or not isinstance(c, int):
                        pe.wait_ge(v_base, c * QT + max(i - 1, 0))
                    for f in range(FK):
                        mm = pe.matmul(bt[i % 2][:, 0:D], hT[:, f, i * P:(i + 1) * P], wd[:, f, :],
                                       start=(f == 0), stop=(f == FK - 1))
                    mm.then_inc(p_dn, 1)

            pe.wait_ge(d_wg, 16)
            pe.wait_ge(d_wu, 16)
            pe.wait_ge(g_zero, 2)
            for f in range(FK):
                gate_up(0, f)
                if f == 1:
                    pe.wait_ge(v_oh, 1)
                    pe.matmul(bp[:, 0:256], upper[:], oneh[:].rearrange("p t n -> p (t n)"), start=True, stop=True)
                    pe.matmul(bp[:, 256:512], allone[:], oneh[:].rearrange("p t n -> p (t n)"), start=True, stop=True
                              ).then_inc(p_px, 1)
            pe.wait_ge(d_wd, 16)
            down(0)
            with pe.Fori(1, CHUNKS) as c:
                for f in range(FK):
                    gate_up(c, f)
                down(c)


UNROLL = 3


def experts(nc, io, mem):
    base, pos, te, ident = mem["base"], mem["pos"], mem["te"], mem["ident2"]
    with ExitStack() as ctx:
        def sb(name, shape, dt=F32):
            return ctx.enter_context(nc.sbuf_tensor(name, shape, dt))

        def sem(name):
            return ctx.enter_context(nc.semaphore(name))

        xs = sb("xs", [P, UNROLL, D])
        xsT = sb("xsT", [P, UNROLL, D])
        wgu = sb("wgu", [P, UNROLL, DK, 2 * FE])
        wdn = sb("wdn", [P, UNROLL, DK, D])
        sil = sb("sil", [P, UNROLL, FE])
        h = sb("h", [P, UNROLL, FE])
        hTt = sb("hTt", [P, UNROLL, FE])
        ysb = sb("ysb", [P, UNROLL, D])
        yg = sb("yg", [P, TILES, D])
        st7 = sb("st7", [P, TILES, 6])
        mv4 = sb("mv4", [P, TILES, 2])
        ve4 = sb("ve4", [P, TILES])
        rstd4 = sb("rstd4", [P, TILES])
        mhalf4 = sb("mhalf4", [P, 4])
        eps4 = sb("eps4", [P, 4])
        bx = ctx.enter_context(nc.psum_tensor("bx", [P, 512], F32))
        bgu = [ctx.enter_context(nc.psum_tensor(f"bgu{i}", [P, 512], F32)) for i in range(UNROLL)]
        bh = ctx.enter_context(nc.psum_tensor("bh", [P, 512], F32))
        by = [ctx.enter_context(nc.psum_tensor(f"by{i}", [P, 512], F32)) for i in range(UNROLL)]

        d_xs = [sem(f"d_xs{i}") for i in range(UNROLL)]
        d_wgu = [sem(f"d_wgu{i}") for i in range(UNROLL)]
        d_wdn = [sem(f"d_wdn{i}") for i in range(UNROLL)]
        d_y = [sem(f"d_y{i}") for i in range(UNROLL)]
        d_yg = [sem(f"d_yg{i}") for i in range(4)]
        d_out = sem("d_out")
        g_c4 = sem("g_c4")
        s_turn = sem("s_turn")
        p_x, a_x, p_e, a_s, v_hh, p_h, v_hT, p_y, v_y = (sem("p_x"), sem("a_x"), sem("p_e"), sem("a_s"), sem("v_hh"),
                                                         sem("p_h"), sem("v_hT"), sem("p_y"), sem("v_y"))
        v_f, v_mv4, g_l4, g_r4, v_out = sem("v_f"), sem("v_mv4"), sem("g_l4"), sem("g_r4"), sem("v_out")
        v_st4 = sem("v_st4")

        block = ctx.enter_context(nc.Block())

        @block.sync
        def _(sp):
            gu_rows = io["gate_up"].rearrange("e (k p) n -> p (e k) n", p=P)
            dn_rows = io["down"].rearrange("e (k p) n -> p (e k) n", p=P)
            xs_rows = io["sorted_x"].rearrange("(t p) n -> p t n", p=P)

            def load(j, r):
                e = sp.value_load(te[0:1, bass.ds(j, 1)], min_val=0, max_val=EXPERTS - 1)
                sp.dma_start(xs[:, r], xs_rows[:, bass.ds(j, 1), :].squeeze(1)).then_inc(d_xs[r], 16)
                sp.dma_start(wgu[:, r], gu_rows[:, bass.ds(e * DK, DK), :]).then_inc(d_wgu[r], 16)
                sp.dma_start(wdn[:, r], dn_rows[:, bass.ds(e * DK, DK), :]).then_inc(d_wdn[r], 16)

            for r in range(UNROLL):
                load(r, r)
            with sp.Fori(0, (ETILES - 1) // UNROLL - 1) as i:
                for r in range(UNROLL):
                    sp.wait_ge(p_y, i * UNROLL + (r + 1))
                    sp.sem_inc(s_turn, 1)
                    load(i * UNROLL + (r + UNROLL), r)
            sp.wait_ge(p_y, ETILES - UNROLL)
            load(ETILES - 1, 0)
            out_rows = io["out"].rearrange("(t p) n -> p t n", p=P)
            for g in range(TILES // 4):
                sp.wait_ge(v_out, 4 * (g + 1))
                sp.dma_start(out_rows[:, 4 * g:4 * g + 4, :], base[:, 4 * g:4 * g + 4, :]).then_inc(d_out, 16)
            sp.wait_ge(d_out, 16 * TILES // 4)

        @block.gpsimd
        def _(pool):
            pool.memset(mhalf4[:], -0.5).then_inc(g_c4, 1)
            pool.wait_ge(g_c4, 1)
            pool.memset(eps4[:], EPS).then_inc(g_c4, 1)
            pool.wait_ge(g_c4, 2)
            y_rows = io["sorted_y"].rearrange("(t p) n -> p t n", p=P)

            def store(j, r):
                pool.wait_ge(v_y, j + 1)
                pool.sem_inc(g_c4, 1)
                pool.dma_start(y_rows[:, bass.ds(j, 1), :].squeeze(1), ysb[:, r]).then_inc(d_y[r], 16)

            with pool.Fori(0, (ETILES - 1) // UNROLL) as i:
                for r in range(UNROLL):
                    store(i * UNROLL + r, r)
            store(ETILES - 1, 0)
            for r in range(UNROLL):
                pool.wait_ge(d_y[r], 16 * ((ETILES - 1 - r) // UNROLL + 1))
            for t in range(TILES):
                pool.indirect_dma_start(yg[:, t, :], None, io["sorted_y"][:, :],
                                        bass.IndirectOffsetOnAxis(pos[:, t:t + 1], 0)).then_inc(d_yg[t // 4], 16)
            for g in range(4):
                pool.wait_ge(v_mv4, 4 * (g + 1))
                pool.tensor_tensor(ve4[:, 4 * g:4 * g + 4], mv4[:, 4 * g:4 * g + 4, 1], eps4[:], ALU.add).then_inc(g_l4, 1)
                pool.wait_ge(g_l4, g + 1)
                pool.tensor_tensor(rstd4[:, 4 * g:4 * g + 4], ve4[:, 4 * g:4 * g + 4], mhalf4[:], ALU.pow).then_inc(g_r4, 1)

        @block.scalar
        def _(act):
            def copy_x(j, r):
                act.wait_ge(p_x, j + 1)
                act.activation(xsT[:, r], bx[:, 0:D], ACT.Copy).then_inc(a_x, 1)

            def gate(j, r):
                act.wait_ge(p_e, j + 1)
                act.activation(sil[:, r], bgu[r][:, 0:FE], ACT.Silu).then_inc(a_s, 1)

            copy_x(0, 0)
            copy_x(1, 1)
            gate(0, 0)
            with act.Fori(0, (ETILES - 1) // UNROLL - 1) as i:
                for n in range(UNROLL):
                    copy_x(i * UNROLL + (n + 2), (2 + n) % UNROLL)
                    gate(i * UNROLL + (n + 1), (1 + n) % UNROLL)
            for j in range(ETILES - UNROLL, ETILES):
                if j + 1 < ETILES:
                    copy_x(j + 1, (j + 1) % UNROLL)
                gate(j, j % UNROLL)

        @block.vector
        def _(dve):
            def product(j, r):
                dve.wait_ge(a_s, j + 1)
                dve.tensor_tensor(h[:, r], sil[:, r], bgu[r][:, FE:2 * FE], ALU.mult).then_inc(v_hh, 1)

            def copy_h(j, r):
                dve.wait_ge(p_h, j + 1)
                dve.tensor_copy(hTt[:, r], bh[:, 0:FE]).then_inc(v_hT, 1)

            def copy_y(j, r, stored):
                dve.wait_ge(p_y, j + 1)
                if stored is not None:
                    dve.wait_ge(d_y[r], stored)
                dve.tensor_copy(ysb[:, r], by[r][:, 0:D]).then_inc(v_y, 1)

            product(0, 0)
            for j in range(1, 1 + UNROLL):
                copy_h(j - 1, (j - 1) % UNROLL)
                product(j, j % UNROLL)
                copy_y(j - 1, (j - 1) % UNROLL, None)
            with dve.Fori(1, (ETILES - 1) // UNROLL) as i:
                for n in range(UNROLL):
                    j = i * UNROLL + (1 + n)
                    copy_h(j - 1, n)
                    product(j, (1 + n) % UNROLL)
                    copy_y(j - 1, n, i * 16)
            copy_h(ETILES - 1, 0)
            copy_y(ETILES - 1, 0, 16 * ((ETILES - 1) // UNROLL))
            for t in range(TILES + 4):
                if t < TILES:
                    if t % 4 == 0:
                        dve.wait_ge(d_yg[t // 4], 64)
                    dve.tensor_tensor(base[:, t], base[:, t], yg[:, t], ALU.add).then_inc(v_f, 1)
                    dve.wait_ge(v_f, t + 1)
                    dve.bn_stats(st7[:, t], base[:, t]).then_inc(v_st4, 1)
                    dve.wait_ge(v_st4, t + 1)
                    dve.bn_aggr(mv4[:, t], st7[:, t]).then_inc(v_mv4, 1)
                if t >= 4:
                    q = t - 4
                    dve.wait_ge(g_r4, q // 4 + 1)
                    dve.tensor_scalar(base[:, q], base[:, q], mv4[:, q, 0:1], rstd4[:, q:q + 1], ALU.subtract, ALU.mult
                                      ).then_inc(v_out, 1)

        @block.tensor
        def _(pe):
            def transpose_x(j, r, landed):
                pe.wait_ge(d_xs[r], landed)
                if not (isinstance(j, int) and j == 0):
                    pe.wait_ge(a_x, j)
                for k in range(DK):
                    mm = pe.transpose(bx[:, k * P:(k + 1) * P], xs[:, r, k * P:(k + 1) * P], ident[:])
                mm.then_inc(p_x, 1)

            def gate_up(j, r, landed):
                pe.wait_ge(d_wgu[r], landed)
                pe.wait_ge(a_x, j + 1)
                for k in range(DK):
                    mm = pe.matmul(bgu[r][:], xsT[:, r, k * P:(k + 1) * P], wgu[:, r, k, :], start=(k == 0), stop=(k == DK - 1))
                mm.then_inc(p_e, 1)

            def transpose_h(j, r):
                pe.wait_ge(v_hh, j + 1)
                if not (isinstance(j, int) and j == 0):
                    pe.wait_ge(v_hT, j)
                for k in range(DK):
                    mm = pe.transpose(bh[:, k * P:(k + 1) * P], h[:, r, k * P:(k + 1) * P], ident[:])
                mm.then_inc(p_h, 1)

            def down(j, r, landed):
                pe.wait_ge(d_wdn[r], landed)
                pe.wait_ge(v_hT, j + 1)
                if not (isinstance(j, int) and j < UNROLL):
                    pe.wait_ge(v_y, j - (UNROLL - 1))
                for k in range(DK):
                    mm = pe.matmul(by[r][:, 0:D], hTt[:, r, k * P:(k + 1) * P], wdn[:, r, k, :], start=(k == 0), stop=(k == DK - 1))
                mm.then_inc(p_y, 1)

            def slot(j, n, i):
                r0, r1, r2 = n, (n + 1) % UNROLL, (n + 2) % UNROLL
                t0, t1, t2 = i + 1, i + 1 + (n + 1) // UNROLL, i + 1 + (n + 2) // UNROLL
                if not (isinstance(j, int) and j == ETILES - 1):
                    transpose_x(j + 1, r2, t2 * 16)
                transpose_h(j - 1, r0)
                gate_up(j, r1, t1 * 16)
                down(j - 1, r0, t0 * 16)

            transpose_x(0, 0, 16)
            transpose_x(1, 1, 16)
            gate_up(0, 0, 16)
            for n in range(UNROLL):
                slot(1 + n, n, 0)
            with pe.Fori(1, (ETILES - 1) // UNROLL - 1) as i:
                for n in range(UNROLL):
                    slot(i * UNROLL + (1 + n), n, i)
            last = (ETILES - 1) // UNROLL - 1
            for n in range(UNROLL):
                slot(last * UNROLL + 1 + n, n, last)
            transpose_h(ETILES - 1, 0)
            down(ETILES - 1, 0, 16 * ((ETILES - 1) // UNROLL + 1))


def program(nc, io, stages=3):
    with ExitStack() as ctx:
        mem = {}
        for name, shape, dt in (("K1", [P, HEADS, KEYS_PAD], F32R), ("K2", [P, HEADS, KEYS_PAD], F32R),
                                ("V", [P, KT, HID], F32), ("ident", [P, P], F32)):
            mem[name] = ctx.enter_context(nc.sbuf_tensor(name, shape, dt))
        before_attention(nc, io, mem)
        if stages > 1:
            attention(nc, io, mem)
    if stages > 2:
        with ExitStack() as ctx:
            mem = {"base": ctx.enter_context(nc.sbuf_tensor("base", [P, TILES, D], F32)),
                   "ident2": ctx.enter_context(nc.sbuf_tensor("ident2", [P, P], F32)),
                   "pos": ctx.enter_context(nc.sbuf_tensor("pos", [P, TILES], mybir.dt.uint32)),
                   "te": ctx.enter_context(nc.sbuf_tensor("te", [P, 2 * TILES], I32))}
            route_and_share(nc, io, mem)
            experts(nc, io, mem)


_SCRATCH = {"x1b": (S, D), "x1T": (D, S), "x2": (S, D), "sorted_x": (2 * S, D), "sorted_y": (ETILES * P, D)}


def kernel(x, ctx_1024, L0_attn_W_in, L0_attn_b_in, L0_attn_log_A, L0_attn_B_p, L0_attn_C_p, L0_attn_W_out,
           L0_attn_b_out, L0_attn_gamma, L0_attn_beta, L0_xattn_Wq, L0_xattn_Wk, L0_xattn_Wv, L0_xattn_Wo,
           L0_xattn_bo, L0_ffn_router_w, L0_ffn_gate_up_proj, L0_ffn_down_proj, L0_ffn_shared_gate_w,
           L0_ffn_shared_up_w, L0_ffn_shared_down_w):
    import numpy as np
    import concourse.bacc as bacc
    from concourse.bass_utils import run_bass_kernel_spmd

    ctx_rows = ctx_1024[0]
    host = {
        "x": x[0], "xT": x[0].T, "ctxT": np.concatenate([ctx_rows, ctx_rows[-1:]]).T,
        "w_inT": L0_attn_W_in.T, "w_outT": L0_attn_W_out.T,
        "cols": np.stack([np.reshape(a, (DK, P)) for a in (L0_attn_b_in, L0_attn_log_A, L0_attn_B_p, L0_attn_C_p)]
                         ).transpose(2, 0, 1),
        "b_out": L0_attn_b_out, "gamma": L0_attn_gamma, "beta": L0_attn_beta, "bo": L0_xattn_bo,
        "wq": L0_xattn_Wq, "wk": L0_xattn_Wk, "wv": L0_xattn_Wv, "wo": L0_xattn_Wo,
        "routerT": L0_ffn_router_w.T, "gate_up": L0_ffn_gate_up_proj, "down": L0_ffn_down_proj,
        "s_gateT": L0_ffn_shared_gate_w.T, "s_upT": L0_ffn_shared_up_w.T, "s_downT": L0_ffn_shared_down_w.T,
        "ident": np.eye(P, dtype=np.float32), "upper": np.triu(np.ones((P, P), np.float32), 1),
        "grid": np.tile(np.concatenate([EXPERTS - np.arange(EXPERTS), P * np.arange(TILES), np.arange(2 * TILES)]
                                       ).astype(np.float32), (P, 1)),
    }
    nc = bacc.Bacc("TRN2", target_bir_lowering=False, num_devices=1)
    io, arrays = {}, {}
    for name, a in host.items():
        a = np.ascontiguousarray(a)
        arrays["in_" + name] = a
        io[name] = nc.dram_tensor("in_" + name, a.shape, mybir.dt.from_np(a.dtype), kind="ExternalInput").ap()
    for name, shape in _SCRATCH.items():
        io[name] = nc.dram_tensor("scratch_" + name, shape, F32, kind="Internal").ap()
    io["out"] = nc.dram_tensor("out_0", (S, D), F32, kind="ExternalOutput").ap()
    program(nc, io)
    r = run_bass_kernel_spmd(nc, [arrays], core_ids=[0])
    return r.results[0]["out_0"].reshape(1, S, D)
```

```python
from contextlib import ExitStack

import concourse.bass as bass
from concourse import mybir

F32 = mybir.dt.float32
F32R = mybir.dt.float32r
I32 = mybir.dt.int32
ALU = mybir.AluOpType
ACT = mybir.ActivationFunctionType
AX = mybir.AxisListType

P = 128
S, D = 2048, 256
TILES = S // P
DK = D // P
KEYS = 1601
KEYS_PAD = 1602
KT = (KEYS + P - 1) // P
LAST = KEYS - (KT - 1) * P
HEADS, DH = 8, 64
HID = HEADS * DH
PAIRS = HEADS // 2
QC = 512
CHUNKS = S // QC
QT = QC // P
EPS = 1e-5
KC = [(0, 402), (402, 400), (802, 400), (1202, 400)]


def before_attention(nc, io, mem):
    K1, K2, V, ident = mem["K1"], mem["K2"], mem["V"], mem["ident"]
    with ExitStack() as ctx:
        def sb(name, shape, dt=F32):
            return ctx.enter_context(nc.sbuf_tensor(name, shape, dt))

        def sem(name):
            return ctx.enter_context(nc.semaphore(name))

        xT = sb("xT", [P, DK, S])
        z = xT[:, :, :].rearrange("p k (a n) -> p (k a) n", n=D)
        state = sb("state", [P, DK, S])
        xring = sb("xring", [P, 2, 4, D])
        w_in = sb("w_in", [P, DK, D])
        w_out = sb("w_out", [P, DK, D])
        ctxT = sb("ctxT", [P, DK, KEYS_PAD])
        wk = sb("wk", [P, DK, HID])
        wv = sb("wv", [P, DK, HID])
        cols = sb("cols", [P, 4, DK])
        rows = sb("rows", [P, 4, D])
        decay = sb("decay", [P, 3, DK])
        bB = sb("bB", [P, DK])
        stats = sb("stats", [P, 4, 2, 6])
        mv = sb("mv", [P, 2, TILES, 2])
        ve = sb("ve", [P, 2, TILES])
        rstd = sb("rstd", [P, 2, TILES])
        mhalf = sb("mhalf", [P, 4])
        x1Tb = sb("x1Tb", [P, 2, DK, P])
        banks = [ctx.enter_context(nc.psum_tensor(f"bank_a{i}", [P, 512], F32)) for i in range(8)]

        d_x = [sem(f"d_xT{c}") for c in range(4)]
        d_small, d_ctx, d_wk, d_wv = sem("d_small"), sem("d_ctx"), sem("d_wk"), sem("d_wv")
        d_xring = [sem(f"d_xring{i}") for i in range(2)]
        d_dup = sem("d_dup")
        d_x1 = sem("d_x1")
        d_x1T = [sem(f"d_x1T{i}") for i in range(2)]
        prep = sem("prep")
        a_exp = sem("a_exp")
        p_in, a_u, v_scan = sem("p_in"), sem("a_u"), sem("v_scan")
        p_out, v_z = sem("p_out"), sem("v_z")
        v_link = sem("v_link")
        v_mv1, v_mv2 = sem("v_mv1"), sem("v_mv2")
        g_const, g_link, g_xb, g_rstd1, g_rstd2 = sem("g_const"), sem("g_link"), sem("g_xb"), sem("g_rstd1"), sem("g_rstd2")
        v_b, v_x1 = sem("v_b"), sem("v_x1")
        p_k, a_khi, v_klo = sem("p_k"), sem("a_khi"), sem("v_klo")
        p_v, a_v = sem("p_v"), sem("a_v")
        p_t, a_t = sem("p_t"), sem("a_t")
        g_x1b = sem("g_x1b")

        G = TILES // 4
        kunits = [(p, j) for p in range(PAIRS) for j in range(len(KC))]
        kv = []
        for n in range(16):
            kv.append(("k", n))
            if n < KT:
                kv.append(("v", n))

        def order(key, val, tr, out=None):
            n = 0
            for t in range(TILES):
                if out:
                    out(t)
                for kind, u in kv[n:n + 2]:
                    (key if kind == "k" else val)(u)
                n += 2
                if tr and t == TILES - 2:
                    for q in range(4):
                        tr(q)
            if tr:
                for q in range(4, TILES):
                    tr(q)

        block = ctx.enter_context(nc.Block())

        @block.sync
        def _(sp):
            sp.dma_start(w_in[:], io["w_inT"].rearrange("(k p) n -> p k n", p=P)).then_inc(d_small, 16)
            sp.dma_start(cols[:], io["cols"]).then_inc(d_small, 16)
            for c in range(4):
                sp.dma_start(xT[:, :, c * 512:(c + 1) * 512],
                             io["xT"].rearrange("(k p) n -> p k n", p=P)[:, :, c * 512:(c + 1) * 512]).then_inc(d_x[c], 16)
            sp.dma_start(w_out[:], io["w_outT"].rearrange("(k p) n -> p k n", p=P)).then_inc(d_small, 16)
            sp.dma_start(wk[:], io["wk"].rearrange("(k p) n -> p k n", p=P)).then_inc(d_wk, 16)
            sp.dma_start(ctxT[:], io["ctxT"].rearrange("(k p) n -> p k n", p=P)).then_inc(d_ctx, 16)
            sp.dma_start(wv[:], io["wv"].rearrange("(k p) n -> p k n", p=P)).then_inc(d_wv, 16)
            for i, n in enumerate(("b_out", "gamma", "beta", "bo")):
                sp.dma_start(rows[:, i, :], io[n].partition_broadcast(P)).then_inc(d_small, 16)
            sp.dma_start(ident[:], io["ident"]).then_inc(d_small, 16)
            for g in range(G):
                if g >= 2:
                    sp.wait_ge(v_b, 4 * (g - 1))
                sp.dma_start(xring[:, g % 2], io["x"].rearrange("(t p) n -> p t n", p=P)[:, 4 * g:4 * g + 4, :]
                             ).then_inc(d_xring[g % 2], 16)
            for h in range(HEADS):
                sp.wait_ge(a_khi, 2 * len(KC) * (h // 2 + 1))
                sp.dma_start(K1[DH:P, h, :].bitcast(F32), K1[0:DH, h, :].bitcast(F32)).then_inc(d_dup, 16)
            for g in range(G):
                sp.wait_ge(g_x1b, g + 1)
                sp.dma_start(io["x1b"].rearrange("(t p) n -> p t n", p=P)[:, 4 * g:4 * g + 4, :],
                             z[:, 4 * g:4 * g + 4, :]).then_inc(d_x1, 16)
            sp.wait_ge(d_x1, 16 * G)
            sp.wait_ge(d_dup, 16 * HEADS)

        @block.gpsimd
        def _(pool):
            pool.memset(mhalf[:], -0.5).then_inc(g_const, 1)
            pool.wait_ge(g_const, 1)
            pool.memset(K2[DH:DH + 1, :, :].bitcast(F32), 1.0).then_inc(g_const, 1)
            pool.wait_ge(g_const, 2)
            pool.wait_ge(d_small, 16 * 8)
            links = [0]

            def link(ins):
                links[0] += 1
                ins.then_inc(g_link, 1)
                pool.wait_ge(g_link, links[0])

            def xb(g):
                pool.wait_ge(d_xring[g % 2], 16 * (g // 2 + 1))
                for t in range(4):
                    ins = pool.tensor_tensor(xring[:, g % 2, t], xring[:, g % 2, t], rows[:, 2, :], ALU.add)
                    ins.then_inc(g_xb, 1)

            def inverse(n, g, ready, done):
                pool.wait_ge(ready, 4 * (g + 1))
                link(pool.tensor_scalar(ve[:, n, 4 * g:4 * g + 4], mv[:, n, 4 * g:4 * g + 4, 1], EPS, None, ALU.add))
                pool.tensor_tensor(rstd[:, n, 4 * g:4 * g + 4], ve[:, n, 4 * g:4 * g + 4], mhalf[:], ALU.pow
                                   ).then_inc(done, 1)

            def x1b(g):
                pool.wait_ge(p_t, 4 * (g + 1))
                pool.wait_ge(v_x1, 4 * (g + 1))
                for t in range(4 * g, 4 * g + 4):
                    ins = pool.tensor_tensor(z[:, t, :], z[:, t, :], rows[:, 3, :], ALU.add)
                ins.then_inc(g_x1b, 1)

            xb(0)
            xb(1)
            for g in range(G + 2):
                if g < G:
                    inverse(0, g, v_mv1, g_rstd1)
                if 1 <= g <= G:
                    inverse(1, g - 1, v_mv2, g_rstd2)
                if g + 2 < G:
                    xb(g + 2)
                if g >= 2:
                    x1b(g - 2)

        @block.scalar
        def _(act):
            act.wait_ge(d_small, 16 * 8)
            act.activation(decay[:, 0], cols[:, 1], ACT.Exp).then_inc(a_exp, 1)
            act.wait_ge(prep, 3)
            for n in range(8):
                c, e = n // 2, n % 2
                act.wait_ge(p_in, n + 1)
                act.activation(state[:, e, c * 512:(c + 1) * 512], banks[n % 2][:], ACT.Identity,
                               bias=bB[:, e:e + 1], scale=cols[:, 2, e:e + 1]).then_inc(a_u, 1)

            def key_high(n):
                p, j = kunits[n]
                k0, kn = KC[j]
                act.wait_ge(p_k, n + 1)
                for h in range(2):
                    act.activation(K1[0:DH, 2 * p + h, k0:k0 + kn], banks[4 + n % 2][DH * h:DH * h + DH, 0:kn],
                                   ACT.Copy).then_inc(a_khi, 1)

            def value(n):
                rows_n = P if n < KT - 1 else LAST
                act.wait_ge(p_v, n + 1)
                act.activation(V[0:rows_n, n, :], banks[6 + n % 2][0:rows_n, :], ACT.Copy).then_inc(a_v, 1)

            def transposed(t):
                act.wait_ge(p_t, t + 1)
                if t >= 2:
                    act.wait_ge(d_x1T[t % 2], 16 * (t // 2))
                act.activation(x1Tb[:, t % 2], banks[t % 2][:, 0:D].rearrange("p (k n) -> p k n", k=DK),
                               ACT.Copy).then_inc(a_t, 1)
                act.wait_ge(a_t, t + 1)
                act.dma_start(io["x1T"].rearrange("(k p) n -> p k n", p=P)[:, :, t * P:(t + 1) * P],
                              x1Tb[:, t % 2]).then_inc(d_x1T[t % 2], 16)

            order(key_high, value, transposed)
            act.wait_ge(d_x1T[0], 16 * TILES // 2)
            act.wait_ge(d_x1T[1], 16 * TILES // 2)

        @block.vector
        def _(dve):
            links = [0]

            def link(ins):
                links[0] += 1
                ins.then_inc(v_link, 1)
                dve.wait_ge(v_link, links[0])

            dve.wait_ge(d_small, 16 * 8)
            dve.wait_ge(a_exp, 1)
            dve.tensor_tensor(bB[:], cols[:, 0], cols[:, 2], ALU.mult).then_inc(prep, 1)
            dve.tensor_scalar(decay[:, 1], decay[:, 0], 1.0, None, ALU.add).then_inc(prep, 1)
            dve.wait_ge(prep, 2)
            dve.reciprocal(decay[:, 2], decay[:, 1]).then_inc(prep, 1)
            for k in range(DK):
                dve.tensor_scalar(w_out[:, k], w_out[:, k], cols[:, 3, k:k + 1], None, ALU.mult).then_inc(prep, 1)
            dve.wait_ge(prep, 3)
            for n in range(8):
                c, e = n // 2, n % 2
                dve.wait_ge(a_u, n + 1)
                if c:
                    dve.wait_ge(v_scan, n - 1)
                u = state[:, e, c * 512:(c + 1) * 512]
                dve.tensor_tensor_scan(u, decay[:, 2, e:e + 1].to_broadcast([P, 512]), u,
                                       state[:, e, c * 512 - 1:c * 512] if c else 0.0,
                                       ALU.mult, ALU.add).then_inc(v_scan, 1)

            def key_low(n):
                p, j = kunits[n]
                k0, kn = KC[j]
                dve.wait_ge(a_khi, 2 * (n + 1))
                for h in range(2):
                    dve.tensor_tensor(K2[0:DH, 2 * p + h, k0:k0 + kn], banks[4 + n % 2][DH * h:DH * h + DH, 0:kn],
                                      K1[0:DH, 2 * p + h, k0:k0 + kn].bitcast(F32), ALU.subtract).then_inc(v_klo, 1)

            def norm_a(t):
                dve.wait_ge(p_out, t + 1)
                dve.tensor_tensor(z[:, t], banks[2 + t % 2][:, 0:D], rows[:, 0, :], ALU.add).then_inc(v_z, 1)
                dve.wait_ge(v_z, t + 1)
                link(dve.bn_stats(stats[:, t % 4, 0, :], z[:, t]))
                dve.bn_aggr(mv[:, 0, t], stats[:, t % 4, 0, :]).then_inc(v_mv1, 1)

            def norm_b(t):
                if t % 4 == 0:
                    dve.wait_ge(g_rstd1, t // 4 + 1)
                dve.wait_ge(g_xb, t + 1)
                link(dve.scalar_tensor_tensor(z[:, t], z[:, t], mv[:, 0, t, 0:1], rows[:, 1, :], ALU.subtract, ALU.mult))
                dve.scalar_tensor_tensor(z[:, t], z[:, t], rstd[:, 0, t:t + 1], xring[:, (t // 4) % 2, t % 4],
                                         ALU.mult, ALU.add).then_inc(v_b, 1)
                dve.wait_ge(v_b, t + 1)
                link(dve.bn_stats(stats[:, t % 4, 1, :], z[:, t]))
                dve.bn_aggr(mv[:, 1, t], stats[:, t % 4, 1, :]).then_inc(v_mv2, 1)

            def norm_c(t):
                if t % 4 == 0:
                    dve.wait_ge(g_rstd2, t // 4 + 1)
                dve.tensor_scalar(z[:, t], z[:, t], mv[:, 1, t, 0:1], rstd[:, 1, t:t + 1],
                                  ALU.subtract, ALU.mult).then_inc(v_x1, 1)

            def token_tile(t):
                norm_a(t)
                if t >= 5:
                    norm_b(t - 5)
                if t >= 10:
                    norm_c(t - 10)

            order(key_low, lambda n: None, None, token_tile)
            for t in range(TILES, TILES + 10):
                if t - 5 < TILES:
                    norm_b(t - 5)
                if t - 10 < TILES:
                    norm_c(t - 10)

        @block.tensor
        def _(pe):
            for n in range(8):
                c, e = n // 2, n % 2
                if n == 0:
                    pe.wait_ge(d_small, 16 * 8)
                pe.wait_ge(d_x[c], 16)
                if n >= 2:
                    pe.wait_ge(a_u, n - 1)
                for k in range(DK):
                    mm = pe.matmul(banks[n % 2][:], w_in[:, k, e * P:(e + 1) * P], xT[:, k, c * 512:(c + 1) * 512],
                                   start=(k == 0), stop=(k == DK - 1))
                mm.then_inc(p_in, 1)
            pe.wait_ge(d_wk, 16)
            pe.wait_ge(d_wv, 16)
            pe.wait_ge(d_ctx, 16)
            pe.wait_ge(prep, 5)
            pe.wait_ge(a_u, 8)

            def out_proj(t):
                pe.wait_ge(v_scan, 2 * (t // 4 + 1))
                if t >= 2:
                    pe.wait_ge(v_z, t - 1)
                for k in range(DK):
                    mm = pe.matmul(banks[2 + t % 2][:, 0:D], state[:, k, t * P:(t + 1) * P], w_out[:, k, :],
                                   start=(k == 0), stop=(k == DK - 1))
                mm.then_inc(p_out, 1)

            def key(n):
                p, j = kunits[n]
                k0, kn = KC[j]
                if n >= 2:
                    pe.wait_ge(v_klo, 2 * (n - 1))
                for k in range(DK):
                    mm = pe.matmul(banks[4 + n % 2][:, 0:kn], wk[:, k, p * P:(p + 1) * P], ctxT[:, k, k0:k0 + kn],
                                   start=(k == 0), stop=(k == DK - 1))
                mm.then_inc(p_k, 1)

            def val(n):
                rows_n = P if n < KT - 1 else LAST
                if n >= 2:
                    pe.wait_ge(a_v, n - 1)
                for k in range(DK):
                    mm = pe.matmul(banks[6 + n % 2][0:rows_n, :], ctxT[:, k, n * P:n * P + rows_n], wv[:, k, :],
                                   start=(k == 0), stop=(k == DK - 1))
                mm.then_inc(p_v, 1)

            def transpose(t):
                pe.wait_ge(v_x1, t + 1)
                if t >= 2:
                    pe.wait_ge(a_t, t - 1)
                for k in range(DK):
                    mm = pe.transpose(banks[t % 2][:, k * P:(k + 1) * P], z[:, t, k * P:(k + 1) * P], ident[:])
                mm.then_inc(p_t, 1)

            order(key, val, transpose, out_proj)


STEP_MX = 1 + 2 * QT * len(KC)
CHUNK_MISC = 2 * PAIRS + 2
G_ADDS = KT - 2
SEED = 1
DIVIDE_AFTER = (4, 7, 10, 13)
OUTPUT_AT = (6, 9)
RESIDUAL_AFTER = [3 * (t - 1) for t in OUTPUT_AT]
RING = 4


def attention(nc, io, mem):
    K1, K2, V, ident = mem["K1"], mem["K2"], mem["V"], mem["ident"]
    with ExitStack() as ctx:
        def sb(name, shape, dt=F32):
            return ctx.enter_context(nc.sbuf_tensor(name, shape, dt))

        def sem(name):
            return ctx.enter_context(nc.semaphore(name))

        wq = sb("wq", [P, DK, HID])
        wo = sb("wo", [P, PAIRS, D])
        x1T = sb("x1T", [P, DK, QC])
        x1 = sb("x1", [P, QT, D])
        Q1 = sb("Q1", [P, 2, 2, QC], F32R)
        Q2 = sb("Q2", [P, 2, 2, QC], F32R)
        probs = sb("probs", [P, RING, 2 * QC])
        accD = sb("accD", [P, 2 * QC])
        accG = sb("accG", [P, 2 * QC])
        ones = sb("ones", [P, DH])
        o_raw = sb("o_raw", [P, QC])
        rsum = sb("rsum", [P, QC])
        oT = sb("oT", [P, PAIRS, QC])
        mxp = sb("mxp", [P, 2, 2 * QT, len(KC)])
        nm = sb("nm", [P, 2, 2 * QT])
        mrow = sb("mrow", [2 * QT, 2, P], F32R)
        st6 = sb("st6", [P, QT, 6])
        mv3 = sb("mv3", [P, QT, 2])
        ve3 = sb("ve3", [P, QT])
        rstd3 = sb("rstd3", [P, QT])
        eps3 = sb("eps3", [P, QT])
        mhalf3 = sb("mhalf3", [P, QT])
        st = [ctx.enter_context(nc.psum_tensor(f"st{i}", [P, 2 * QC], F32)) for i in range(2)]
        av = ctx.enter_context(nc.psum_tensor("av", [P, QC], F32))
        misc = ctx.enter_context(nc.psum_tensor("misc", [P, QC], F32))
        mx = [ctx.enter_context(nc.psum_tensor(f"mx{i}", [P, QC], F32)) for i in range(2)]

        d_w, d_x1Tc, d_x1c, d_x2 = sem("d_w"), sem("d_x1Tc"), sem("d_x1c"), sem("d_x2")
        d_q2 = [sem(f"d_q2_{i}") for i in range(2)]
        d_m = [sem(f"d_m_{i}") for i in range(2)]
        p_q, a_hi, v_lo = sem("p_q"), sem("a_hi"), sem("v_lo")
        p_mx, v_mx, v_nm, p_mT, v_mT = sem("p_mx"), sem("v_mx"), sem("v_nm"), sem("p_mT"), sem("v_mT")
        p_qk = sem("p_qk")
        a_probs = sem("a_probs")
        p_pv = sem("p_pv")
        v_add, g_add = sem("v_add"), sem("g_add")
        a_av, p_sum, v_misc, v_o = sem("a_av"), sem("p_sum"), sem("v_misc"), sem("v_o")
        p_wo, v_r, v_mv3, g_rs3, v_x2 = sem("p_wo"), sem("v_r"), sem("v_mv3"), sem("g_rs3"), sem("v_x2")
        v_rsum = sem("v_rsum")
        v_stats = sem("v_stats")
        s_free = sem("s_free")
        v_link3, g_link3, g_ones = sem("v_link3"), sem("g_link3"), sem("g_ones")

        def rows_of(t):
            return P if t < KT - 1 else LAST

        def max_use(c, p):
            return c * CHUNK_MISC + (2 * p + 2 if p else 0)

        def sum_use(c, p):
            return c * CHUNK_MISC + (2 * p + 5 if p < PAIRS - 1 else CHUNK_MISC + 1)

        def out_use(c, a):
            return (c + 1) * CHUNK_MISC + 2 + a

        LAST_SUM_USE = CHUNKS * CHUNK_MISC

        def parity(p):
            return (p + 1) % 2

        block = ctx.enter_context(nc.Block())

        @block.sync
        def _(sp):
            sp.dma_start(wq[:], io["wq"].rearrange("(k p) n -> p k n", p=P)).then_inc(d_w, 16)
            sp.dma_start(x1T[:], io["x1T"].rearrange("(k p) n -> p k n", p=P)[:, :, 0:QC]).then_inc(d_x1Tc, 16)
            sp.dma_start(wo[:], io["wo"].rearrange("(k p) n -> p k n", p=P)).then_inc(d_w, 16)
            sp.dma_start(x1[:], io["x1b"].rearrange("(t p) n -> p t n", p=P)[:, 0:QT, :]).then_inc(d_x1c, 16)

            def queries(F, par, n):
                sp.wait_ge(a_hi, (F + 1) * 2)
                sp.sem_inc(s_free, 1)
                if n:
                    sp.wait_ge(p_qk, SEED + (F - 1) * KT)
                sp.sem_inc(s_free, 1)
                sp.dma_start(Q2[0:DH, par].bitcast(F32), Q1[0:DH, par].bitcast(F32)).then_inc(d_q2[par], 16)

            def maxima(F, par):
                sp.wait_ge(v_mT, F + 1)
                sp.sem_inc(s_free, 1)
                for h in range(2):
                    sp.dma_start(Q2[DH:DH + 1, par, h, :].bitcast(F32), mrow[QT * h:QT * h + QT, par, :].bitcast(F32)
                                 ).then_inc(d_m[par], 16)

            def store(c):
                sp.wait_ge(v_x2, (c + 1) * QT)
                sp.sem_inc(s_free, 1)
                sp.dma_start(io["x2"].rearrange("(t p) n -> p t n", p=P)[:, bass.ds(c * QT, QT), :], x1[:]).then_inc(d_x2, 16)
                sp.sem_inc(s_free, 1)

            def chunk(c, first, last):
                for p in range(PAIRS):
                    F = c * PAIRS + (p + 1)
                    if p == 1 and not first:
                        store(c - 1)
                    maxima(c * PAIRS + p, p % 2)
                    if not (last and p == PAIRS - 1):
                        queries(F, parity(p), True)
                    if p == PAIRS - 2 and not last:
                        sp.wait_ge(p_q, (c + 1) * PAIRS)
                        sp.sem_inc(s_free, 1)
                        sp.sem_inc(s_free, 1)
                        sp.dma_start(x1T[:], io["x1T"].rearrange("(k p) n -> p k n", p=P)[:, :, bass.ds((c + 1) * QC, QC)]
                                     ).then_inc(d_x1Tc, 16)
                    if p == 1 and not first:
                        sp.wait_ge(d_x2, c * 16)
                        sp.sem_inc(s_free, 1)
                        sp.dma_start(x1[:], io["x1b"].rearrange("(t p) n -> p t n", p=P)[:, bass.ds(c * QT, QT), :]
                                     ).then_inc(d_x1c, 16)

            queries(0, 0, False)
            chunk(0, True, False)
            with sp.Fori(1, CHUNKS - 1) as c:
                chunk(c, False, False)
            chunk(CHUNKS - 1, False, True)
            store(CHUNKS - 1)
            sp.wait_ge(d_x2, CHUNKS * 16)

        @block.gpsimd
        def _(pool):
            pool.sem_inc(g_add, G_ADDS)
            pool.memset(ones[:], 1.0).then_inc(g_ones, 1)
            pool.wait_ge(g_ones, 1)
            pool.memset(mhalf3[:], -0.5).then_inc(g_ones, 1)
            pool.wait_ge(g_ones, 2)
            pool.memset(eps3[:], EPS).then_inc(g_ones, 1)
            pool.wait_ge(g_ones, 3)

            def inverse(c):
                pool.wait_ge(v_mv3, (c + 1) * QT)
                pool.tensor_tensor(ve3[:], mv3[:, :, 1], eps3[:], ALU.add).then_inc(g_link3, 1)
                pool.wait_ge(g_link3, c + 1)
                pool.tensor_tensor(rstd3[:], ve3[:], mhalf3[:], ALU.pow).then_inc(g_rs3, 1)
                pool.wait_ge(g_rs3, c + 1)

            def chunk(c, first):
                for p in range(PAIRS):
                    for n, t in enumerate(range(2, KT)):
                        if p == 0 and t == KT - 1 and not first:
                            inverse(c - 1)
                        r = rows_of(t)
                        pool.wait_ge(a_probs, (c * PAIRS + p) * KT + (2 + t + 1))
                        if n == 0:
                            pool.wait_ge(p_sum, SEED + c * PAIRS + p)
                            pool.wait_ge(v_add, c * PAIRS + (p + 1))
                            so_far = accD
                        else:
                            so_far = accG
                            pool.wait_ge(g_add, (c * PAIRS + p) * G_ADDS + (G_ADDS + n))
                        pool.tensor_tensor(accG[0:r], so_far[0:r], probs[0:r, (p * KT + t) % RING], ALU.add).then_inc(g_add, 1)

            chunk(0, True)
            with pool.Fori(1, CHUNKS) as c:
                chunk(c, False)
            inverse(CHUNKS - 1)

        @block.scalar
        def _(act):
            act.sem_inc(a_probs, 2)
            act.sem_inc(a_av, SEED)

            def q_high(F, par, h, n):
                act.wait_ge(p_q, F + 1)
                if n and h == 0:
                    act.wait_ge(p_qk, SEED + (F - 1) * KT)
                act.activation(Q1[0:DH, par, h], mx[par][DH * h:DH * h + DH, :], ACT.Copy).then_inc(a_hi, 1)

            def exp(c, p, t):
                g = p * KT + t
                s, r = g % RING, rows_of(t)
                act.wait_ge(p_qk, SEED + c * PAIRS * KT + (g + 1))
                act.wait_ge(p_pv, c * PAIRS * KT + (g + 1))
                old = (t - RING) % KT
                if old < 2:
                    act.wait_ge(v_add, c * PAIRS + (p + 1))
                else:
                    since = p + (1 if t >= RING else 0)
                    act.wait_ge(g_add, c * PAIRS * G_ADDS + (since * G_ADDS + (old - 1)))
                act.activation(probs[0:r, s], st[g % 2][0:r, :], ACT.Exp, scale=DH ** -0.5).then_inc(a_probs, 1)

            def copy_av(c, p):
                act.wait_ge(p_pv, (c * PAIRS + (p + 1)) * KT + RING)
                act.wait_ge(v_o, SEED + (c * PAIRS + p) * QT)
                act.activation(o_raw[:], av[:], ACT.Copy).then_inc(a_av, 1)

            def chunk(c, first, last):
                for p in range(PAIRS):
                    ahead = not (last and p == PAIRS - 1)
                    F = c * PAIRS + (p + 1)
                    if ahead:
                        q_high(F, parity(p), 0, True)
                        q_high(F, parity(p), 1, True)
                    if p > 0:
                        copy_av(c, p - 1)
                    elif not first:
                        copy_av(c - 1, PAIRS - 1)
                    for t in range(KT):
                        exp(c, p, t)

            for h in range(2):
                q_high(0, 0, h, False)
            chunk(0, True, False)
            with act.Fori(1, CHUNKS - 1) as c:
                chunk(c, False, False)
            chunk(CHUNKS - 1, False, True)
            copy_av(CHUNKS - 1, PAIRS - 1)

        @block.vector
        def _(dve):
            def q_low(F, par):
                for h in range(2):
                    dve.wait_ge(a_hi, F * 2 + (h + 1))
                    ins = dve.tensor_tensor(Q1[DH:P, par, h], mx[par][DH * h:DH * h + DH, :],
                                            Q1[0:DH, par, h].bitcast(F32), ALU.subtract).then_inc(v_lo, 1)
                dve.wait_ge(v_lo, F * 2 + 2)
                dve.sem_inc(v_mx, 1)

            def piece_maxima(F, par, between):
                for u in range(2 * QT):
                    for j, (k0, kn) in enumerate(KC):
                        n = len(KC) * u + j + 1
                        dve.wait_ge(p_mx, F * (STEP_MX - 1) + n)
                        dve.tensor_reduce(mxp[:, par, u, j:j + 1], mx[(par + n) % 2][:, 0:kn], AX.X, ALU.max
                                          ).then_inc(v_mx, 1)
                        if n in between:
                            between[n]()
                dve.wait_ge(v_mx, F * STEP_MX + STEP_MX)
                dve.tensor_reduce(nm[:, par], mxp[:, par], AX.X, ALU.max, negate=True).then_inc(v_nm, 1)

            def max_row(F, par):
                dve.wait_ge(p_mT, F + 1)
                dve.tensor_copy(mrow[:, par], misc[0:2 * QT, 0:P]).then_inc(v_mT, 1)
                dve.wait_ge(v_mT, F + 1)
                dve.sem_inc(v_misc, 1)

            def divide(c, p, i):
                S0 = c * PAIRS + p
                if i == 0:
                    dve.wait_ge(p_sum, SEED + S0 + 1)
                    dve.wait_ge(v_o, SEED + S0 * QT)
                cols = slice(i * P, (i + 1) * P)
                dve.reciprocal(rsum[:, cols], misc[:, cols]).then_inc(v_rsum, 1)
                dve.wait_ge(v_rsum, S0 * QT + (i + 1))
                if i == QT - 1:
                    dve.sem_inc(v_misc, 1)
                if i == 0:
                    dve.wait_ge(a_av, SEED + S0 + 1)
                    if p == 0:
                        dve.wait_ge(p_wo, SEED + c * QT)
                dve.tensor_tensor(oT[:, p, cols], o_raw[:, cols], rsum[:, cols], ALU.mult).then_inc(v_o, 1)

            def residual(c, i, bank):
                dve.wait_ge(p_wo, SEED + c * QT + (i + 2 - i % 2))
                if i == 0:
                    dve.wait_ge(d_x1c, (c + 1) * 16)
                dve.tensor_tensor(x1[:, i], bank[:, (i % 2) * D:(i % 2 + 1) * D], x1[:, i], ALU.add).then_inc(v_r, 1)
                dve.wait_ge(v_r, c * QT + (i + 1))
                if i % 2:
                    dve.sem_inc(v_misc, 1)
                dve.bn_stats(st6[:, i], x1[:, i]).then_inc(v_link3, 1)
                dve.wait_ge(v_link3, c * QT + (i + 1))
                dve.sem_inc(v_stats, 1)
                dve.bn_aggr(mv3[:, i], st6[:, i]).then_inc(v_mv3, 1)

            def norm(c):
                dve.wait_ge(g_rs3, c + 1)
                for i in range(QT):
                    dve.tensor_scalar(x1[:, i], x1[:, i], mv3[:, i, 0:1], rstd3[:, i:i + 1], ALU.subtract, ALU.mult
                                      ).then_inc(v_x2, 1)

            def first_sum(c, p):
                dve.wait_ge(a_probs, (c * PAIRS + p) * KT + 4)
                dve.wait_ge(g_add, (c * PAIRS + p) * G_ADDS + 1)
                dve.tensor_tensor(accD[:], probs[:, (p * KT) % RING], probs[:, (p * KT + 1) % RING], ALU.add
                                  ).then_inc(v_add, 1)

            def chunk(c, first, last):
                for p in range(PAIRS):
                    ahead = not (last and p == PAIRS - 1)
                    F = c * PAIRS + (p + 1)
                    between = {1: lambda: first_sum(c, p)}
                    if p or not first:
                        before = (c, p - 1) if p else (c - 1, PAIRS - 1)
                        for i, n in enumerate(DIVIDE_AFTER):
                            between[n] = lambda i=i: divide(*before, i)
                    if p == 0 and not first:
                        for i, n in enumerate(RESIDUAL_AFTER):
                            between[n] = lambda i=i: (residual(c - 1, 2 * i, misc), residual(c - 1, 2 * i + 1, misc))
                    max_row(c * PAIRS + p, p % 2)
                    if p == 0 and first:
                        dve.sem_inc(v_misc, 3)
                    if ahead:
                        q_low(F, parity(p))
                        piece_maxima(F, parity(p), between)
                    else:
                        for n in sorted(between):
                            between[n]()
                    if p == 0 and not first:
                        norm(c - 1)

            dve.sem_inc(v_o, SEED)
            dve.sem_inc(v_misc, SEED)
            q_low(0, 0)
            piece_maxima(0, 0, {})
            chunk(0, True, False)
            with dve.Fori(1, CHUNKS - 1) as c:
                chunk(c, False, False)
            chunk(CHUNKS - 1, False, True)
            for i in range(QT):
                divide(CHUNKS - 1, PAIRS - 1, i)
            for i in range(QT):
                residual(CHUNKS - 1, i, mx[i // 2])
            norm(CHUNKS - 1)

        @block.tensor
        def _(pe):
            pe.sem_inc(p_pv, RING)
            for begun in (p_qk, p_sum, p_wo):
                pe.sem_inc(begun, SEED)

            def q_proj(pair, par):
                for k in range(DK):
                    mm = pe.matmul(mx[par][:], wq[:, k, pair * P:(pair + 1) * P], x1T[:, k, :],
                                   start=(k == 0), stop=(k == DK - 1))
                mm.then_inc(p_q, 1)

            def max_scores(F, pair, par, use, n):
                u, j = (n - 1) // len(KC), (n - 1) % len(KC)
                h, i = u // QT, u % QT
                k0, kn = KC[j]
                if n == 1:
                    pe.wait_ge(v_lo, F * 2 + 2)
                if use is not None:
                    pe.wait_ge(v_mx, use + (n - 1))
                elif n >= 2:
                    pe.wait_ge(v_mx, n - 1)
                pe.matmul(mx[(par + n) % 2][:, 0:kn], Q1[:, par, h, i * P:(i + 1) * P], K1[:, 2 * pair + h, k0:k0 + kn],
                          start=True, stop=True).then_inc(p_mx, 1)

            def max_transpose(c, p):
                pe.wait_ge(v_nm, c * PAIRS + (p + 1))
                pe.wait_ge(v_misc, SEED + max_use(c, p))
                pe.transpose(misc[0:2 * QT, 0:P], nm[:, p % 2], ident[:]).then_inc(p_mT, 1)

            def scores_1(c, p, t):
                g, r = p * KT + t, rows_of(t)
                pe.wait_ge(a_probs, c * PAIRS * KT + (g + 1))
                for h in range(2):
                    pe.matmul(st[g % 2][0:r, h * QC:(h + 1) * QC], K1[:, 2 * p + h, t * P:t * P + r], Q1[:, p % 2, h],
                              start=True, stop=False)

            def scores_2(c, p, t):
                g, r = p * KT + t, rows_of(t)
                par = p % 2
                if t == 0:
                    pe.wait_ge(d_q2[par], (c * 2 + (p // 2 + 1)) * 16)
                    pe.wait_ge(d_m[par], (c * 2 + (p // 2 + 1)) * 32)
                for h in range(2):
                    mm = pe.matmul(st[g % 2][0:r, h * QC:(h + 1) * QC], K2[0:DH + 1, 2 * p + h, t * P:t * P + r],
                                   Q2[0:DH + 1, par, h], start=False, stop=True)
                mm.then_inc(p_qk, 1)

            def values(c, p, t):
                g, r = p * KT + t, rows_of(t)
                pe.wait_ge(a_probs, c * PAIRS * KT + (g + 3))
                if t == 0:
                    pe.wait_ge(a_av, SEED + c * PAIRS + p)
                for h in range(2):
                    mm = pe.matmul(av[h * DH:(h + 1) * DH, :], V[0:r, t, (2 * p + h) * DH:(2 * p + h + 1) * DH],
                                   probs[0:r, g % RING, h * QC:(h + 1) * QC], start=(t == 0), stop=(t == KT - 1))
                mm.then_inc(p_pv, 1)

            def sums(c, p, use):
                S0 = c * PAIRS + p
                pe.wait_ge(g_add, (S0 + 2) * G_ADDS)
                pe.wait_ge(v_misc, SEED + use)
                for h in range(2):
                    mm = pe.matmul(misc[h * DH:(h + 1) * DH, :], ones[:], accG[:, h * QC:(h + 1) * QC], start=True, stop=True)
                mm.then_inc(p_sum, 1)

            def output(c, a):
                pe.wait_ge(v_misc, SEED + out_use(c, a))
                pe.wait_ge(v_o, SEED + (c * PAIRS + PAIRS) * QT)
                for i in (2 * a, 2 * a + 1):
                    for p in range(PAIRS):
                        mm = pe.matmul(misc[:, (i % 2) * D:(i % 2 + 1) * D], oT[:, p, i * P:(i + 1) * P], wo[:, p, :],
                                       start=(p == 0), stop=(p == PAIRS - 1))
                    mm.then_inc(p_wo, 1)

            def last_output(end):
                steps = CHUNKS * PAIRS
                if not end:
                    pe.wait_ge(v_o, SEED + (steps - 1) * QT)
                    pe.wait_ge(v_mx, steps * STEP_MX)
                for i in range(QT):
                    if end:
                        pe.wait_ge(v_o, SEED + (steps - 1) * QT + (i + 1))
                    for p in ((PAIRS - 1,) if end else range(PAIRS - 1)):
                        mm = pe.matmul(mx[i // 2][:, (i % 2) * D:(i % 2 + 1) * D], oT[:, p, i * P:(i + 1) * P], wo[:, p, :],
                                       start=(p == 0 and i % 2 == 0), stop=end, skip_group_check=True)
                    if end:
                        mm.then_inc(p_wo, 1)

            def chunk(c, first, last):
                for p in range(PAIRS):
                    ahead = not (last and p == PAIRS - 1)
                    F, pair, par = c * PAIRS + (p + 1), (p + 1) % PAIRS, parity(p)
                    before = (c, p - 1) if p else None if first else (c - 1, PAIRS - 1)
                    use = F * STEP_MX
                    done = [0]

                    def next_piece():
                        done[0] += 1
                        if ahead and done[0] < STEP_MX:
                            max_scores(F, pair, par, use, done[0])

                    scores_1(c, p, 0)
                    max_transpose(c, p)
                    scores_1(c, p, 1)
                    if ahead:
                        pe.wait_ge(v_mx, use - 1)
                        if pair == 0:
                            pe.wait_ge(d_x1Tc, (c + 2) * 16)
                        q_proj(pair, par)
                    if before:
                        values(*before, KT - 1)
                    scores_2(c, p, 0)
                    scores_2(c, p, 1)
                    if before:
                        sums(*before, sum_use(*before))
                    values(c, p, 0)
                    for t in range(2, KT):
                        scores_1(c, p, t)
                        next_piece()
                        scores_2(c, p, t)
                        next_piece()
                        values(c, p, t - 1)
                        next_piece()
                        if p == 0 and not first and t in OUTPUT_AT:
                            output(c - 1, OUTPUT_AT.index(t))

            pe.wait_ge(d_w, 32)
            pe.wait_ge(d_x1Tc, 16)
            pe.wait_ge(g_ones, 1)
            q_proj(0, 0)
            for n in range(1, STEP_MX):
                max_scores(0, 0, 0, None, n)
            chunk(0, True, False)
            with pe.Fori(1, CHUNKS - 1) as c:
                chunk(c, False, False)
            chunk(CHUNKS - 1, False, True)
            values(CHUNKS - 1, PAIRS - 1, KT - 1)
            last_output(False)
            sums(CHUNKS - 1, PAIRS - 1, LAST_SUM_USE)
            last_output(True)


EXPERTS, FE = 16, 256
SF = 1024
FK = SF // P
ETILES = TILES + EXPERTS - 1
GRID_REV, GRID_THR, GRID_J = 0, EXPERTS, EXPERTS + TILES


def route_and_share(nc, io, mem):
    x2, pos, te, ident = mem["x2"], mem["pos"], mem["te"], mem["ident2"]
    w_gate_up, w_down = mem["w_gate_up"], mem["w_down"]
    with ExitStack() as ctx:
        def sb(name, shape, dt=F32):
            return ctx.enter_context(nc.sbuf_tensor(name, shape, dt))

        def sem(name):
            return ctx.enter_context(nc.semaphore(name))

        x2s = sb("x2s", [P, TILES, D])
        x2T = sb("x2T", [P, DK, S])
        wr = sb("wr", [P, DK, EXPERTS])
        wg = sb("wg", [P, DK, SF])
        wu = sb("wu", [P, DK, SF])
        wd = sb("wd", [P, FK, D])
        upper = sb("upper", [P, P])
        allone = sb("allone", [P, P])
        grid = sb("grid", [P, EXPERTS + TILES + 2 * TILES])
        zero = sb("zero", [P, 4, D])
        silu = sb("silu", [P, 2, 512])
        hT = sb("hT", [P, FK, 512])
        lg = sb("lg", [P, TILES, EXPERTS])
        top = sb("top", [P, TILES])
        esc = sb("esc", [P, 3, TILES])
        work = sb("work", [P, 2, TILES, EXPERTS])
        oneh = sb("oneh", [P, TILES, EXPERTS])
        rev = sb("rev", [P, TILES])
        carry = sb("carry", [P, TILES + 1, EXPERTS])
        nt = sb("nt", [P, EXPERTS])
        incl = sb("incl", [P, EXPERTS])
        off = sb("off", [P, 2, EXPERTS])
        posf = sb("posf", [P, TILES])
        cmpj = sb("cmpj", [P, 2 * TILES, EXPERTS])
        tef = sb("tef", [P, 2, 2 * TILES])
        onesr = sb("onesr", [P, EXPERTS])
        bt = [ctx.enter_context(nc.psum_tensor(f"bt{i}", [P, 512], F32)) for i in range(2)]
        bg = [ctx.enter_context(nc.psum_tensor(f"bg{i}", [P, 512], F32)) for i in range(2)]
        bu = [ctx.enter_context(nc.psum_tensor(f"bu{i}", [P, 512], F32)) for i in range(2)]
        br = ctx.enter_context(nc.psum_tensor("br", [P, 512], F32))
        bp = ctx.enter_context(nc.psum_tensor("bp", [P, 512], F32))

        d_x2i, d_r, d_wg, d_wu, d_wd, d_zero, d_scatter = (sem("d_x2i"), sem("d_r"), sem("d_wg"), sem("d_wu"),
                                                           sem("d_wd"), sem("d_zero"), sem("d_scatter"))
        g_zero = sem("g_zero")
        p_tr, a_tr, p_lg = sem("p_tr"), sem("a_tr"), sem("p_lg")
        v_route = sem("v_route")
        a_sc, v_oh, p_px, v_pos, v_score, g_x2s = (sem("a_sc"), sem("v_oh"), sem("p_px"), sem("v_pos"),
                                                   sem("v_score"), sem("g_x2s"))
        p_gu, a_silu, v_h, p_dn, v_base = sem("p_gu"), sem("a_silu"), sem("v_h"), sem("p_dn"), sem("v_base")

        block = ctx.enter_context(nc.Block())

        @block.sync
        def _(sp):
            sp.dma_start(ident[:], io["ident"]).then_inc(d_r, 16)
            sp.dma_start(x2[:], io["x2"].rearrange("(t p) n -> p t n", p=P)).then_inc(d_x2i, 16)
            sp.dma_start(wr[:], io["routerT"].rearrange("(k p) n -> p k n", p=P)).then_inc(d_r, 16)
            sp.dma_start(grid[:], io["grid"]).then_inc(d_r, 16)
            sp.dma_start(upper[:], io["upper"]).then_inc(d_r, 16)
            sp.dma_start(wg[:], io["s_gateT"].rearrange("(k p) n -> p k n", p=P)).then_inc(d_wg, 16)
            sp.dma_start(wu[:], io["s_upT"].rearrange("(k p) n -> p k n", p=P)).then_inc(d_wu, 16)
            sp.dma_start(wd[:], io["s_downT"].rearrange("(k p) n -> p k n", p=P)).then_inc(d_wd, 16)
            sp.wait_ge(g_zero, 1)
            for t in range(0, 2 * TILES, 4):
                sp.dma_start(io["sorted_x"].rearrange("(t p) n -> p t n", p=P)[:, t:t + 4, :], zero[:]).then_inc(d_zero, 16)
            for e in range(0, EXPERTS, 4):
                sp.dma_start(w_gate_up[:, e * DK:(e + 4) * DK, :],
                             io["gate_up"].rearrange("e (k p) n -> p (e k) n", p=P)[:, e * DK:(e + 4) * DK, :]
                             ).then_inc(mem["d_experts"], 16)
                sp.dma_start(w_down[:, e * DK:(e + 4) * DK, :],
                             io["down"].rearrange("e (k p) n -> p (e k) n", p=P)[:, e * DK:(e + 4) * DK, :]
                             ).then_inc(mem["d_experts"], 16)
            sp.wait_ge(d_zero, 16 * 2 * TILES // 4)
            sp.wait_ge(d_scatter, 16 * TILES)

        @block.gpsimd
        def _(pool):
            pool.memset(zero[:], 0.0).then_inc(g_zero, 1)
            pool.wait_ge(g_zero, 1)
            pool.memset(allone[:], 1.0).then_inc(g_zero, 1)
            pool.wait_ge(g_zero, 2)
            pool.memset(onesr[:], 1.0).then_inc(g_zero, 1)
            pool.wait_ge(g_zero, 3)
            pool.memset(carry[:, 0, :], 0.0).then_inc(g_zero, 1)
            pool.wait_ge(g_zero, 4)
            pool.wait_ge(v_score, 2)
            for t in range(TILES):
                pool.tensor_scalar(x2s[:, t], x2[:, t], esc[:, 2, t:t + 1], 0.0, ALU.mult, ALU.add).then_inc(g_x2s, 1)
            pool.wait_ge(v_pos, 1)
            pool.wait_ge(d_zero, 16 * 2 * TILES // 4)
            for t in range(TILES):
                pool.wait_ge(g_x2s, t + 1)
                pool.indirect_dma_start(io["sorted_x"][:, :], bass.IndirectOffsetOnAxis(pos[:, t:t + 1], 0),
                                        x2s[:, t, :], None).then_inc(d_scatter, 16)

        @block.scalar
        def _(act):
            for t in range(TILES):
                act.wait_ge(p_tr, t + 1)
                act.activation(x2T[:, :, t * P:(t + 1) * P], bt[t % 2][:, 0:D].rearrange("p (k n) -> p k n", k=DK),
                               ACT.Copy).then_inc(a_tr, 1)
            act.wait_ge(v_route, 2)
            act.activation(esc[:, 0], top[:], ACT.Exp, scale=-1.0).then_inc(a_sc, 1)

            def gates(c):
                for f in range(FK):
                    act.wait_ge(p_gu, c * FK + (f + 1))
                    if f > 1 or not isinstance(c, int):
                        act.wait_ge(v_h, c * FK + max(f - 1, 0))
                    act.activation(silu[:, f % 2], bg[f % 2][:], ACT.Silu).then_inc(a_silu, 1)

            gates(0)
            with act.Fori(1, CHUNKS) as c:
                gates(c)

        @block.vector
        def _(dve):
            n_route = [0]

            def step(ins):
                n_route[0] += 1
                ins.then_inc(v_route, 1)
                dve.wait_ge(v_route, n_route[0])

            def by_tile(ap):
                return ap.unsqueeze(2).to_broadcast([P, TILES, EXPERTS])

            def by_expert(ap, n=TILES):
                return ap.unsqueeze(1).to_broadcast([P, n, EXPERTS])

            def choose():
                dve.wait_ge(p_lg, 1)
                dve.wait_ge(d_r, 64)
                step(dve.tensor_copy(lg[:], br[:, 0:TILES * EXPERTS].rearrange("p (t n) -> p t n", n=EXPERTS)))
                step(dve.tensor_reduce(top[:], lg[:], AX.X, ALU.max))
                step(dve.tensor_tensor(work[:, 0], lg[:], by_tile(top[:]), ALU.is_equal))
                step(dve.tensor_tensor(work[:, 1], work[:, 0], by_expert(grid[:, GRID_REV:GRID_REV + EXPERTS]), ALU.mult))
                step(dve.tensor_reduce(rev[:], work[:, 1], AX.X, ALU.max))
                dve.tensor_tensor(oneh[:], by_expert(grid[:, GRID_REV:GRID_REV + EXPERTS]), by_tile(rev[:]), ALU.is_equal
                                  ).then_inc(v_oh, 1)
                dve.wait_ge(a_sc, 1)
                dve.tensor_scalar(esc[:, 1], esc[:, 0], 1.0, None, ALU.add).then_inc(v_score, 1)
                dve.wait_ge(v_score, 1)
                dve.reciprocal(esc[:, 2], esc[:, 1]).then_inc(v_score, 1)

            def count():
                dve.wait_ge(p_px, 1)
                dve.wait_ge(g_zero, 4)
                for t in range(TILES):
                    step(dve.tensor_tensor(carry[:, t + 1], bp[:, 256 + t * EXPERTS:256 + (t + 1) * EXPERTS], carry[:, t],
                                           ALU.add))

            def place():
                counts = carry[:, TILES, :].unsqueeze(2).to_broadcast([P, EXPERTS, TILES])
                thresholds = grid[:, GRID_THR:GRID_THR + TILES].unsqueeze(1).to_broadcast([P, EXPERTS, TILES])
                step(dve.tensor_tensor(work[:, 0], counts, thresholds, ALU.is_gt))
                step(dve.tensor_reduce(nt[:], work[:, 0], AX.X, ALU.add))
                step(dve.tensor_tensor_scan(incl[:], onesr[:], nt[:], 0.0, ALU.mult, ALU.add))
                step(dve.tensor_tensor(off[:, 0], incl[:], nt[:], ALU.subtract))
                step(dve.tensor_scalar(off[:, 1], off[:, 0], float(P), None, ALU.mult))
                step(dve.tensor_tensor(work[:, 0], bp[:, 0:256].rearrange("p (t n) -> p t n", n=EXPERTS),
                                       carry[:, 0:TILES, :], ALU.add))
                step(dve.tensor_tensor(work[:, 1], work[:, 0], by_expert(off[:, 1]), ALU.add))
                step(dve.tensor_tensor(work[:, 0], work[:, 1], oneh[:], ALU.mult))
                step(dve.tensor_reduce(posf[:], work[:, 0], AX.X, ALU.add))
                dve.tensor_copy(pos[:], posf[:]).then_inc(v_pos, 1)

            def experts():
                tiles = grid[:, GRID_J:GRID_J + 2 * TILES].unsqueeze(2).to_broadcast([P, 2 * TILES, EXPERTS])
                step(dve.tensor_tensor(cmpj[:], by_expert(incl[:], 2 * TILES), tiles, ALU.is_le))
                step(dve.tensor_reduce(tef[:, 0], cmpj[:], AX.X, ALU.add))
                step(dve.tensor_scalar(tef[:, 1], tef[:, 0], float(EXPERTS - 1), None, ALU.min))
                step(dve.tensor_copy(te[:], tef[:, 1]))

            def hidden(c, f):
                dve.wait_ge(a_silu, c * FK + (f + 1))
                dve.tensor_tensor(hT[:, f], silu[:, f % 2], bu[f % 2][:], ALU.mult).then_inc(v_h, 1)

            def residual(c):
                for i in range(QT):
                    dve.wait_ge(p_dn, c * QT + (i + 1))
                    t = c * QT + i
                    xx = x2[:, t] if isinstance(t, int) else x2[:, bass.ds(t, 1), :].squeeze(1)
                    dve.tensor_tensor(xx, bt[i % 2][:, 0:D], xx, ALU.add).then_inc(v_base, 1)

            hidden_steps = {0: choose, 2: count, 4: place, 6: experts}
            for f in range(FK):
                if f in hidden_steps:
                    hidden_steps[f]()
                hidden(0, f)
            dve.wait_ge(g_x2s, TILES)
            residual(0)
            with dve.Fori(1, CHUNKS) as c:
                for f in range(FK):
                    hidden(c, f)
                residual(c)

        @block.tensor
        def _(pe):
            pe.wait_ge(d_r, 64)
            pe.wait_ge(d_x2i, 16)

            def logits(t):
                pe.wait_ge(a_tr, t + 1)
                for k in range(DK):
                    mm = pe.matmul(br[:, t * EXPERTS:(t + 1) * EXPERTS], x2T[:, k, t * P:(t + 1) * P], wr[:, k, :],
                                   start=(k == 0), stop=(k == DK - 1))
                if t == TILES - 1:
                    mm.then_inc(p_lg, 1)

            for t in range(TILES):
                if t >= 2:
                    pe.wait_ge(a_tr, t - 1)
                for k in range(DK):
                    mm = pe.transpose(bt[t % 2][:, k * P:(k + 1) * P], x2[:, t, k * P:(k + 1) * P], ident[:])
                mm.then_inc(p_tr, 1)
                if t >= 2:
                    logits(t - 2)
            logits(TILES - 2)
            logits(TILES - 1)

            def gate_up(c, f):
                cols = slice(c * 512, (c + 1) * 512) if isinstance(c, int) else bass.ds(c * 512, 512)
                if f >= 2 or not isinstance(c, int):
                    pe.wait_ge(v_h, c * FK + max(f - 1, 0))
                for w, bank in ((wg, bg), (wu, bu)):
                    for k in range(DK):
                        mm = pe.matmul(bank[f % 2][:], w[:, k, f * P:(f + 1) * P], x2T[:, k, cols],
                                       start=(k == 0), stop=(k == DK - 1))
                mm.then_inc(p_gu, 1)

            def down(c):
                pe.wait_ge(v_h, (c + 1) * FK)
                for i in range(QT):
                    if i >= 2 or not isinstance(c, int):
                        pe.wait_ge(v_base, c * QT + max(i - 1, 0))
                    for f in range(FK):
                        mm = pe.matmul(bt[i % 2][:, 0:D], hT[:, f, i * P:(i + 1) * P], wd[:, f, :],
                                       start=(f == 0), stop=(f == FK - 1))
                    mm.then_inc(p_dn, 1)

            pe.wait_ge(d_wg, 16)
            pe.wait_ge(d_wu, 16)
            pe.wait_ge(g_zero, 2)
            for f in range(FK):
                gate_up(0, f)
                if f == 1:
                    pe.wait_ge(v_oh, 1)
                    pe.matmul(bp[:, 0:256], upper[:], oneh[:].rearrange("p t n -> p (t n)"), start=True, stop=True)
                    pe.matmul(bp[:, 256:512], allone[:], oneh[:].rearrange("p t n -> p (t n)"), start=True, stop=True
                              ).then_inc(p_px, 1)
            pe.wait_ge(d_wd, 16)
            down(0)
            with pe.Fori(1, CHUNKS) as c:
                for f in range(FK):
                    gate_up(c, f)
                down(c)


UNROLL = 6


def experts(nc, io, mem):
    base, pos, te, ident = mem["x2"], mem["pos"], mem["te"], mem["ident2"]
    w_gate_up, w_down = mem["w_gate_up"], mem["w_down"]
    with ExitStack() as ctx:
        def sb(name, shape, dt=F32):
            return ctx.enter_context(nc.sbuf_tensor(name, shape, dt))

        def sem(name):
            return ctx.enter_context(nc.semaphore(name))

        xs = sb("xs", [P, UNROLL, D])
        xsT = sb("xsT", [P, UNROLL, D])
        sil = sb("sil", [P, UNROLL, FE])
        h = sb("h", [P, UNROLL, FE])
        hTt = sb("hTt", [P, UNROLL, FE])
        ysb = sb("ysb", [P, UNROLL, D])
        yg = sb("yg", [P, TILES, D])
        st7 = sb("st7", [P, TILES, 6])
        mv4 = sb("mv4", [P, TILES, 2])
        ve4 = sb("ve4", [P, TILES])
        rstd4 = sb("rstd4", [P, TILES])
        mhalf4 = sb("mhalf4", [P, 4])
        eps4 = sb("eps4", [P, 4])
        bx = [ctx.enter_context(nc.psum_tensor(f"bx{i}", [P, 512], F32)) for i in range(2)]
        bgu = [ctx.enter_context(nc.psum_tensor(f"bgu{i}", [P, 512], F32)) for i in range(2)]
        bh = [ctx.enter_context(nc.psum_tensor(f"bh{i}", [P, 512], F32)) for i in range(2)]
        by = [ctx.enter_context(nc.psum_tensor(f"by{i}", [P, 512], F32)) for i in range(2)]

        d_xs = [sem(f"d_xs{i}") for i in range(UNROLL)]
        d_y = [sem(f"d_y{i}") for i in range(UNROLL)]
        d_yg = [sem(f"d_yg{i}") for i in range(4)]
        d_out = sem("d_out")
        g_c4 = sem("g_c4")
        s_turn = sem("s_turn")
        p_x, a_x, p_e, a_s, v_hh, p_h, v_hT, p_y, v_y = (sem("p_x"), sem("a_x"), sem("p_e"), sem("a_s"), sem("v_hh"),
                                                         sem("p_h"), sem("v_hT"), sem("p_y"), sem("v_y"))
        v_f, v_mv4, g_l4, g_r4, v_out = sem("v_f"), sem("v_mv4"), sem("g_l4"), sem("g_r4"), sem("v_out")
        v_st4 = sem("v_st4")

        block = ctx.enter_context(nc.Block())

        @block.sync
        def _(sp):
            xs_rows = io["sorted_x"].rearrange("(t p) n -> p t n", p=P)

            def load(j, r):
                sp.dma_start(xs[:, r], xs_rows[:, bass.ds(j, 1), :].squeeze(1)).then_inc(d_xs[r], 16)

            for r in range(UNROLL):
                load(r, r)
            with sp.Fori(0, (ETILES - 1) // UNROLL - 1) as i:
                for r in range(UNROLL):
                    sp.wait_ge(p_x, i * UNROLL + (r + 1))
                    sp.sem_inc(s_turn, 1)
                    load(i * UNROLL + (r + UNROLL), r)
            sp.wait_ge(p_x, ETILES - UNROLL)
            load(ETILES - 1, 0)
            out_rows = io["out"].rearrange("(t p) n -> p t n", p=P)
            for g in range(TILES // 4):
                sp.wait_ge(v_out, 4 * (g + 1))
                sp.dma_start(out_rows[:, 4 * g:4 * g + 4, :], base[:, 4 * g:4 * g + 4, :]).then_inc(d_out, 16)
            sp.wait_ge(d_out, 16 * TILES // 4)

        @block.gpsimd
        def _(pool):
            pool.memset(mhalf4[:], -0.5).then_inc(g_c4, 1)
            pool.wait_ge(g_c4, 1)
            pool.memset(eps4[:], EPS).then_inc(g_c4, 1)
            pool.wait_ge(g_c4, 2)
            y_rows = io["sorted_y"].rearrange("(t p) n -> p t n", p=P)

            def store(j, r):
                pool.wait_ge(v_y, j + 1)
                pool.sem_inc(g_c4, 1)
                pool.dma_start(y_rows[:, bass.ds(j, 1), :].squeeze(1), ysb[:, r]).then_inc(d_y[r], 16)

            with pool.Fori(0, (ETILES - 1) // UNROLL) as i:
                for r in range(UNROLL):
                    store(i * UNROLL + r, r)
            store(ETILES - 1, 0)
            for r in range(UNROLL):
                pool.wait_ge(d_y[r], 16 * ((ETILES - 1 - r) // UNROLL + 1))
            for t in range(TILES):
                pool.indirect_dma_start(yg[:, t, :], None, io["sorted_y"][:, :],
                                        bass.IndirectOffsetOnAxis(pos[:, t:t + 1], 0)).then_inc(d_yg[t // 4], 16)
            for g in range(4):
                pool.wait_ge(v_mv4, 4 * (g + 1))
                pool.tensor_tensor(ve4[:, 4 * g:4 * g + 4], mv4[:, 4 * g:4 * g + 4, 1], eps4[:], ALU.add).then_inc(g_l4, 1)
                pool.wait_ge(g_l4, g + 1)
                pool.tensor_tensor(rstd4[:, 4 * g:4 * g + 4], ve4[:, 4 * g:4 * g + 4], mhalf4[:], ALU.pow).then_inc(g_r4, 1)

        @block.scalar
        def _(act):
            def copy_x(j, r):
                act.wait_ge(p_x, j + 1)
                act.activation(xsT[:, r], bx[r % 2][:, 0:D], ACT.Copy).then_inc(a_x, 1)

            def gate(j, r):
                act.wait_ge(p_e, j + 1)
                act.activation(sil[:, r], bgu[r % 2][:, 0:FE], ACT.Silu).then_inc(a_s, 1)

            copy_x(0, 0)
            copy_x(1, 1)
            gate(0, 0)
            with act.Fori(0, (ETILES - 1) // UNROLL - 1) as i:
                for n in range(UNROLL):
                    copy_x(i * UNROLL + (n + 2), (2 + n) % UNROLL)
                    gate(i * UNROLL + (n + 1), (1 + n) % UNROLL)
            for j in range(ETILES - UNROLL, ETILES):
                if j + 1 < ETILES:
                    copy_x(j + 1, (j + 1) % UNROLL)
                gate(j, j % UNROLL)

        @block.vector
        def _(dve):
            def product(j, r):
                dve.wait_ge(a_s, j + 1)
                dve.tensor_tensor(h[:, r], sil[:, r], bgu[r % 2][:, FE:2 * FE], ALU.mult).then_inc(v_hh, 1)

            def copy_h(j, r):
                dve.wait_ge(p_h, j + 1)
                dve.tensor_copy(hTt[:, r], bh[r % 2][:, 0:FE]).then_inc(v_hT, 1)

            def copy_y(j, r, stored):
                dve.wait_ge(p_y, j + 1)
                if stored is not None:
                    dve.wait_ge(d_y[r], stored)
                dve.tensor_copy(ysb[:, r], by[r % 2][:, 0:D]).then_inc(v_y, 1)

            product(0, 0)
            for j in range(1, 1 + UNROLL):
                copy_h(j - 1, (j - 1) % UNROLL)
                product(j, j % UNROLL)
                copy_y(j - 1, (j - 1) % UNROLL, None)
            with dve.Fori(1, (ETILES - 1) // UNROLL) as i:
                for n in range(UNROLL):
                    j = i * UNROLL + (1 + n)
                    copy_h(j - 1, n)
                    product(j, (1 + n) % UNROLL)
                    copy_y(j - 1, n, i * 16)
            copy_h(ETILES - 1, 0)
            copy_y(ETILES - 1, 0, 16 * ((ETILES - 1) // UNROLL))
            for t in range(TILES + 4):
                if t < TILES:
                    if t % 4 == 0:
                        dve.wait_ge(d_yg[t // 4], 64)
                    dve.tensor_tensor(base[:, t], base[:, t], yg[:, t], ALU.add).then_inc(v_f, 1)
                    dve.wait_ge(v_f, t + 1)
                    dve.bn_stats(st7[:, t], base[:, t]).then_inc(v_st4, 1)
                    dve.wait_ge(v_st4, t + 1)
                    dve.bn_aggr(mv4[:, t], st7[:, t]).then_inc(v_mv4, 1)
                if t >= 4:
                    q = t - 4
                    dve.wait_ge(g_r4, q // 4 + 1)
                    dve.tensor_scalar(base[:, q], base[:, q], mv4[:, q, 0:1], rstd4[:, q:q + 1], ALU.subtract, ALU.mult
                                      ).then_inc(v_out, 1)

        @block.tensor
        def _(pe):
            def expert_of(j):
                return pe.value_load(te[0:1, bass.ds(j, 1)], min_val=0, max_val=EXPERTS - 1)

            def transpose_x(j, r, landed):
                pe.wait_ge(d_xs[r], landed)
                if not (isinstance(j, int) and j < 2):
                    pe.wait_ge(a_x, j - 1)
                for k in range(DK):
                    mm = pe.transpose(bx[r % 2][:, k * P:(k + 1) * P], xs[:, r, k * P:(k + 1) * P], ident[:])
                mm.then_inc(p_x, 1)

            def gate_up(j, r):
                e = expert_of(j)
                pe.wait_ge(a_x, j + 1)
                for k in range(DK):
                    mm = pe.matmul(bgu[r % 2][:], xsT[:, r, k * P:(k + 1) * P],
                                   w_gate_up[:, bass.ds(e * DK + k, 1), :].squeeze(1), start=(k == 0), stop=(k == DK - 1))
                mm.then_inc(p_e, 1)

            def transpose_h(j, r):
                pe.wait_ge(v_hh, j + 1)
                if not (isinstance(j, int) and j < 2):
                    pe.wait_ge(v_hT, j - 1)
                for k in range(DK):
                    mm = pe.transpose(bh[r % 2][:, k * P:(k + 1) * P], h[:, r, k * P:(k + 1) * P], ident[:])
                mm.then_inc(p_h, 1)

            def down(j, r):
                e = expert_of(j)
                pe.wait_ge(v_hT, j + 1)
                if not (isinstance(j, int) and j < 2):
                    pe.wait_ge(v_y, j - 1)
                for k in range(DK):
                    mm = pe.matmul(by[r % 2][:, 0:D], hTt[:, r, k * P:(k + 1) * P],
                                   w_down[:, bass.ds(e * DK + k, 1), :].squeeze(1), start=(k == 0), stop=(k == DK - 1))
                mm.then_inc(p_y, 1)

            def slot(j, n, i):
                r0, r1, r2 = n, (n + 1) % UNROLL, (n + 2) % UNROLL
                if not (isinstance(j, int) and j == ETILES - 1):
                    transpose_x(j + 1, r2, (i + 1 + (n + 2) // UNROLL) * 16)
                transpose_h(j - 1, r0)
                gate_up(j, r1)
                down(j - 1, r0)

            transpose_x(0, 0, 16)
            transpose_x(1, 1, 16)
            pe.wait_ge(mem["d_experts"], 16 * 2 * EXPERTS // 4)
            gate_up(0, 0)
            for n in range(UNROLL):
                slot(1 + n, n, 0)
            with pe.Fori(1, (ETILES - 1) // UNROLL - 1) as i:
                for n in range(UNROLL):
                    slot(i * UNROLL + (1 + n), n, i)
            last = (ETILES - 1) // UNROLL - 1
            for n in range(UNROLL):
                slot(last * UNROLL + 1 + n, n, last)
            transpose_h(ETILES - 1, 0)
            down(ETILES - 1, 0)


def program(nc, io, stages=3):
    with ExitStack() as ctx:
        mem = {}
        for name, shape, dt in (("K1", [P, HEADS, KEYS_PAD], F32R), ("K2", [P, HEADS, KEYS_PAD], F32R),
                                ("V", [P, KT, HID], F32), ("ident", [P, P], F32)):
            mem[name] = ctx.enter_context(nc.sbuf_tensor(name, shape, dt))
        before_attention(nc, io, mem)
        if stages > 1:
            attention(nc, io, mem)
    if stages > 2:
        with ExitStack() as ctx:
            mem = {"x2": ctx.enter_context(nc.sbuf_tensor("x2", [P, TILES, D], F32)),
                   "w_gate_up": ctx.enter_context(nc.sbuf_tensor("w_gate_up", [P, EXPERTS * DK, 2 * FE], F32)),
                   "w_down": ctx.enter_context(nc.sbuf_tensor("w_down", [P, EXPERTS * DK, D], F32)),
                   "d_experts": ctx.enter_context(nc.semaphore("d_experts")),
                   "ident2": ctx.enter_context(nc.sbuf_tensor("ident2", [P, P], F32)),
                   "pos": ctx.enter_context(nc.sbuf_tensor("pos", [P, TILES], mybir.dt.uint32)),
                   "te": ctx.enter_context(nc.sbuf_tensor("te", [P, 2 * TILES], I32))}
            route_and_share(nc, io, mem)
            experts(nc, io, mem)


_SCRATCH = {"x1b": (S, D), "x1T": (D, S), "x2": (S, D), "sorted_x": (2 * S, D), "sorted_y": (ETILES * P, D)}


def kernel(x, ctx_1024, L0_attn_W_in, L0_attn_b_in, L0_attn_log_A, L0_attn_B_p, L0_attn_C_p, L0_attn_W_out,
           L0_attn_b_out, L0_attn_gamma, L0_attn_beta, L0_xattn_Wq, L0_xattn_Wk, L0_xattn_Wv, L0_xattn_Wo,
           L0_xattn_bo, L0_ffn_router_w, L0_ffn_gate_up_proj, L0_ffn_down_proj, L0_ffn_shared_gate_w,
           L0_ffn_shared_up_w, L0_ffn_shared_down_w):
    import numpy as np
    import concourse.bacc as bacc
    from concourse.bass_utils import run_bass_kernel_spmd

    ctx_rows = ctx_1024[0]
    host = {
        "x": x[0], "xT": x[0].T, "ctxT": np.concatenate([ctx_rows, ctx_rows[-1:]]).T,
        "w_inT": L0_attn_W_in.T, "w_outT": L0_attn_W_out.T,
        "cols": np.stack([np.reshape(a, (DK, P)) for a in (L0_attn_b_in, L0_attn_log_A, L0_attn_B_p, L0_attn_C_p)]
                         ).transpose(2, 0, 1),
        "b_out": L0_attn_b_out, "gamma": L0_attn_gamma, "beta": L0_attn_beta, "bo": L0_xattn_bo,
        "wq": L0_xattn_Wq, "wk": L0_xattn_Wk, "wv": L0_xattn_Wv, "wo": L0_xattn_Wo,
        "routerT": L0_ffn_router_w.T, "gate_up": L0_ffn_gate_up_proj, "down": L0_ffn_down_proj,
        "s_gateT": L0_ffn_shared_gate_w.T, "s_upT": L0_ffn_shared_up_w.T, "s_downT": L0_ffn_shared_down_w.T,
        "ident": np.eye(P, dtype=np.float32), "upper": np.triu(np.ones((P, P), np.float32), 1),
        "grid": np.tile(np.concatenate([EXPERTS - np.arange(EXPERTS), P * np.arange(TILES), np.arange(2 * TILES)]
                                       ).astype(np.float32), (P, 1)),
    }
    nc = bacc.Bacc("TRN2", target_bir_lowering=False, num_devices=1)
    io, arrays = {}, {}
    for name, a in host.items():
        a = np.ascontiguousarray(a)
        arrays["in_" + name] = a
        io[name] = nc.dram_tensor("in_" + name, a.shape, mybir.dt.from_np(a.dtype), kind="ExternalInput").ap()
    for name, shape in _SCRATCH.items():
        io[name] = nc.dram_tensor("scratch_" + name, shape, F32, kind="Internal").ap()
    io["out"] = nc.dram_tensor("out_0", (S, D), F32, kind="ExternalOutput").ap()
    program(nc, io)
    r = run_bass_kernel_spmd(nc, [arrays], core_ids=[0])
    return r.results[0]["out_0"].reshape(1, S, D)
```

```python
from contextlib import ExitStack

import concourse.bass as bass
from concourse import mybir

F32 = mybir.dt.float32
F32R = mybir.dt.float32r
I32 = mybir.dt.int32
ALU = mybir.AluOpType
ACT = mybir.ActivationFunctionType
AX = mybir.AxisListType

P = 128
S, D = 2048, 256
TILES = S // P
DK = D // P
KEYS = 1601
KEYS_PAD = 1602
KT = (KEYS + P - 1) // P
LAST = KEYS - (KT - 1) * P
HEADS, DH = 8, 64
HID = HEADS * DH
PAIRS = HEADS // 2
QC = 512
CHUNKS = S // QC
QT = QC // P
EPS = 1e-5
TILE_U = 2 * QT
KC = [(0, 402), (402, 400), (802, 400), (1202, 400)]


def before_attention(nc, io, mem):
    K1, K2, V, ident = mem["K1"], mem["K2"], mem["V"], mem["ident"]
    with ExitStack() as ctx:
        def sb(name, shape, dt=F32):
            return ctx.enter_context(nc.sbuf_tensor(name, shape, dt))

        def sem(name):
            return ctx.enter_context(nc.semaphore(name))

        xT = sb("xT", [P, DK, S])
        z = xT[:, :, :].rearrange("p k (a n) -> p (k a) n", n=D)
        state = sb("state", [P, DK, S])
        xring = sb("xring", [P, 2, 4, D])
        w_in = sb("w_in", [P, DK, D])
        w_out = sb("w_out", [P, DK, D])
        ctxT = sb("ctxT", [P, DK, KEYS_PAD])
        wk = sb("wk", [P, DK, HID])
        wv = sb("wv", [P, DK, HID])
        cols = sb("cols", [P, 4, DK])
        rows = mem["x1"]
        decay = sb("decay", [P, 3, DK])
        bB = sb("bB", [P, DK])
        stats = sb("stats", [P, 4, 2, 6])
        mv = sb("mv", [P, 2, TILES, 2])
        ve = sb("ve", [P, 2, TILES])
        rstd = sb("rstd", [P, 2, TILES])
        mhalf = sb("mhalf", [P, 4])
        shift = sb("shift", [P, TILES])
        wq0 = sb("wq0", [P, DK, P])
        x1Tb = w_in[:, :, :].rearrange("p k (a n) -> p a k n", n=P)
        x1T, Q1, mxp, nm = mem["x1T"], mem["Q1"][0], mem["mxp"], mem["nm"]
        banks = [ctx.enter_context(nc.psum_tensor(f"bank_a{i}", [P, 512], F32)) for i in range(8)]

        d_x = [sem(f"d_xT{c}") for c in range(4)]
        d_win, d_rows = sem("d_win"), sem("d_rows")
        d_ident = sem("d_ident")
        d_ctx, d_wv = sem("d_ctx"), sem("d_wv")
        d_xring = [sem(f"d_xring{i}") for i in range(2)]
        d_dup0 = sem("d_dup0")
        d_dup = mem["d_dup"]
        d_x1 = sem("d_x1")
        d_x1T = [sem(f"d_x1T{i}") for i in range(2)]
        prep = sem("prep")
        a_exp = sem("a_exp")
        p_in, a_u, v_scan = sem("p_in"), sem("a_u"), sem("v_scan")
        p_out, v_z = sem("p_out"), sem("v_z")
        v_link = sem("v_link")
        v_mv1, v_mv2 = sem("v_mv1"), sem("v_mv2")
        g_const, g_link, g_xb, g_rstd1, g_rstd2 = sem("g_const"), sem("g_link"), sem("g_xb"), sem("g_rstd1"), sem("g_rstd2")
        v_b = sem("v_b")
        p_k, a_khi, v_klo = sem("p_k"), sem("a_khi"), sem("v_klo")
        p_v, a_v = sem("p_v"), sem("a_v")
        p_t, a_t = sem("p_t"), sem("a_t")
        g_x1b = sem("g_x1b")
        v_shift2, a_x1 = sem("v_shift2"), sem("a_x1")
        p_q0, a_q0, v_q0 = sem("p_q0"), sem("a_q0"), sem("v_q0")
        p_mx0, v_mx0, v_nm0 = sem("p_mx0"), sem("v_mx0"), sem("v_nm0")

        G = TILES // 4
        kunits = [(p, j) for p in range(PAIRS) for j in range(len(KC))]
        kv = ([("k", n) for n in range(4)] + [("v", n) for n in range(8)] + [("k", n) for n in range(4, 8)]
              + [u for n in range(8, KT) for u in (("k", n), ("v", n))] + [("k", n) for n in range(KT, 16)])
        PIECES = TILE_U * len(KC)
        THREE_FROM = 24

        def slots(out=None, key=None, val=None, norm_b=None, shifts=None, norm_c=None, tr=None, query=None, piece=None,
                  low=None):
            def do(f, n, end):
                if f and 0 <= n < end:
                    f(n)

            pieces = iter(range(PIECES))
            for t in range(len(kv) + 4):
                do(out, t, TILES)
                do(norm_b, t - 5, TILES)
                if t % 4 == 1:
                    do(shifts, (t - 9) // 4, G)
                do(norm_c, t - 10, TILES)
                do(tr, t - 12, TILES)
                if t == 16:
                    do(query, 0, 1)
                if t > 16:
                    do(piece, next(pieces, -1), PIECES)
                if t < len(kv):
                    kind, u = kv[t]
                    do(key if kind == "k" else val, u, 16)
                if t > 16:
                    do(piece, next(pieces, -1), PIECES)
                if t < len(kv) and kv[t][0] == "k":
                    do(low, kv[t][1], 16)
                if t >= THREE_FROM:
                    do(piece, next(pieces, -1), PIECES)

        block = ctx.enter_context(nc.Block())

        @block.sync
        def _(sp):
            sp.dma_start(w_in[:], io["w_inT"].rearrange("(k p) n -> p k n", p=P)).then_inc(d_win, 16)
            sp.dma_start(cols[:], io["cols"]).then_inc(d_win, 16)
            for c in range(4):
                sp.dma_start(xT[:, :, c * 512:(c + 1) * 512],
                             io["xT"].rearrange("(k p) n -> p k n", p=P)[:, :, c * 512:(c + 1) * 512]).then_inc(d_x[c], 16)
            sp.dma_start(w_out[:], io["w_outT"].rearrange("(k p) n -> p k n", p=P)).then_inc(d_rows, 16)
            for i, n in enumerate(("b_out", "gamma", "beta", "bo")):
                sp.dma_start(rows[:, i, :], io[n].partition_broadcast(P)).then_inc(d_rows, 16)
            sp.dma_start(wk[:], io["wk"].rearrange("(k p) n -> p k n", p=P)).then_inc(d_ctx, 16)
            sp.dma_start(ctxT[:], io["ctxT"].rearrange("(k p) n -> p k n", p=P)).then_inc(d_ctx, 16)

            def load_x(g):
                sp.dma_start(xring[:, g % 2], io["x"].rearrange("(t p) n -> p t n", p=P)[:, 4 * g:4 * g + 4, :]
                             ).then_inc(d_xring[g % 2], 16)

            load_x(0)
            sp.dma_start(wv[:], io["wv"].rearrange("(k p) n -> p k n", p=P)).then_inc(d_wv, 16)
            load_x(1)
            sp.dma_start(ident[:], io["ident"]).then_inc(d_ident, 16)
            sp.dma_start(wq0[:], io["wq"].rearrange("(k p) n -> p k n", p=P)[:, :, 0:P]).then_inc(d_ident, 16)

            def repeat_keys(p):
                sp.wait_ge(a_khi, 2 * len(KC) * (p + 1))
                for h in (2 * p, 2 * p + 1):
                    sp.dma_start(K1[DH:P, h, :].bitcast(F32), K1[0:DH, h, :].bitcast(F32)
                                 ).then_inc(d_dup if p else d_dup0, 16)

            def store_x1b(g):
                sp.wait_ge(g_x1b, g + 1)
                sp.dma_start(io["x1b"].rearrange("(t p) n -> p t n", p=P)[:, 4 * g:4 * g + 4, :],
                             z[:, 4 * g:4 * g + 4, :]).then_inc(d_x1, 16)

            repeat_keys(0)
            for g in (2, 3):
                sp.wait_ge(v_b, 4 * (g - 1))
                load_x(g)
            store_x1b(0)
            repeat_keys(1)
            store_x1b(1)
            repeat_keys(2)
            store_x1b(2)
            store_x1b(3)
            repeat_keys(3)
            sp.wait_ge(d_x1, 16 * G)

        @block.gpsimd
        def _(pool):
            pool.memset(mhalf[:], -0.5).then_inc(g_const, 1)
            pool.wait_ge(g_const, 1)
            pool.memset(K2[DH:DH + 1, :, :].bitcast(F32), 1.0).then_inc(g_const, 1)
            pool.wait_ge(g_const, 2)
            pool.wait_ge(d_rows, 80)
            links = [0]

            def link(ins):
                links[0] += 1
                ins.then_inc(g_link, 1)
                pool.wait_ge(g_link, links[0])

            def xb(g):
                pool.wait_ge(d_xring[g % 2], 16 * (g // 2 + 1))
                for t in range(4):
                    ins = pool.tensor_tensor(xring[:, g % 2, t], xring[:, g % 2, t], rows[:, 2, :], ALU.add)
                    ins.then_inc(g_xb, 1)

            def inverse(n, g, ready, done):
                pool.wait_ge(ready, 4 * (g + 1))
                link(pool.tensor_scalar(ve[:, n, 4 * g:4 * g + 4], mv[:, n, 4 * g:4 * g + 4, 1], EPS, None, ALU.add))
                pool.tensor_tensor(rstd[:, n, 4 * g:4 * g + 4], ve[:, n, 4 * g:4 * g + 4], mhalf[:], ALU.pow
                                   ).then_inc(done, 1)

            def x1b(g):
                pool.wait_ge(p_t, 4 * (g + 1))
                pool.wait_ge(a_x1, 4 * (g + 1))
                for t in range(4 * g, 4 * g + 4):
                    ins = pool.tensor_tensor(z[:, t, :], z[:, t, :], rows[:, 3, :], ALU.add)
                ins.then_inc(g_x1b, 1)

            def first(g):
                inverse(0, g, v_mv1, g_rstd1)

            def second(g):
                inverse(1, g, v_mv2, g_rstd2)

            for step, g in ((xb, 0), (xb, 1), (first, 0), (first, 1), (second, 0), (xb, 2), (first, 2), (second, 1),
                            (xb, 3), (first, 3), (x1b, 0), (second, 2), (x1b, 1), (second, 3), (x1b, 2), (x1b, 3)):
                step(g)

        @block.scalar
        def _(act):
            act.wait_ge(d_win, 32)
            act.activation(decay[:, 0], cols[:, 1], ACT.Exp).then_inc(a_exp, 1)
            act.wait_ge(prep, 3)
            for n in range(8):
                c, e = n // 2, n % 2
                act.wait_ge(p_in, n + 1)
                act.activation(state[:, e, c * 512:(c + 1) * 512], banks[n % 2][:], ACT.Identity,
                               bias=bB[:, e:e + 1], scale=cols[:, 2, e:e + 1]).then_inc(a_u, 1)

            def key_high(n):
                p, j = kunits[n]
                k0, kn = KC[j]
                act.wait_ge(p_k, n + 1)
                for h in range(2):
                    act.activation(K1[0:DH, 2 * p + h, k0:k0 + kn], banks[4 + n % 2][DH * h:DH * h + DH, 0:kn],
                                   ACT.Copy).then_inc(a_khi, 1)

            def value(n):
                rows_n = P if n < KT - 1 else LAST
                act.wait_ge(p_v, n + 1)
                act.activation(V[0:rows_n, n, :], banks[6 + n % 2][0:rows_n, :], ACT.Copy).then_inc(a_v, 1)

            def transposed(t):
                act.wait_ge(p_t, t + 1)
                if t < QT:
                    act.activation(x1T[:, :, t * P:(t + 1) * P], banks[t % 2][:, 0:D].rearrange("p (k n) -> p k n", k=DK),
                                   ACT.Copy).then_inc(a_t, 1)
                    return
                if t >= QT + 2:
                    act.wait_ge(d_x1T[t % 2], 16 * ((t - QT) // 2))
                act.activation(x1Tb[:, t % 2], banks[t % 2][:, 0:D].rearrange("p (k n) -> p k n", k=DK),
                               ACT.Copy).then_inc(a_t, 1)
                act.wait_ge(a_t, t + 1)
                act.dma_start(io["x1T"].rearrange("(k p) n -> p k n", p=P)[:, :, t * P:(t + 1) * P],
                              x1Tb[:, t % 2]).then_inc(d_x1T[t % 2], 16)

            def norm_c(t):
                if t % 4 == 0:
                    act.wait_ge(v_shift2, t // 4 + 1)
                act.activation(z[:, t], z[:, t], ACT.Identity, bias=shift[:, t:t + 1], scale=rstd[:, 1, t:t + 1]
                               ).then_inc(a_x1, 1)

            def query_high(_):
                act.wait_ge(p_q0, 1)
                for h in range(2):
                    act.activation(Q1[0:DH, h], banks[2][DH * h:DH * h + DH, :], ACT.Copy).then_inc(a_q0, 1)

            slots(key=key_high, val=value, norm_c=norm_c, tr=transposed, query=query_high)
            act.wait_ge(d_x1T[0], 16 * (TILES - QT) // 2)
            act.wait_ge(d_x1T[1], 16 * (TILES - QT) // 2)

        @block.vector
        def _(dve):
            links = [0]

            def link(ins):
                links[0] += 1
                ins.then_inc(v_link, 1)
                dve.wait_ge(v_link, links[0])

            dve.wait_ge(d_win, 32)
            dve.wait_ge(a_exp, 1)
            dve.tensor_tensor(bB[:], cols[:, 0], cols[:, 2], ALU.mult).then_inc(prep, 1)
            dve.tensor_scalar(decay[:, 1], decay[:, 0], 1.0, None, ALU.add).then_inc(prep, 1)
            dve.wait_ge(prep, 2)
            dve.reciprocal(decay[:, 2], decay[:, 1]).then_inc(prep, 1)
            dve.wait_ge(d_rows, 80)
            for k in range(DK):
                dve.tensor_scalar(w_out[:, k], w_out[:, k], cols[:, 3, k:k + 1], None, ALU.mult).then_inc(prep, 1)
            dve.wait_ge(prep, 3)
            for n in range(8):
                c, e = n // 2, n % 2
                dve.wait_ge(a_u, n + 1)
                if c:
                    dve.wait_ge(v_scan, n - 1)
                u = state[:, e, c * 512:(c + 1) * 512]
                dve.tensor_tensor_scan(u, decay[:, 2, e:e + 1].to_broadcast([P, 512]), u,
                                       state[:, e, c * 512 - 1:c * 512] if c else 0.0,
                                       ALU.mult, ALU.add).then_inc(v_scan, 1)

            def key_low(n):
                p, j = kunits[n]
                k0, kn = KC[j]
                dve.wait_ge(a_khi, 2 * (n + 1))
                for h in range(2):
                    dve.tensor_tensor(K2[0:DH, 2 * p + h, k0:k0 + kn], banks[4 + n % 2][DH * h:DH * h + DH, 0:kn],
                                      K1[0:DH, 2 * p + h, k0:k0 + kn].bitcast(F32), ALU.subtract).then_inc(v_klo, 1)

            def norm_a(t):
                if t == 0:
                    dve.wait_ge(d_rows, 80)
                dve.wait_ge(p_out, t + 1)
                dve.tensor_tensor(z[:, t], banks[2 + t % 2][:, 0:D], rows[:, 0, :], ALU.add).then_inc(v_z, 1)
                dve.wait_ge(v_z, t + 1)
                link(dve.bn_stats(stats[:, t % 4, 0, :], z[:, t]))
                dve.bn_aggr(mv[:, 0, t], stats[:, t % 4, 0, :]).then_inc(v_mv1, 1)

            def norm_b(t):
                if t % 4 == 0:
                    dve.wait_ge(g_rstd1, t // 4 + 1)
                dve.wait_ge(g_xb, t + 1)
                link(dve.scalar_tensor_tensor(z[:, t], z[:, t], mv[:, 0, t, 0:1], rows[:, 1, :], ALU.subtract, ALU.mult))
                dve.scalar_tensor_tensor(z[:, t], z[:, t], rstd[:, 0, t:t + 1], xring[:, (t // 4) % 2, t % 4],
                                         ALU.mult, ALU.add).then_inc(v_b, 1)
                dve.wait_ge(v_b, t + 1)
                link(dve.bn_stats(stats[:, t % 4, 1, :], z[:, t]))
                dve.bn_aggr(mv[:, 1, t], stats[:, t % 4, 1, :]).then_inc(v_mv2, 1)

            def shifts(g):
                dve.wait_ge(g_rstd2, g + 1)
                tiles = slice(4 * g, 4 * g + 4)
                dve.scalar_tensor_tensor(shift[:, tiles], mv[:, 1, tiles, 0], -1.0, rstd[:, 1, tiles], ALU.mult, ALU.mult
                                         ).then_inc(v_shift2, 1)

            def query_low(_):
                for h in range(2):
                    dve.wait_ge(a_q0, h + 1)
                    dve.tensor_tensor(Q1[DH:P, h], banks[2][DH * h:DH * h + DH, :], Q1[0:DH, h].bitcast(F32), ALU.subtract
                                      ).then_inc(v_q0, 1)

            def piece_maximum(n):
                dve.wait_ge(p_mx0, n + 1)
                u, j = n // len(KC), n % len(KC)
                dve.tensor_reduce(mxp[:, 0, u, j:j + 1], banks[2 + (n + 1) % 2][:, 0:KC[j][1]], AX.X, ALU.max
                                  ).then_inc(v_mx0, 1)

            slots(out=norm_a, low=key_low, norm_b=norm_b, shifts=shifts, query=query_low, piece=piece_maximum)
            dve.wait_ge(v_mx0, PIECES)
            dve.tensor_reduce(nm[:, 0], mxp[:, 0], AX.X, ALU.max, negate=True).then_inc(v_nm0, 1)
            dve.wait_ge(v_nm0, 1)

        @block.tensor
        def _(pe):
            for n in range(8):
                c, e = n // 2, n % 2
                if n == 0:
                    pe.wait_ge(d_win, 32)
                pe.wait_ge(d_x[c], 16)
                if n >= 2:
                    pe.wait_ge(a_u, n - 1)
                for k in range(DK):
                    mm = pe.matmul(banks[n % 2][:], w_in[:, k, e * P:(e + 1) * P], xT[:, k, c * 512:(c + 1) * 512],
                                   start=(k == 0), stop=(k == DK - 1))
                mm.then_inc(p_in, 1)
            pe.wait_ge(prep, 5)
            pe.wait_ge(a_u, 8)

            def out_proj(t):
                pe.wait_ge(v_scan, 2 * (t // 4 + 1))
                if t >= 2:
                    pe.wait_ge(v_z, t - 1)
                for k in range(DK):
                    mm = pe.matmul(banks[2 + t % 2][:, 0:D], state[:, k, t * P:(t + 1) * P], w_out[:, k, :],
                                   start=(k == 0), stop=(k == DK - 1))
                mm.then_inc(p_out, 1)

            def key(n):
                p, j = kunits[n]
                k0, kn = KC[j]
                if n == 0:
                    pe.wait_ge(d_ctx, 32)
                if n >= 2:
                    pe.wait_ge(v_klo, 2 * (n - 1))
                for k in range(DK):
                    mm = pe.matmul(banks[4 + n % 2][:, 0:kn], wk[:, k, p * P:(p + 1) * P], ctxT[:, k, k0:k0 + kn],
                                   start=(k == 0), stop=(k == DK - 1))
                mm.then_inc(p_k, 1)

            def val(n):
                rows_n = P if n < KT - 1 else LAST
                if n == 0:
                    pe.wait_ge(d_wv, 16)
                if n >= 2:
                    pe.wait_ge(a_v, n - 1)
                for k in range(DK):
                    mm = pe.matmul(banks[6 + n % 2][0:rows_n, :], ctxT[:, k, n * P:n * P + rows_n], wv[:, k, :],
                                   start=(k == 0), stop=(k == DK - 1))
                mm.then_inc(p_v, 1)

            def transpose(t):
                if t == 0:
                    pe.wait_ge(d_ident, 32)
                pe.wait_ge(a_x1, t + 1)
                if t >= 2:
                    pe.wait_ge(a_t, t - 1)
                for k in range(DK):
                    mm = pe.transpose(banks[t % 2][:, k * P:(k + 1) * P], z[:, t, k * P:(k + 1) * P], ident[:])
                mm.then_inc(p_t, 1)

            def query(_):
                pe.wait_ge(a_t, QT)
                pe.wait_ge(v_z, TILES)
                for k in range(DK):
                    mm = pe.matmul(banks[2][:], wq0[:, k, :], x1T[:, k, :], start=(k == 0), stop=(k == DK - 1))
                mm.then_inc(p_q0, 1)

            def piece(n):
                u, j = n // len(KC), n % len(KC)
                h, i = u // QT, u % QT
                k0, kn = KC[j]
                if n == 0:
                    pe.wait_ge(v_q0, 2)
                    pe.wait_ge(d_dup0, 32)
                if n >= 2:
                    pe.wait_ge(v_mx0, n - 1)
                pe.matmul(banks[2 + (n + 1) % 2][:, 0:kn], Q1[:, h, i * P:(i + 1) * P], K1[:, h, k0:k0 + kn],
                          start=True, stop=True).then_inc(p_mx0, 1)

            slots(out=out_proj, key=key, val=val, tr=transpose, query=query, piece=piece)


STEP_MX = 1 + 2 * QT * len(KC)
CHUNK_MISC = 2 * PAIRS + 2
G_ADDS = KT - 1
DIVS = 8
LAST_V = (3, 5, 7, 9, 11, 12)
SEED = 1
DIVIDE_AFTER = (2, 4, 6, 9, 12, 15, 18, 21)
OUTPUT_AT = (9, 11)
RESIDUAL_AFTER = [3 * (t - 1) for t in OUTPUT_AT]
RING = 4


def attention(nc, io, mem):
    K1, K2, V, ident = mem["K1"], mem["K2"], mem["V"], mem["ident"]
    x1T, mxp, nm = mem["x1T"], mem["mxp"], mem["nm"]
    with ExitStack() as ctx:
        def sb(name, shape, dt=F32):
            return ctx.enter_context(nc.sbuf_tensor(name, shape, dt))

        def sem(name):
            return ctx.enter_context(nc.semaphore(name))

        wq = sb("wq", [P, DK, HID])
        wo = sb("wo", [P, PAIRS, D])
        x1 = mem["x1"]
        Q1 = [mem["Q1"][0], sb("Q1b", [P, 2, QC], F32R)]
        Q2 = sb("Q2", [P, 2, 2, QC], F32R)
        probs = sb("probs", [P, RING, 2 * QC])
        accG = sb("accG", [P, 2 * QC])
        accL = sb("accL", [P, 2 * QC])
        ones = sb("ones", [P, DH])
        o_raw = sb("o_raw", [P, QC])
        rsum = sb("rsum", [P, QC])
        oT = sb("oT", [P, PAIRS, QC])
        mrow = sb("mrow", [2 * QT, 2, P], F32R)
        st6 = sb("st6", [P, QT, 6])
        mv3 = sb("mv3", [P, QT, 2])
        ve3 = sb("ve3", [P, QT])
        rstd3 = sb("rstd3", [P, QT])
        eps3 = sb("eps3", [P, QT])
        mhalf3 = sb("mhalf3", [P, QT])
        st = [ctx.enter_context(nc.psum_tensor(f"st{i}", [P, 2 * QC], F32)) for i in range(2)]
        av = ctx.enter_context(nc.psum_tensor("av", [P, QC], F32))
        misc = ctx.enter_context(nc.psum_tensor("misc", [P, QC], F32))
        mx = [ctx.enter_context(nc.psum_tensor(f"mx{i}", [P, QC], F32)) for i in range(2)]

        d_wq = sem("d_wq")
        d_wo, d_x1Tc, d_x1c, d_x2 = sem("d_wo"), sem("d_x1Tc"), sem("d_x1c"), sem("d_x2")
        d_q2 = [sem(f"d_q2_{i}") for i in range(2)]
        d_m = [sem(f"d_m_{i}") for i in range(2)]
        p_q, a_hi, v_lo = sem("p_q"), sem("a_hi"), sem("v_lo")
        p_mx, v_mx, v_nm, p_mT, v_mT = sem("p_mx"), sem("v_mx"), sem("v_nm"), sem("p_mT"), sem("v_mT")
        p_qk = sem("p_qk")
        a_probs = sem("a_probs")
        p_pv = sem("p_pv")
        v_add, g_add = sem("v_add"), sem("g_add")
        a_av, p_sum, v_misc, v_o = sem("a_av"), sem("p_sum"), sem("v_misc"), sem("v_o")
        p_wo, v_r, v_mv3, g_rs3, v_x2 = sem("p_wo"), sem("v_r"), sem("v_mv3"), sem("g_rs3"), sem("v_x2")
        v_rsum = sem("v_rsum")
        v_stats = sem("v_stats")
        s_free = sem("s_free")
        v_link3, g_link3, g_ones = sem("v_link3"), sem("g_link3"), sem("g_ones")

        def rows_of(t):
            return P if t < KT - 1 else LAST

        def max_use(c, p):
            return c * CHUNK_MISC + (2 * p + 2 if p else 0)

        def sum_use(c, p):
            return c * CHUNK_MISC + (2 * p + 5 if p < PAIRS - 1 else CHUNK_MISC + 1)

        def out_use(c, a):
            return (c + 1) * CHUNK_MISC + 2 + a

        LAST_SUM_USE = CHUNKS * CHUNK_MISC

        def parity(p):
            return (p + 1) % 2

        block = ctx.enter_context(nc.Block())

        @block.sync
        def _(sp):
            def queries(F, par, n):
                sp.wait_ge(a_hi, (F + 1) * 2)
                sp.sem_inc(s_free, 1)
                if n:
                    sp.wait_ge(p_qk, SEED + (F - 1) * KT)
                sp.sem_inc(s_free, 1)
                sp.dma_start(Q2[0:DH, par].bitcast(F32), Q1[par][0:DH].bitcast(F32)).then_inc(d_q2[par], 16)

            def maxima(F, par):
                sp.wait_ge(v_mT, F + 1)
                sp.sem_inc(s_free, 1)
                for h in range(2):
                    sp.dma_start(Q2[DH:DH + 1, par, h, :].bitcast(F32), mrow[QT * h:QT * h + QT, par, :].bitcast(F32)
                                 ).then_inc(d_m[par], 16)

            def store(c):
                sp.wait_ge(v_x2, (c + 1) * QT)
                sp.sem_inc(s_free, 1)
                sp.dma_start(io["x2"].rearrange("(t p) n -> p t n", p=P)[:, bass.ds(c * QT, QT), :], x1[:]).then_inc(d_x2, 16)
                sp.sem_inc(s_free, 1)

            def chunk(c, first, last):
                for p in range(PAIRS):
                    F = c * PAIRS + (p + 1)
                    maxima(c * PAIRS + p, p % 2)
                    if not (last and p == PAIRS - 1):
                        queries(F, parity(p), True)
                    if p == PAIRS - 2 and not last:
                        sp.wait_ge(p_q, (c + 1) * PAIRS)
                        sp.sem_inc(s_free, 1)
                        sp.sem_inc(s_free, 1)
                        sp.dma_start(x1T[:], io["x1T"].rearrange("(k p) n -> p k n", p=P)[:, :, bass.ds((c + 1) * QC, QC)]
                                     ).then_inc(d_x1Tc, 16)
                    if p == 1 and not first:
                        store(c - 1)
                        sp.wait_ge(d_x2, c * 16)
                        sp.sem_inc(s_free, 1)
                        sp.dma_start(x1[:], io["x1b"].rearrange("(t p) n -> p t n", p=P)[:, bass.ds(c * QT, QT), :]
                                     ).then_inc(d_x1c, 16)

            sp.dma_start(wq[:], io["wq"].rearrange("(k p) n -> p k n", p=P)).then_inc(d_wq, 16)
            queries(0, 0, False)
            sp.dma_start(wo[:], io["wo"].rearrange("(k p) n -> p k n", p=P)).then_inc(d_wo, 16)
            sp.dma_start(x1[:], io["x1b"].rearrange("(t p) n -> p t n", p=P)[:, 0:QT, :]).then_inc(d_x1c, 16)
            chunk(0, True, False)
            with sp.Fori(1, CHUNKS - 1) as c:
                chunk(c, False, False)
            chunk(CHUNKS - 1, False, True)
            sp.wait_ge(p_qk, SEED + (CHUNKS * PAIRS - 1) * KT)
            for c in range(CHUNKS - 1):
                sp.dma_start(mem["x2"][:, c * QT:(c + 1) * QT], io["x2"].rearrange("(t p) n -> p t n", p=P)[:, c * QT:(c + 1) * QT, :]
                             ).then_inc(mem["d_x2i"][c], 16)
            for i, name in enumerate(("s_gateT", "s_upT")):
                sp.dma_start(mem["uncut"][:, i], io[name].rearrange("(k p) n -> p k n", p=P)).then_inc(mem["d_gu"], 16)

        @block.gpsimd
        def _(pool):
            pool.sem_inc(g_add, G_ADDS)
            pool.memset(ones[:], 1.0).then_inc(g_ones, 1)
            pool.wait_ge(g_ones, 1)
            pool.memset(mhalf3[:], -0.5).then_inc(g_ones, 1)
            pool.wait_ge(g_ones, 2)
            pool.memset(eps3[:], EPS).then_inc(g_ones, 1)
            pool.wait_ge(g_ones, 3)

            def inverse(c):
                pool.wait_ge(v_mv3, (c + 1) * QT)
                pool.tensor_tensor(ve3[:], mv3[:, :, 1], eps3[:], ALU.add).then_inc(g_link3, 1)
                pool.wait_ge(g_link3, c + 1)
                pool.tensor_tensor(rstd3[:], ve3[:], mhalf3[:], ALU.pow).then_inc(g_rs3, 1)
                pool.wait_ge(g_rs3, c + 1)

            def chunk(c, first, last):
                for p in range(PAIRS):
                    shared = LAST_V if last and p == PAIRS - 1 else ()
                    for n, t in enumerate(t for t in range(1, KT) if t not in shared):
                        if p == 0 and t == KT - 1 and not first:
                            inverse(c - 1)
                        r = rows_of(t)
                        pool.wait_ge(a_probs, (c * PAIRS + p) * KT + (2 + t + 1))
                        if n == 0:
                            pool.wait_ge(p_sum, SEED + c * PAIRS + p)
                            so_far = probs[:, (p * KT) % RING]
                        else:
                            so_far = accG
                            pool.wait_ge(g_add, (c * PAIRS + p) * G_ADDS + (G_ADDS + n))
                        pool.tensor_tensor(accG[0:r], so_far[0:r], probs[0:r, (p * KT + t) % RING], ALU.add).then_inc(g_add, 1)

            chunk(0, True, False)
            with pool.Fori(1, CHUNKS - 1) as c:
                chunk(c, False, False)
            chunk(CHUNKS - 1, False, True)

        @block.scalar
        def _(act):
            act.sem_inc(a_probs, 2)
            act.sem_inc(a_av, SEED)

            def q_high(F, par, h, n):
                act.wait_ge(p_q, F + 1)
                if n and h == 0:
                    act.wait_ge(p_qk, SEED + (F - 1) * KT)
                act.activation(Q1[par][0:DH, h], mx[par][DH * h:DH * h + DH, :], ACT.Copy).then_inc(a_hi, 1)

            def exp(c, p, t):
                g = p * KT + t
                s, r = g % RING, rows_of(t)
                last_step = isinstance(c, int) and c * PAIRS + p == CHUNKS * PAIRS - 1
                act.wait_ge(p_qk, SEED + c * PAIRS * KT + (g + 1))
                act.wait_ge(p_pv, c * PAIRS * KT + (g + 1))
                old = (t - RING) % KT
                if last_step and t >= RING:
                    if old in LAST_V:
                        act.wait_ge(v_add, LAST_V.index(old) + 1)
                    else:
                        alone = [k for k in range(1, KT) if k not in LAST_V]
                        act.wait_ge(g_add, CHUNKS * PAIRS * G_ADDS + alone.index(max(old, 1)) + 1)
                else:
                    since = p + (1 if t >= RING else 0)
                    act.wait_ge(g_add, c * PAIRS * G_ADDS + (since * G_ADDS + max(old, 1)))
                act.activation(probs[0:r, s], st[g % 2][0:r, :], ACT.Exp, scale=DH ** -0.5).then_inc(a_probs, 1)

            def copy_av(c, p):
                act.wait_ge(p_pv, (c * PAIRS + (p + 1)) * KT + RING)
                act.wait_ge(v_o, SEED + (c * PAIRS + p) * DIVS)
                act.activation(o_raw[:], av[:], ACT.Copy).then_inc(a_av, 1)

            def chunk(c, first, last):
                for p in range(PAIRS):
                    ahead = not (last and p == PAIRS - 1)
                    F = c * PAIRS + (p + 1)
                    if ahead:
                        q_high(F, parity(p), 0, True)
                        q_high(F, parity(p), 1, True)
                    if p > 0:
                        copy_av(c, p - 1)
                    elif not first:
                        copy_av(c - 1, PAIRS - 1)
                    for t in range(KT):
                        exp(c, p, t)

            act.sem_inc(a_hi, 2)
            chunk(0, True, False)
            with act.Fori(1, CHUNKS - 1) as c:
                chunk(c, False, False)
            chunk(CHUNKS - 1, False, True)
            copy_av(CHUNKS - 1, PAIRS - 1)

        @block.vector
        def _(dve):
            def q_low(F, par):
                for h in range(2):
                    dve.wait_ge(a_hi, F * 2 + (h + 1))
                    ins = dve.tensor_tensor(Q1[par][DH:P, h], mx[par][DH * h:DH * h + DH, :],
                                            Q1[par][0:DH, h].bitcast(F32), ALU.subtract).then_inc(v_lo, 1)
                dve.wait_ge(v_lo, F * 2 + 2)
                dve.sem_inc(v_mx, 1)

            def piece_maxima(F, par, between):
                for u in range(2 * QT):
                    for j, (k0, kn) in enumerate(KC):
                        n = len(KC) * u + j + 1
                        dve.wait_ge(p_mx, F * (STEP_MX - 1) + n)
                        dve.tensor_reduce(mxp[:, par, u, j:j + 1], mx[(par + n) % 2][:, 0:kn], AX.X, ALU.max
                                          ).then_inc(v_mx, 1)
                        if n in between:
                            between[n]()
                dve.wait_ge(v_mx, F * STEP_MX + STEP_MX)
                dve.tensor_reduce(nm[:, par], mxp[:, par], AX.X, ALU.max, negate=True).then_inc(v_nm, 1)

            def max_row(F, par):
                dve.wait_ge(p_mT, F + 1)
                dve.tensor_copy(mrow[:, par], misc[0:2 * QT, 0:P]).then_inc(v_mT, 1)
                dve.wait_ge(v_mT, F + 1)
                dve.sem_inc(v_misc, 1)

            def divide(c, p, i):
                S0 = c * PAIRS + p
                if i == 0:
                    dve.wait_ge(p_sum, SEED + S0 + 1)
                    dve.wait_ge(v_o, SEED + S0 * DIVS)
                cols = slice(i * QC // DIVS, (i + 1) * QC // DIVS)
                dve.reciprocal(rsum[:, cols], misc[:, cols]).then_inc(v_rsum, 1)
                dve.wait_ge(v_rsum, S0 * DIVS + (i + 1))
                if i == DIVS - 1:
                    dve.sem_inc(v_misc, 1)
                if i == 0:
                    dve.wait_ge(a_av, SEED + S0 + 1)
                    if p == 0:
                        dve.wait_ge(p_wo, SEED + c * QT)
                dve.tensor_tensor(oT[:, p, cols], o_raw[:, cols], rsum[:, cols], ALU.mult).then_inc(v_o, 1)

            def residual(c, i, bank):
                dve.wait_ge(p_wo, SEED + c * QT + (i + 2 - i % 2))
                if i == 0:
                    dve.wait_ge(d_x1c, (c + 1) * 16)
                dve.tensor_tensor(x1[:, i], bank[:, (i % 2) * D:(i % 2 + 1) * D], x1[:, i], ALU.add).then_inc(v_r, 1)
                dve.wait_ge(v_r, c * QT + (i + 1))
                if isinstance(c, int) and c == CHUNKS - 1:
                    return
                if i % 2:
                    dve.sem_inc(v_misc, 1)
                dve.bn_stats(st6[:, i], x1[:, i]).then_inc(v_link3, 1)
                dve.wait_ge(v_link3, c * QT + (i + 1))
                dve.sem_inc(v_stats, 1)
                dve.bn_aggr(mv3[:, i], st6[:, i]).then_inc(v_mv3, 1)

            def norm(c):
                dve.wait_ge(g_rs3, c + 1)
                for i in range(QT):
                    dve.tensor_scalar(x1[:, i], x1[:, i], mv3[:, i, 0:1], rstd3[:, i:i + 1], ALU.subtract, ALU.mult
                                      ).then_inc(v_x2, 1)

            def chunk(c, first, last):
                for p in range(PAIRS):
                    ahead = not (last and p == PAIRS - 1)
                    F = c * PAIRS + (p + 1)
                    between = {}
                    if p or not first:
                        before = (c, p - 1) if p else (c - 1, PAIRS - 1)
                        for i, n in enumerate(DIVIDE_AFTER):
                            between[n] = lambda i=i: divide(*before, i)
                    if p == 1 and not first:
                        between[1] = lambda: norm(c - 1)
                    if p == 0 and not first:
                        for i, n in enumerate(RESIDUAL_AFTER):
                            between[n] = lambda i=i: (residual(c - 1, 2 * i, misc), residual(c - 1, 2 * i + 1, misc))
                    max_row(c * PAIRS + p, p % 2)
                    if p == 0 and first:
                        dve.sem_inc(v_misc, 3)
                    if ahead:
                        q_low(F, parity(p))
                        piece_maxima(F, parity(p), between)
                    else:
                        for n in sorted(between):
                            between[n]()
                        for n, t in enumerate(LAST_V):
                            r = rows_of(t)
                            dve.wait_ge(a_probs, (c * PAIRS + p) * KT + (2 + t + 1))
                            place = probs[0:r, (p * KT + t) % RING]
                            if n == 0:
                                dve.tensor_copy(accL[:], place).then_inc(v_add, 1)
                            else:
                                dve.wait_ge(v_add, n)
                                dve.tensor_tensor(accL[0:r], accL[0:r], place, ALU.add).then_inc(v_add, 1)

            dve.sem_inc(v_o, SEED)
            dve.sem_inc(v_misc, SEED)
            dve.sem_inc(v_lo, 2)
            dve.sem_inc(v_mx, STEP_MX)
            dve.sem_inc(v_nm, 1)
            chunk(0, True, False)
            with dve.Fori(1, CHUNKS - 1) as c:
                chunk(c, False, False)
            chunk(CHUNKS - 1, False, True)
            for i in range(DIVS):
                divide(CHUNKS - 1, PAIRS - 1, i)
            for i in range(QT):
                residual(CHUNKS - 1, i, mx[i // 2])

        @block.tensor
        def _(pe):
            pe.sem_inc(p_pv, RING)
            for begun in (p_qk, p_sum, p_wo):
                pe.sem_inc(begun, SEED)
            pe.sem_inc(p_q, 1)
            pe.sem_inc(p_mx, STEP_MX - 1)

            def q_proj(pair, par):
                for k in range(DK):
                    mm = pe.matmul(mx[par][:], wq[:, k, pair * P:(pair + 1) * P], x1T[:, k, :],
                                   start=(k == 0), stop=(k == DK - 1))
                mm.then_inc(p_q, 1)

            def max_scores(F, pair, par, use, n):
                u, j = (n - 1) // len(KC), (n - 1) % len(KC)
                h, i = u // QT, u % QT
                k0, kn = KC[j]
                if n == 1:
                    pe.wait_ge(v_lo, F * 2 + 2)
                pe.wait_ge(v_mx, use + (n - 1))
                pe.matmul(mx[(par + n) % 2][:, 0:kn], Q1[par][:, h, i * P:(i + 1) * P], K1[:, 2 * pair + h, k0:k0 + kn],
                          start=True, stop=True).then_inc(p_mx, 1)

            def max_transpose(c, p):
                pe.wait_ge(v_nm, c * PAIRS + (p + 1))
                pe.wait_ge(v_misc, SEED + max_use(c, p))
                pe.transpose(misc[0:2 * QT, 0:P], nm[:, p % 2], ident[:]).then_inc(p_mT, 1)

            def scores_1(c, p, t):
                g, r = p * KT + t, rows_of(t)
                pe.wait_ge(a_probs, c * PAIRS * KT + (g + 1))
                for h in range(2):
                    pe.matmul(st[g % 2][0:r, h * QC:(h + 1) * QC], K1[:, 2 * p + h, t * P:t * P + r], Q1[p % 2][:, h],
                              start=True, stop=False)

            def scores_2(c, p, t):
                g, r = p * KT + t, rows_of(t)
                par = p % 2
                if t == 0:
                    pe.wait_ge(d_q2[par], (c * 2 + (p // 2 + 1)) * 16)
                    pe.wait_ge(d_m[par], (c * 2 + (p // 2 + 1)) * 32)
                for h in range(2):
                    mm = pe.matmul(st[g % 2][0:r, h * QC:(h + 1) * QC], K2[0:DH + 1, 2 * p + h, t * P:t * P + r],
                                   Q2[0:DH + 1, par, h], start=False, stop=True)
                mm.then_inc(p_qk, 1)

            def values(c, p, t):
                g, r = p * KT + t, rows_of(t)
                pe.wait_ge(a_probs, c * PAIRS * KT + (g + 3))
                if t == 0:
                    pe.wait_ge(a_av, SEED + c * PAIRS + p)
                for h in range(2):
                    mm = pe.matmul(av[h * DH:(h + 1) * DH, :], V[0:r, t, (2 * p + h) * DH:(2 * p + h + 1) * DH],
                                   probs[0:r, g % RING, h * QC:(h + 1) * QC], start=(t == 0), stop=(t == KT - 1))
                mm.then_inc(p_pv, 1)

            def sums(c, p, use, shared=False):
                S0 = c * PAIRS + p
                parts = [accG]
                if shared:
                    parts.append(accL)
                    pe.wait_ge(v_add, len(LAST_V))
                    pe.wait_ge(g_add, CHUNKS * PAIRS * G_ADDS + G_ADDS - len(LAST_V))
                else:
                    pe.wait_ge(g_add, (S0 + 2) * G_ADDS)
                pe.wait_ge(v_misc, SEED + use)
                for acc in parts:
                    for h in range(2):
                        mm = pe.matmul(misc[h * DH:(h + 1) * DH, :], ones[:], acc[:, h * QC:(h + 1) * QC],
                                       start=acc is parts[0], stop=acc is parts[-1])
                mm.then_inc(p_sum, 1)

            def output(c, a):
                pe.wait_ge(d_wo, 16)
                pe.wait_ge(v_misc, SEED + out_use(c, a))
                pe.wait_ge(v_o, SEED + (c * PAIRS + PAIRS) * DIVS)
                for i in (2 * a, 2 * a + 1):
                    for p in range(PAIRS):
                        mm = pe.matmul(misc[:, (i % 2) * D:(i % 2 + 1) * D], oT[:, p, i * P:(i + 1) * P], wo[:, p, :],
                                       start=(p == 0), stop=(p == PAIRS - 1))
                    mm.then_inc(p_wo, 1)

            def last_output(end):
                steps = CHUNKS * PAIRS
                if not end:
                    pe.wait_ge(v_o, SEED + (steps - 1) * DIVS)
                    pe.wait_ge(v_mx, steps * STEP_MX)
                for i in range(QT):
                    if end:
                        pe.wait_ge(v_o, SEED + (steps - 1) * DIVS + (i + 1) * DIVS // QT)
                    for p in ((PAIRS - 1,) if end else range(PAIRS - 1)):
                        mm = pe.matmul(mx[i // 2][:, (i % 2) * D:(i % 2 + 1) * D], oT[:, p, i * P:(i + 1) * P], wo[:, p, :],
                                       start=(p == 0 and i % 2 == 0), stop=end, skip_group_check=True)
                    if end:
                        mm.then_inc(p_wo, 1)

            def chunk(c, first, last):
                for p in range(PAIRS):
                    ahead = not (last and p == PAIRS - 1)
                    F, pair, par = c * PAIRS + (p + 1), (p + 1) % PAIRS, parity(p)
                    before = (c, p - 1) if p else None if first else (c - 1, PAIRS - 1)
                    use = F * STEP_MX
                    done = [0]

                    def next_piece():
                        done[0] += 1
                        if ahead and done[0] < STEP_MX:
                            max_scores(F, pair, par, use, done[0])

                    scores_1(c, p, 0)
                    max_transpose(c, p)
                    scores_1(c, p, 1)
                    if ahead:
                        pe.wait_ge(v_mx, use - 1)
                        if first and p == 0:
                            pe.wait_ge(d_wq, 16)
                            pe.wait_ge(mem["d_dup"], (HEADS - 2) * 16)
                        if pair == 0:
                            pe.wait_ge(d_x1Tc, (c + 1) * 16)
                        q_proj(pair, par)
                    if before:
                        values(*before, KT - 1)
                    scores_2(c, p, 0)
                    scores_2(c, p, 1)
                    if before:
                        sums(*before, sum_use(*before))
                    values(c, p, 0)
                    for t in range(2, KT):
                        scores_1(c, p, t)
                        next_piece()
                        scores_2(c, p, t)
                        next_piece()
                        values(c, p, t - 1)
                        next_piece()
                        if p == 0 and not first and t in OUTPUT_AT:
                            output(c - 1, OUTPUT_AT.index(t))

            pe.wait_ge(g_ones, 1)
            chunk(0, True, False)
            with pe.Fori(1, CHUNKS - 1) as c:
                chunk(c, False, False)
            chunk(CHUNKS - 1, False, True)
            values(CHUNKS - 1, PAIRS - 1, KT - 1)
            last_output(False)
            sums(CHUNKS - 1, PAIRS - 1, LAST_SUM_USE, shared=True)
            last_output(True)


EXPERTS, FE = 16, 256
SF = 1024
FK = SF // P
ETILES = TILES + EXPERTS - 1
GRID_REV, GRID_THR, GRID_J, GRID_ID = 0, EXPERTS, EXPERTS + TILES, EXPERTS + TILES + ETILES
GRID = GRID_ID + TILES
ROW = D + 1
ZT = 4


def route_and_share(nc, io, mem):
    x2, pos, te, ident = mem["x2"], mem["pos"], mem["te"], mem["ident"]
    w_gate_up, w_down = mem["w_gate_up"], mem["w_down"]
    with ExitStack() as ctx:
        def sb(name, shape, dt=F32):
            return ctx.enter_context(nc.sbuf_tensor(name, shape, dt))

        def sem(name):
            return ctx.enter_context(nc.semaphore(name))

        wgu = [[sb(f"w{n}_{part}", [P, DK, SF], F32R) for part in ("high", "low")] for n in ("gate", "up")]
        uncut = [mem["uncut"][:, i] for i in range(2)]
        x2s = sb("x2s", [P, TILES // 2, ROW])
        x2T = [sb("x2T", [P, DK, S], F32R), mem["x2T_low"]]
        wr = sb("wr", [P, DK, EXPERTS])
        wr_parts = [sb(f"wr_{part}", [P, DK, EXPERTS], F32R) for part in ("high", "low")]
        wd = sb("wd", [P, FK, D])
        upper = sb("upper", [P, P])
        allone = sb("allone", [P, P])
        grid = sb("grid", [P, GRID])
        zero = sb("zero", [P, ROW])
        hT = sb("hT", [P, FK, 512])
        lg = sb("lg", [P, TILES, EXPERTS])
        top = sb("top", [P, TILES])
        esc = sb("esc", [P, 3, TILES])
        work = sb("work", [P, 2, TILES, EXPERTS])
        oneh = sb("oneh", [P, TILES, EXPERTS])
        rev = sb("rev", [P, TILES])
        carry = sb("carry", [P, TILES + 1, EXPERTS])
        nt = sb("nt", [P, EXPERTS])
        incl = sb("incl", [P, EXPERTS])
        off = sb("off", [P, 2, EXPERTS])
        posf = sb("posf", [P, TILES])
        cmpj = sb("cmpj", [P, ETILES, EXPERTS])
        tef = sb("tef", [P, 2, ETILES])
        onesr = sb("onesr", [P, EXPERTS])
        stl = sb("stl", [P, QT, 6])
        mvl = sb("mvl", [P, QT, 2])
        rsl = sb("rsl", [P, 2, QT])
        constl = sb("constl", [P, 2, QT])
        bt = [ctx.enter_context(nc.psum_tensor(f"bt{i}", [P, 512], F32)) for i in range(2)]
        bg = [ctx.enter_context(nc.psum_tensor(f"bg{i}", [P, 512], F32)) for i in range(2)]
        bu = [ctx.enter_context(nc.psum_tensor(f"bu{i}", [P, 512], F32)) for i in range(2)]
        br = ctx.enter_context(nc.psum_tensor("br", [P, 512], F32))
        bp = ctx.enter_context(nc.psum_tensor("bp", [P, 512], F32))

        d_x2i, d_gu = mem["d_x2i"], mem["d_gu"]
        a_wr, v_wr = sem("a_wr"), sem("v_wr")
        v_mvl, g_vel, g_rsl, v_last = sem("v_mvl"), sem("g_vel"), sem("g_rsl"), sem("v_last")
        d_r, d_wd, d_zero, d_scatter = sem("d_r"), sem("d_wd"), sem("d_zero"), sem("d_scatter")
        g_zero = sem("g_zero")
        p_tr, a_tr = sem("p_tr"), sem("a_tr")
        p_lgT, a_lgT = sem("p_lgT"), sem("a_lgT")
        v_route = sem("v_route")
        a_sc, v_oh, p_px, v_pos, v_score, g_x2s = (sem("a_sc"), sem("v_oh"), sem("p_px"), sem("v_pos"),
                                                   sem("v_score"), sem("g_x2s"))
        a_whi, v_wlo, v_xlo = sem("a_whi"), sem("v_wlo"), sem("v_xlo")
        p_gu, a_silu, v_h, p_dn, v_base = sem("p_gu"), sem("a_silu"), sem("v_h"), sem("p_dn"), sem("v_base")

        LOGITS_AT = {0: 0, 2: 1, 4: 2, 6: 3}
        lgT = work[0:EXPERTS, :, :, :].rearrange("p a t n -> p (a t n)")

        def bank_of(t):
            return (bt[0], bt[1], br, bp)[t] if t < QT else bt[t % 2]

        def tiles_at(f):
            return [t for t in (QT + 2 * f, QT + 2 * f + 1) if t < TILES]


        block = ctx.enter_context(nc.Block())

        @block.sync
        def _(sp):
            sp.dma_start(wr[:], io["routerT"].rearrange("(k p) n -> p k n", p=P)).then_inc(d_r, 16)
            sp.dma_start(grid[:], io["grid"]).then_inc(d_r, 16)
            sp.dma_start(upper[:], io["upper"]).then_inc(d_r, 16)
            sp.dma_start(wd[:], io["s_downT"].rearrange("(k p) n -> p k n", p=P)).then_inc(d_wd, 16)
            sp.wait_ge(g_zero, 1)
            for t in range(0, ETILES, ZT):
                n = min(ZT, ETILES - t)
                sp.dma_start(io["sorted_x"].rearrange("(t p) n -> p t n", p=P)[:, t:t + n, :],
                             zero[:].unsqueeze(1).to_broadcast([P, n, ROW])
                             ).then_inc(d_zero, 16)
            def load_gate_up(e):
                sp.dma_start(w_gate_up[:, e * DK:(e + 4) * DK, :],
                             io["gate_up"].rearrange("e (k p) n -> p (e k) n", p=P)[:, e * DK:(e + 4) * DK, :]
                             ).then_inc(mem["d_experts"], 16)

            for e in range(4, EXPERTS, 4):
                load_gate_up(e)
            down_rows = io["down"].rearrange("e (k p) n -> p (e k) n", p=P)
            sp.dma_start(w_down[:, 0:EXPERTS, :], down_rows[:, 0:EXPERTS, :]).then_inc(mem["d_experts"], 16)
            sp.wait_ge(v_wlo, 2 * FK)
            load_gate_up(0)
            sp.wait_ge(d_zero, 16 * ((ETILES + ZT - 1) // ZT))
            sp.wait_ge(d_scatter, 16 * TILES)
            sp.wait_ge(p_gu, CHUNKS * FK)
            for r in range(UNROLL):
                sp.dma_start(mem["xs"][:, r], io["sorted_x"].rearrange("(t p) n -> p t n", p=P)[:, r, :]
                             ).then_inc(mem["d_xs"][r], 16)
            sp.dma_start(w_down[:, EXPERTS:2 * EXPERTS, :], down_rows[:, EXPERTS:2 * EXPERTS, :]
                         ).then_inc(mem["d_experts"], 16)

        @block.gpsimd
        def _(pool):
            pool.memset(constl[:, 0], EPS).then_inc(g_vel, 1)
            pool.wait_ge(g_vel, 1)
            pool.memset(constl[:, 1], -0.5).then_inc(g_vel, 1)
            pool.wait_ge(g_vel, 2)
            pool.wait_ge(v_mvl, 2 * QT)
            pool.tensor_tensor(rsl[:, 0], mvl[:, :, 1], constl[:, 0], ALU.add).then_inc(g_vel, 1)
            pool.wait_ge(g_vel, 3)
            pool.tensor_tensor(rsl[:, 1], rsl[:, 0], constl[:, 1], ALU.pow).then_inc(g_rsl, 1)
            pool.memset(zero[:], 0.0).then_inc(g_zero, 1)
            pool.wait_ge(g_zero, 1)
            pool.memset(allone[:], 1.0).then_inc(g_zero, 1)
            pool.wait_ge(g_zero, 2)
            pool.memset(onesr[:], 1.0).then_inc(g_zero, 1)
            pool.wait_ge(g_zero, 3)
            pool.memset(carry[:, 0, :], 0.0).then_inc(g_zero, 1)
            pool.wait_ge(g_zero, 4)
            pool.wait_ge(v_score, 2)
            pool.wait_ge(v_last, QT)
            for half in range(2):
                tiles = range(half * TILES // 2, (half + 1) * TILES // 2)
                if half:
                    pool.wait_ge(d_scatter, 16 * TILES // 2)
                else:
                    pool.wait_ge(d_r, 48)
                for n, t in enumerate(tiles):
                    pool.tensor_scalar(x2s[:, n, 0:D], x2[:, t], esc[:, 2, t:t + 1], 0.0, ALU.mult, ALU.add
                                       ).then_inc(g_x2s, 1)
                pool.tensor_copy(x2s[:, :, D], grid[:, GRID_ID + tiles[0]:GRID_ID + tiles[-1] + 1]).then_inc(g_zero, 1)
                if not half:
                    pool.wait_ge(v_pos, 1)
                    pool.wait_ge(d_zero, 16 * ((ETILES + ZT - 1) // ZT))
                pool.wait_ge(g_zero, 4 + half + 1)
                for n, t in enumerate(tiles):
                    pool.wait_ge(g_x2s, t + 1)
                    pool.indirect_dma_start(io["sorted_x"][:, :], bass.IndirectOffsetOnAxis(pos[:, t:t + 1], 0),
                                            x2s[:, n, :], None).then_inc(d_scatter, 16)

        @block.scalar
        def _(act):
            def cut_high(f):
                act.wait_ge(d_gu, 32)
                for n in range(2):
                    act.activation(wgu[n][0][:, :, f * P:(f + 1) * P], uncut[n][:, :, f * P:(f + 1) * P], ACT.Copy
                                   ).then_inc(a_whi, 1)

            def copy_transposed(tiles):
                for t in tiles:
                    act.wait_ge(p_tr, t + 1)
                    act.activation(x2T[0][:, :, t * P:(t + 1) * P], bank_of(t)[:, 0:D].rearrange("p (k n) -> p k n", k=DK),
                                   ACT.Copy).then_inc(a_tr, 1)

            def gates(c):
                for f in range(FK):
                    if isinstance(c, int):
                        copy_transposed(tiles_at(f)[:1])
                    act.wait_ge(p_gu, c * FK + (f + 1))
                    act.activation(hT[:, f], bg[f % 2][:], ACT.Silu).then_inc(a_silu, 1)
                    if isinstance(c, int) and f + 2 < FK:
                        cut_high(f + 2)
                    if isinstance(c, int):
                        copy_transposed(tiles_at(f)[1:])
                    if isinstance(c, int) and f in LOGITS_AT:
                        act.wait_ge(p_lgT, 2 * LOGITS_AT[f] + 1)
                        act.activation(lgT, br[0:EXPERTS, :], ACT.Copy).then_inc(a_lgT, 1)

            cut_high(0)
            copy_transposed(range(QT))
            cut_high(1)
            act.wait_ge(d_r, 48)
            act.activation(wr_parts[0][:], wr[:], ACT.Copy).then_inc(a_wr, 1)
            gates(0)
            act.wait_ge(v_route, 2)
            act.activation(esc[:, 0], top[:], ACT.Exp, scale=-1.0).then_inc(a_sc, 1)
            with act.Fori(1, CHUNKS) as c:
                gates(c)

        @block.vector
        def _(dve):
            n_route = [0]

            def step(ins):
                n_route[0] += 1
                ins.then_inc(v_route, 1)
                dve.wait_ge(v_route, n_route[0])

            def by_tile(ap):
                return ap.unsqueeze(2).to_broadcast([P, TILES, EXPERTS])

            def by_expert(ap, n=TILES):
                return ap.unsqueeze(1).to_broadcast([P, n, EXPERTS])

            def choose():
                dve.wait_ge(p_lgT, 2 * CHUNKS)
                dve.wait_ge(d_r, 48)
                step(dve.tensor_copy(lg[:], bp[:, 0:TILES * EXPERTS].rearrange("p (t n) -> p t n", n=EXPERTS)))
                step(dve.tensor_reduce(top[:], lg[:], AX.X, ALU.max))
                step(dve.tensor_tensor(work[:, 0], lg[:], by_tile(top[:]), ALU.is_equal))
                step(dve.tensor_tensor(work[:, 1], work[:, 0], by_expert(grid[:, GRID_REV:GRID_REV + EXPERTS]), ALU.mult))
                step(dve.tensor_reduce(rev[:], work[:, 1], AX.X, ALU.max))
                dve.tensor_tensor(oneh[:], by_expert(grid[:, GRID_REV:GRID_REV + EXPERTS]), by_tile(rev[:]), ALU.is_equal
                                  ).then_inc(v_oh, 1)
                dve.wait_ge(a_sc, 1)
                dve.tensor_scalar(esc[:, 1], esc[:, 0], 1.0, None, ALU.add).then_inc(v_score, 1)
                dve.wait_ge(v_score, 1)
                dve.reciprocal(esc[:, 2], esc[:, 1]).then_inc(v_score, 1)

            def count():
                dve.wait_ge(p_px, 1)
                dve.wait_ge(g_zero, 4)
                for t in range(TILES):
                    step(dve.tensor_tensor(carry[:, t + 1], bp[:, 256 + t * EXPERTS:256 + (t + 1) * EXPERTS], carry[:, t],
                                           ALU.add))

            def place():
                counts = carry[:, TILES, :].unsqueeze(2).to_broadcast([P, EXPERTS, TILES])
                thresholds = grid[:, GRID_THR:GRID_THR + TILES].unsqueeze(1).to_broadcast([P, EXPERTS, TILES])
                step(dve.tensor_tensor(work[:, 0], counts, thresholds, ALU.is_gt))
                step(dve.tensor_reduce(nt[:], work[:, 0], AX.X, ALU.add))
                step(dve.tensor_tensor_scan(incl[:], onesr[:], nt[:], 0.0, ALU.mult, ALU.add))
                step(dve.tensor_tensor(off[:, 0], incl[:], nt[:], ALU.subtract))
                step(dve.tensor_scalar(off[:, 1], off[:, 0], float(P), None, ALU.mult))
                step(dve.tensor_tensor(work[:, 0], bp[:, 0:256].rearrange("p (t n) -> p t n", n=EXPERTS),
                                       carry[:, 0:TILES, :], ALU.add))
                step(dve.tensor_tensor(work[:, 1], work[:, 0], by_expert(off[:, 1]), ALU.add))
                step(dve.tensor_tensor(work[:, 0], work[:, 1], oneh[:], ALU.mult))
                step(dve.tensor_reduce(posf[:], work[:, 0], AX.X, ALU.add))
                dve.tensor_copy(pos[:], posf[:]).then_inc(v_pos, 1)

            def experts():
                tiles = grid[:, GRID_J:GRID_J + ETILES].unsqueeze(2).to_broadcast([P, ETILES, EXPERTS])
                step(dve.tensor_tensor(cmpj[:], by_expert(incl[:], ETILES), tiles, ALU.is_le))
                step(dve.tensor_reduce(tef[:, 0], cmpj[:], AX.X, ALU.add))
                step(dve.tensor_scalar(tef[:, 1], tef[:, 0], float(EXPERTS - 1), None, ALU.min))
                step(dve.tensor_copy(te[:], tef[:, 1]))

            def hidden(c, f):
                dve.wait_ge(a_silu, c * FK + (f + 1))
                dve.tensor_tensor(hT[:, f], hT[:, f], bu[f % 2][:], ALU.mult).then_inc(v_h, 1)

            def residual(c, tiles=range(QT)):
                dve.wait_ge(g_x2s, TILES // 2 if isinstance(c, int) else TILES)
                for i in tiles:
                    dve.wait_ge(p_dn, c * QT + (i + 1))
                    t = c * QT + i
                    xx = x2[:, t] if isinstance(t, int) else x2[:, bass.ds(t, 1), :].squeeze(1)
                    dve.tensor_tensor(xx, bt[i % 2][:, 0:D], xx, ALU.add).then_inc(v_base, 1)

            def x_low(tiles):
                for t in tiles:
                    dve.wait_ge(a_tr, t + 1)
                    tile = slice(t * P, (t + 1) * P)
                    dve.tensor_tensor(x2T[1][:, :, tile], bank_of(t)[:, 0:D].rearrange("p (k n) -> p k n", k=DK),
                                      x2T[0][:, :, tile].bitcast(F32), ALU.subtract).then_inc(v_xlo, 1)

            def w_low(f):
                for n in range(2):
                    cols = slice(f * P, (f + 1) * P)
                    dve.wait_ge(a_whi, 2 * f + n + 1)
                    dve.tensor_tensor(wgu[n][1][:, :, cols], uncut[n][:, :, cols], wgu[n][0][:, :, cols].bitcast(F32),
                                      ALU.subtract).then_inc(v_wlo, 1)

            w_low(0)
            x_low(range(QT))
            w_low(1)
            for i in range(QT):
                dve.bn_stats(stl[:, i], mem["x1"][:, i]).then_inc(v_mvl, 1)
            for i in range(QT):
                dve.wait_ge(v_mvl, i + 1)
                dve.bn_aggr(mvl[:, i], stl[:, i]).then_inc(v_mvl, 1)
            dve.wait_ge(g_rsl, 1)
            for i in range(QT):
                dve.tensor_scalar(x2[:, TILES - QT + i], mem["x1"][:, i], mvl[:, i, 0:1], rsl[:, 1, i:i + 1],
                                  ALU.subtract, ALU.mult).then_inc(v_last, 1)

            dve.wait_ge(a_wr, 1)
            dve.tensor_tensor(wr_parts[1][:], wr[:], wr_parts[0][:].bitcast(F32), ALU.subtract).then_inc(v_wr, 1)

            for f in range(FK):
                x_low(tiles_at(f)[:1])
                hidden(0, f)
                x_low(tiles_at(f)[1:])
                if f + 2 < FK:
                    w_low(f + 2)
            choose()
            residual(0, (0, 1))
            count()
            place()
            residual(0, (2, 3))
            experts()
            with dve.Fori(1, CHUNKS) as c:
                for f in range(FK):
                    hidden(c, f)
                residual(c)

        @block.tensor
        def _(pe):
            def logits(c):
                pe.wait_ge(v_xlo, (c + 1) * QT)
                if c:
                    pe.wait_ge(a_lgT, c)
                for k in range(DK):
                    for n, (xp, wp) in enumerate(((0, 0), (1, 0), (0, 1))):
                        mm = pe.matmul(br[0:EXPERTS, :], wr_parts[wp][:, k, :], x2T[xp][:, k, c * 512:(c + 1) * 512],
                                       start=(k == n == 0), stop=(k == DK - 1 and n == 2))
                mm.then_inc(p_lgT, 1)

            def logits_by_token(c):
                pe.wait_ge(a_lgT, c + 1)
                for i in range(QT):
                    t = c * QT + i
                    mm = pe.transpose(bp[:, t * EXPERTS:(t + 1) * EXPERTS], lgT[:, i * P:(i + 1) * P],
                                      ident[0:EXPERTS, 0:EXPERTS])
                mm.then_inc(p_lgT, 1)

            def transposes(tiles):
                for t in tiles:
                    if t >= TILES - QT:
                        pe.wait_ge(v_last, t - (TILES - QT) + 1)
                    elif t % QT == 0:
                        pe.wait_ge(d_x2i[t // QT], 16)
                    if t >= QT:
                        pe.wait_ge(v_xlo, t - 1)
                    for k in range(DK):
                        mm = pe.transpose(bank_of(t)[:, k * P:(k + 1) * P], x2[:, t, k * P:(k + 1) * P], ident[:])
                    mm.then_inc(p_tr, 1)

            def gate_up(c, f):
                cols = slice(c * 512, (c + 1) * 512) if isinstance(c, int) else bass.ds(c * 512, 512)
                if f >= 2 or not isinstance(c, int):
                    pe.wait_ge(v_h, c * FK + max(f - 1, 0))
                if isinstance(c, int):
                    pe.wait_ge(v_wlo, 2 * (f + 1))
                for w, bank in zip(wgu, (bg, bu)):
                    products = [(w[0], x2T[0]), (w[1], x2T[0]), (w[0], x2T[1])]
                    for k in range(DK):
                        for n, (wp, xp) in enumerate(products):
                            mm = pe.matmul(bank[f % 2][:], wp[:, k, f * P:(f + 1) * P], xp[:, k, cols],
                                           start=(k == n == 0), stop=(k == DK - 1 and n == len(products) - 1))
                    if bank is bg and isinstance(c, int):
                        transposes(tiles_at(f)[:1])
                mm.then_inc(p_gu, 1)

            def down(c, tiles=range(QT)):
                if 0 in tiles:
                    pe.wait_ge(v_h, c * FK + (FK - 1))
                for i in tiles:
                    if i >= 2 or not isinstance(c, int):
                        pe.wait_ge(v_base, c * QT + max(i - 1, 0))
                    for f in range(FK):
                        if i == 0 and f == FK - 1:
                            pe.wait_ge(v_h, c * FK + FK)
                        mm = pe.matmul(bt[i % 2][:, 0:D], hT[:, f, i * P:(i + 1) * P], wd[:, f, :],
                                       start=(f == 0), stop=(f == FK - 1))
                    mm.then_inc(p_dn, 1)

            transposes(range(QT))
            pe.wait_ge(v_xlo, QT)
            for f in range(FK):
                gate_up(0, f)
                transposes(tiles_at(f)[1:])
                if f == 0:
                    pe.wait_ge(d_r, 48)
                    pe.wait_ge(v_wr, 1)
                if f in LOGITS_AT:
                    logits(LOGITS_AT[f])
                if f - 1 in LOGITS_AT:
                    logits_by_token(LOGITS_AT[f - 1])
            pe.wait_ge(d_wd, 16)
            down(0, (0, 1))
            pe.wait_ge(v_oh, 1)
            pe.wait_ge(g_zero, 2)
            pe.matmul(bp[:, 0:256], upper[:], oneh[:].rearrange("p t n -> p (t n)"), start=True, stop=True)
            pe.matmul(bp[:, 256:512], allone[:], oneh[:].rearrange("p t n -> p (t n)"), start=True, stop=True
                      ).then_inc(p_px, 1)
            down(0, (2, 3))
            with pe.Fori(1, CHUNKS) as c:
                for f in range(FK):
                    gate_up(c, f)
                down(c)


UNROLL = 6
TURNS = (ETILES - 1) // UNROLL


def experts(nc, io, mem):
    base, pos, te, ident = mem["x2"], mem["pos"], mem["te"], mem["ident"]
    w_gate_up, w_down = mem["w_gate_up"], mem["w_down"]
    with ExitStack() as ctx:
        def sb(name, shape, dt=F32):
            return ctx.enter_context(nc.sbuf_tensor(name, shape, dt))

        def sem(name):
            return ctx.enter_context(nc.semaphore(name))

        sb("xs_place", [P, UNROLL, ROW])
        xs = mem["xs"]
        xsT = sb("xsT", [P, UNROLL, D])
        sil = sb("sil", [P, UNROLL, FE])
        h = sb("h", [P, UNROLL, FE])
        hTt = sb("hTt", [P, UNROLL, FE])
        ysb = sb("ysb", [P, UNROLL, D])
        row = sb("row", [P, UNROLL], mybir.dt.uint32)
        yg = sb("yg", [P, TILES, D])
        st7 = sb("st7", [P, TILES, 6])
        mv4 = sb("mv4", [P, TILES, 2])
        ve4 = sb("ve4", [P, TILES])
        rstd4 = sb("rstd4", [P, TILES])
        shift4 = sb("shift4", [P, TILES])
        mhalf4 = sb("mhalf4", [P, 4])
        eps4 = sb("eps4", [P, 4])
        bx = [ctx.enter_context(nc.psum_tensor(f"bx{i}", [P, 512], F32)) for i in range(2)]
        bgu = [ctx.enter_context(nc.psum_tensor(f"bgu{i}", [P, 512], F32)) for i in range(2)]
        bh = [ctx.enter_context(nc.psum_tensor(f"bh{i}", [P, 512], F32)) for i in range(2)]
        by = [ctx.enter_context(nc.psum_tensor(f"by{i}", [P, 512], F32)) for i in range(2)]

        d_xs = mem["d_xs"]
        d_y = [sem(f"d_y{i}") for i in range(UNROLL)]
        d_yg = [sem(f"d_yg{i}") for i in range(4)]
        d_out = sem("d_out")
        g_c4 = sem("g_c4")
        s_turn, v_row = sem("s_turn"), sem("v_row")
        p_x, a_x, p_e, a_s, v_hh, p_h, v_hT, p_y, v_y = (sem("p_x"), sem("a_x"), sem("p_e"), sem("a_s"), sem("v_hh"),
                                                         sem("p_h"), sem("v_hT"), sem("p_y"), sem("v_y"))
        v_f, v_mv4, g_l4, g_r4, v_shift = sem("v_f"), sem("v_mv4"), sem("g_l4"), sem("g_r4"), sem("v_shift")
        v_st4, a_out = sem("v_st4"), sem("a_out")
        g_f = sem("g_f")
        LAST_ACT = TILES - 2

        block = ctx.enter_context(nc.Block())

        @block.sync
        def _(sp):
            xs_rows = io["sorted_x"].rearrange("(t p) n -> p t n", p=P)

            def load(j, r):
                sp.dma_start(xs[:, r], xs_rows[:, bass.ds(j, 1), :].squeeze(1)).then_inc(d_xs[r], 16)

            with sp.Fori(0, TURNS - 1) as i:
                for r in range(UNROLL):
                    sp.wait_ge(p_x, i * UNROLL + (r + 1))
                    sp.wait_ge(v_row, i * UNROLL + (r + 1))
                    sp.sem_inc(s_turn, 1)
                    load(i * UNROLL + (r + UNROLL), r)
            for j in range(TURNS * UNROLL, ETILES):
                sp.wait_ge(p_x, j - UNROLL + 1)
                sp.wait_ge(v_row, j - UNROLL + 1)
                load(j, j % UNROLL)
            for r in range(UNROLL):
                sp.wait_ge(d_y[r], 16 * ((ETILES - 1 - r) // UNROLL + 1))
            for g in range(TILES // 4):
                sp.dma_start(yg[:, 4 * g:4 * g + 4, :],
                             io["routed"][1:S + 1, :].rearrange("(t p) n -> p t n", p=P)[:, 4 * g:4 * g + 4, :]
                             ).then_inc(d_yg[g], 16)
            out_rows = io["out"].rearrange("(t p) n -> p t n", p=P)
            for t in range(0, TILES, 2):
                if t < LAST_ACT:
                    sp.wait_ge(a_out, t + 2)
                else:
                    sp.wait_ge(v_f, TILES // 2 + t + 2 - LAST_ACT)
                sp.dma_start(out_rows[:, t:t + 2, :], base[:, t:t + 2, :]).then_inc(d_out, 16)
            sp.wait_ge(d_out, 16 * TILES // 2)

        @block.gpsimd
        def _(pool):
            pool.memset(mhalf4[:], -0.5).then_inc(g_c4, 1)
            pool.wait_ge(g_c4, 1)
            pool.memset(eps4[:], EPS).then_inc(g_c4, 1)
            pool.wait_ge(g_c4, 2)

            def store(j, r, turn):
                pool.wait_ge(v_y, j + 1)
                pool.sem_inc(g_c4, 1)
                if r or turn is not None:
                    before = (r - 1) % UNROLL
                    pool.wait_ge(d_y[before], 16 * ((0 if turn is None else turn) + (1 if r else 0)))
                    pool.sem_inc(g_c4, 1)
                pool.indirect_dma_start(io["routed"][:, :], bass.IndirectOffsetOnAxis(row[:, r:r + 1], 0),
                                        ysb[:, r, :], None).then_inc(d_y[r], 16)

            for r in range(UNROLL):
                store(r, r, None)
            with pool.Fori(1, TURNS) as i:
                for r in range(UNROLL):
                    store(i * UNROLL + r, r, i)
            for j in range(TURNS * UNROLL, ETILES):
                store(j, j % UNROLL, j // UNROLL)

            def inverse(g):
                pool.wait_ge(v_mv4, 4 * (g + 1))
                pool.tensor_tensor(ve4[:, 4 * g:4 * g + 4], mv4[:, 4 * g:4 * g + 4, 1], eps4[:], ALU.add).then_inc(g_l4, 1)
                pool.wait_ge(g_l4, g + 1)
                pool.tensor_tensor(rstd4[:, 4 * g:4 * g + 4], ve4[:, 4 * g:4 * g + 4], mhalf4[:], ALU.pow).then_inc(g_r4, 1)

            def sums(g):
                pool.wait_ge(d_yg[g], 16)
                for t in (4 * g + 1, 4 * g + 3):
                    pool.tensor_tensor(base[:, t], base[:, t], yg[:, t], ALU.add).then_inc(g_f, 1)

            sums(0)
            for g in range(4):
                if g < 3:
                    sums(g + 1)
                inverse(g)

        @block.scalar
        def _(act):
            def copy_x(j, r):
                act.wait_ge(p_x, j + 1)
                act.activation(xsT[:, r], bx[r % 2][:, 0:D], ACT.Copy).then_inc(a_x, 1)

            def gate(j, r):
                act.wait_ge(p_e, j + 1)
                act.activation(sil[:, r], bgu[r % 2][:, 0:FE], ACT.Silu).then_inc(a_s, 1)

            copy_x(0, 0)
            copy_x(1, 1)
            gate(0, 0)
            with act.Fori(0, TURNS - 1) as i:
                for n in range(UNROLL):
                    copy_x(i * UNROLL + (n + 2), (2 + n) % UNROLL)
                    gate(i * UNROLL + (n + 1), (1 + n) % UNROLL)
            for j in range((TURNS - 1) * UNROLL + 1, ETILES):
                if j + 1 < ETILES:
                    copy_x(j + 1, (j + 1) % UNROLL)
                gate(j, j % UNROLL)
            for t in range(LAST_ACT):
                if t % 4 == 0:
                    act.wait_ge(v_shift, t // 4 + 1)
                act.activation(base[:, t], base[:, t], ACT.Identity, bias=shift4[:, t:t + 1], scale=rstd4[:, t:t + 1]
                               ).then_inc(a_out, 1)

        @block.vector
        def _(dve):
            def product(j, r):
                dve.wait_ge(a_s, j + 1)
                dve.tensor_tensor(h[:, r], sil[:, r], bgu[r % 2][:, FE:2 * FE], ALU.mult).then_inc(v_hh, 1)

            def copy_h(j, r):
                dve.wait_ge(p_h, j + 1)
                dve.tensor_copy(hTt[:, r], bh[r % 2][:, 0:FE]).then_inc(v_hT, 1)

            def copy_y(j, r, stored):
                dve.wait_ge(p_y, j + 1)
                if stored is not None:
                    dve.wait_ge(d_y[r], stored)
                dve.tensor_copy(row[:, r:r + 1], xs[:, r, D:D + 1]).then_inc(v_row, 1)
                dve.tensor_copy(ysb[:, r], by[r % 2][:, 0:D]).then_inc(v_y, 1)

            product(0, 0)
            for j in range(1, 1 + UNROLL):
                copy_h(j - 1, (j - 1) % UNROLL)
                product(j, j % UNROLL)
                copy_y(j - 1, (j - 1) % UNROLL, None)
            with dve.Fori(1, TURNS) as i:
                for n in range(UNROLL):
                    j = i * UNROLL + (1 + n)
                    copy_h(j - 1, n)
                    product(j, (1 + n) % UNROLL)
                    copy_y(j - 1, n, i * 16)
            for j in range(TURNS * UNROLL + 1, ETILES + 1):
                copy_h(j - 1, (j - 1) % UNROLL)
                if j < ETILES:
                    product(j, j % UNROLL)
                copy_y(j - 1, (j - 1) % UNROLL, 16 * ((j - 1) // UNROLL))
            for t in range(TILES + 6):
                if t < TILES and t % 2 == 0:
                    if t % 4 == 0:
                        dve.wait_ge(d_yg[t // 4], 16)
                    dve.tensor_tensor(base[:, t], base[:, t], yg[:, t], ALU.add).then_inc(v_f, 1)
                if 1 <= t <= TILES:
                    if (t - 1) % 2:
                        dve.wait_ge(g_f, t // 2)
                    else:
                        dve.wait_ge(v_f, (t - 1) // 2 + 1)
                    dve.bn_stats(st7[:, t - 1], base[:, t - 1]).then_inc(v_st4, 1)
                if 2 <= t <= TILES + 1:
                    dve.wait_ge(v_st4, t - 1)
                    dve.bn_aggr(mv4[:, t - 2], st7[:, t - 2]).then_inc(v_mv4, 1)
                if t >= 9 and t % 4 == 1:
                    g = (t - 9) // 4
                    dve.wait_ge(g_r4, g + 1)
                    dve.scalar_tensor_tensor(shift4[:, 4 * g:4 * g + 4], mv4[:, 4 * g:4 * g + 4, 0], -1.0,
                                             rstd4[:, 4 * g:4 * g + 4], ALU.mult, ALU.mult).then_inc(v_shift, 1)
            dve.wait_ge(v_shift, TILES // 4)
            for t in range(LAST_ACT, TILES):
                dve.tensor_scalar(base[:, t], base[:, t], rstd4[:, t:t + 1], shift4[:, t:t + 1], ALU.mult, ALU.add
                                  ).then_inc(v_f, 1)

        @block.tensor
        def _(pe):
            def expert_of(j):
                return pe.value_load(te[0:1, bass.ds(j, 1)], min_val=0, max_val=EXPERTS - 1)

            def transpose_x(j, r, landed):
                pe.wait_ge(d_xs[r], landed)
                if not (isinstance(j, int) and j < 2):
                    pe.wait_ge(a_x, j - 1)
                for k in range(DK):
                    mm = pe.transpose(bx[r % 2][:, k * P:(k + 1) * P], xs[:, r, k * P:(k + 1) * P], ident[:])
                mm.then_inc(p_x, 1)

            def gate_up(j, r, e):
                pe.wait_ge(a_x, j + 1)
                for k in range(DK):
                    mm = pe.matmul(bgu[r % 2][:], xsT[:, r, k * P:(k + 1) * P],
                                   w_gate_up[:, bass.ds(e * DK + k, 1), :].squeeze(1), start=(k == 0), stop=(k == DK - 1))
                mm.then_inc(p_e, 1)

            def transpose_h(j, r):
                pe.wait_ge(v_hh, j + 1)
                if not (isinstance(j, int) and j < 2):
                    pe.wait_ge(v_hT, j - 1)
                for k in range(DK):
                    mm = pe.transpose(bh[r % 2][:, k * P:(k + 1) * P], h[:, r, k * P:(k + 1) * P], ident[:])
                mm.then_inc(p_h, 1)

            def down(j, r):
                e = expert_of(j)
                pe.wait_ge(v_hT, j + 1)
                if not (isinstance(j, int) and j < 2):
                    pe.wait_ge(v_y, j - 1)
                for k in range(DK):
                    mm = pe.matmul(by[r % 2][:, 0:D], hTt[:, r, k * P:(k + 1) * P],
                                   w_down[:, bass.ds(e * DK + k, 1), :].squeeze(1), start=(k == 0), stop=(k == DK - 1))
                mm.then_inc(p_y, 1)

            def slot(j, n, i):
                r0, r1, r2 = n, (n + 1) % UNROLL, (n + 2) % UNROLL
                e = expert_of(j)
                if not (isinstance(j, int) and j == ETILES - 1):
                    transpose_x(j + 1, r2, (i + 1 + (n + 2) // UNROLL) * 16)
                transpose_h(j - 1, r0)
                gate_up(j, r1, e)
                down(j - 1, r0)

            transpose_x(0, 0, 16)
            transpose_x(1, 1, 16)
            pe.wait_ge(mem["d_experts"], 16 * (EXPERTS // 4 + 2))
            gate_up(0, 0, expert_of(0))
            for n in range(UNROLL):
                slot(1 + n, n, 0)
            with pe.Fori(1, TURNS - 1) as i:
                for n in range(UNROLL):
                    slot(i * UNROLL + (1 + n), n, i)
            for j in range((TURNS - 1) * UNROLL + 1, ETILES):
                slot(j, (j - 1) % UNROLL, (j - 1) // UNROLL)
            transpose_h(ETILES - 1, (ETILES - 1) % UNROLL)
            down(ETILES - 1, (ETILES - 1) % UNROLL)


def program(nc, io, stages=3):
    with ExitStack() as outer:
        def sb(name, shape, dt=F32):
            return outer.enter_context(nc.sbuf_tensor(name, shape, dt))

        def next_address():
            return (nc.sbuf_base + 31) // 32 * 32

        mem = {"ident": sb("ident", [P, P]),
               "x1": sb("x1", [P, QT, D])}
        start = next_address()
        mem["x2"] = nc.alloc_sbuf_tensor_at("x2", [P, TILES, D], F32, offset=start)
        mem["uncut"] = nc.alloc_sbuf_tensor_at("uncut", [P, 2, DK, SF], F32, offset=start + 4 * TILES * D)
        mem["d_dup"] = outer.enter_context(nc.semaphore("d_dup"))
        mem["d_x2i"] = [outer.enter_context(nc.semaphore(f"d_x2i{c}")) for c in range(CHUNKS - 1)]
        mem["d_gu"] = outer.enter_context(nc.semaphore("d_gu"))
        mem["d_xs"] = [outer.enter_context(nc.semaphore(f"d_xs{i}")) for i in range(UNROLL)]
        mem["d_experts"] = outer.enter_context(nc.semaphore("d_experts"))
        with ExitStack() as ctx:
            for name, shape, dt in (("K1", [P, HEADS, KEYS_PAD], F32R), ("K2", [P, HEADS, KEYS_PAD], F32R),
                                    ("V", [P, KT, HID], F32),
                                    ("x1T", [P, DK, QC], F32),
                                    ("mxp", [P, 2, TILE_U, len(KC)], F32),
                                    ("nm", [P, 2, TILE_U], F32)):
                mem[name] = ctx.enter_context(nc.sbuf_tensor(name, shape, dt))
            mem["Q1"] = [ctx.enter_context(nc.sbuf_tensor("Q1a", [P, 2, QC], F32R))]
            before_attention(nc, io, mem)
            if stages > 1:
                attention(nc, io, mem)
        if stages > 2:
            sb("x2_place", [P, TILES, D])
            mem["w_gate_up"] = sb("w_gate_up", [P, EXPERTS * DK, 2 * FE])
            w_down_at = next_address()
            mem["w_down"] = sb("w_down", [P, EXPERTS * DK, D])
            mem["pos"] = sb("pos", [P, TILES], mybir.dt.uint32)
            mem["te"] = sb("te", [P, ETILES], I32)
            mem["x2T_low"] = nc.alloc_sbuf_tensor_at("x2T_low", [P, DK, S], F32R, offset=w_down_at + 4 * EXPERTS * D)
            mem["xs"] = nc.alloc_sbuf_tensor_at("xs", [P, UNROLL, ROW], F32, offset=next_address())
            route_and_share(nc, io, mem)
            experts(nc, io, mem)


_SCRATCH = {"x1b": (S, D), "x1T": (D, S), "x2": (S, D), "sorted_x": (ETILES * P, ROW), "routed": (S + 1, D)}


def kernel(x, ctx_1024, L0_attn_W_in, L0_attn_b_in, L0_attn_log_A, L0_attn_B_p, L0_attn_C_p, L0_attn_W_out,
           L0_attn_b_out, L0_attn_gamma, L0_attn_beta, L0_xattn_Wq, L0_xattn_Wk, L0_xattn_Wv, L0_xattn_Wo,
           L0_xattn_bo, L0_ffn_router_w, L0_ffn_gate_up_proj, L0_ffn_down_proj, L0_ffn_shared_gate_w,
           L0_ffn_shared_up_w, L0_ffn_shared_down_w):
    import numpy as np
    import concourse.bacc as bacc
    from concourse.bass_utils import run_bass_kernel_spmd

    ctx_rows = ctx_1024[0]
    host = {
        "x": x[0], "xT": x[0].T, "ctxT": np.concatenate([ctx_rows, ctx_rows[-1:]]).T,
        "w_inT": L0_attn_W_in.T, "w_outT": L0_attn_W_out.T,
        "cols": np.stack([np.reshape(a, (DK, P)) for a in (L0_attn_b_in, L0_attn_log_A, L0_attn_B_p, L0_attn_C_p)]
                         ).transpose(2, 0, 1),
        "b_out": L0_attn_b_out, "gamma": L0_attn_gamma, "beta": L0_attn_beta, "bo": L0_xattn_bo,
        "wq": L0_xattn_Wq, "wk": L0_xattn_Wk, "wv": L0_xattn_Wv, "wo": L0_xattn_Wo,
        "routerT": L0_ffn_router_w.T, "gate_up": L0_ffn_gate_up_proj, "down": L0_ffn_down_proj,
        "s_gateT": L0_ffn_shared_gate_w.T, "s_upT": L0_ffn_shared_up_w.T, "s_downT": L0_ffn_shared_down_w.T,
        "ident": np.eye(P, dtype=np.float32), "upper": np.triu(np.ones((P, P), np.float32), 1),
        "grid": np.concatenate([np.tile(np.concatenate([EXPERTS - np.arange(EXPERTS), P * np.arange(TILES), np.arange(ETILES)]
                                       ).astype(np.float32), (P, 1)),
                                (1 + np.arange(P)[:, None] + P * np.arange(TILES)[None, :]).astype(np.float32)], 1),
    }
    nc = bacc.Bacc("TRN2", target_bir_lowering=False, num_devices=1)
    io, arrays = {}, {}
    for name, a in host.items():
        a = np.ascontiguousarray(a)
        arrays["in_" + name] = a
        io[name] = nc.dram_tensor("in_" + name, a.shape, mybir.dt.from_np(a.dtype), kind="ExternalInput").ap()
    for name, shape in _SCRATCH.items():
        io[name] = nc.dram_tensor("scratch_" + name, shape, F32, kind="Internal").ap()
    io["out"] = nc.dram_tensor("out_0", (S, D), F32, kind="ExternalOutput").ap()
    program(nc, io)
    r = run_bass_kernel_spmd(nc, [arrays], core_ids=[0])
    return r.results[0]["out_0"].reshape(1, S, D)
```
